# Optimizing a Trainium2 kernel written in Bass

```python
import numpy as np
import jax
import jax.numpy as jnp

def _softmax(x, axis=-1):
    return jax.nn.softmax(x, axis=axis)

def _gelu(x):
    return jax.nn.gelu(x, approximate=True)

def _silu(x):
    return jax.nn.silu(x)

def _sigmoid(x):
    return jax.nn.sigmoid(x)

def _layernorm(x, axis=-1, eps=1e-05):
    m = jnp.mean(x, axis=axis, keepdims=True)
    v = jnp.var(x, axis=axis, keepdims=True)
    return (x - m) / jnp.sqrt(v + eps)

def _scatter_add(tgt, idx, src, axis=0):
    return tgt.at[idx].add(src)

def _segment_sum(src, seg, n):
    return jax.ops.segment_sum(src, seg, n)
kernel_name = 'mk_xattn_ffn_d2_seqx_r8_2bdd24'

def setup_inputs(seed: int=0):
    np.random.seed(seed)
    _w = jnp.asarray

    def _rec_inputs():
        import jax
        import jax.numpy as jnp
        _rk = jax.random.key(seed)
        x = -0.0003929 + 0.9999 * jax.random.normal(jax.random.fold_in(_rk, 1), (4, 256, 256), jnp.float32)
        _lenS = 256 - jax.random.randint(jax.random.fold_in(_rk, 7), (4,), 0, max(1, 256 // 4) + 1, jnp.int32)
        _lenS2 = 256 - jax.random.randint(jax.random.fold_in(_rk, 8), (4,), 0, max(1, 256 // 4) + 1, jnp.int32)
        _ctx_1024P = jax.random.normal(jax.random.fold_in(_rk, 11), (4, 16, 128), jnp.float32)
        _ctx_1024c = jax.random.dirichlet(jax.random.fold_in(_rk, 511), 0.3 * jnp.ones((16,), jnp.float32), (4, 256))
        _ctx_1024t = jnp.einsum('bsk,bkd->bsd', _ctx_1024c, _ctx_1024P)
        _ctx_1024t = _ctx_1024t * jax.lax.rsqrt(jnp.mean(jnp.square(_ctx_1024t)) + 1e-12) * 0.953939
        ctx_1024 = -0.000494167 + 1.00018 * (_ctx_1024t + 0.3 * jax.random.normal(jax.random.fold_in(_rk, 611), (4, 256, 128), jnp.float32))
        _validS = jnp.arange(256)[None, :] < _lenS[:, None]
        _validS2 = jnp.arange(256)[None, :] < _lenS2[:, None]
        _causal = jnp.tril(jnp.ones((256, 256), dtype=bool))
        mask_BxS2_bf1 = jnp.ones((4, 256), dtype=bool)
        return (x, ctx_1024, mask_BxS2_bf1)
    x, ctx_1024, mask_BxS2_bf1 = _rec_inputs()

    def _L0_xattn_setup():
        import jax, jax.numpy as jnp
        import numpy as np
        N_HEADS = 16
        N_KV_HEADS = 8
        HEAD_DIM = 128
        D_TEXT = 256
        D_VISION = 128
        GROUPS = N_HEADS // N_KV_HEADS
        key = jax.random.key(seed)
        ks = jax.random.split(key, 6)
        B, T_text, T_vis = (4, 256, 72)
        text_hidden = jax.random.normal(ks[0], (B, T_text, D_TEXT), dtype=jnp.float32)
        vision_tokens = jax.random.normal(ks[1], (B, T_vis, D_VISION), dtype=jnp.float32)
        vision_mask = jnp.ones((B, T_vis), dtype=bool)
        s = 0.02
        Wq = jax.random.normal(ks[2], (D_TEXT, N_HEADS * HEAD_DIM), dtype=jnp.float32) * s
        Wk = jax.random.normal(ks[3], (D_VISION, N_KV_HEADS * HEAD_DIM), dtype=jnp.float32) * s
        Wv = jax.random.normal(ks[4], (D_VISION, N_KV_HEADS * HEAD_DIM), dtype=jnp.float32) * s
        Wo = jax.random.normal(ks[5], (N_HEADS * HEAD_DIM, D_TEXT), dtype=jnp.float32) * s
        return {'text_hidden': text_hidden, 'vision_tokens': vision_tokens, 'vision_mask': vision_mask, 'Wq': Wq, 'Wk': Wk, 'Wv': Wv, 'Wo': Wo}
    _L0_xattn_all = _L0_xattn_setup()
    _L0_xattn_in = {k: v for k, v in _L0_xattn_all.items() if k in ('Wq', 'Wk', 'Wv', 'Wo')}
    del _L0_xattn_all

    def _L0_ffn_setup():
        import jax, jax.numpy as jnp
        import numpy as np
        B, L, D = (2, 128, 256)
        E, K = (8, 2)
        H, HS = (176, 352)
        key = jax.random.key(seed)
        ks = jax.random.split(key, 9)
        s = 0.02
        return {'x': jax.random.normal(ks[0], (B, L, D), dtype=jnp.float32), 'gate_w': jax.random.normal(ks[1], (E, D), dtype=jnp.float32) * s, 'w_gate': jax.random.normal(ks[2], (E, D, H), dtype=jnp.float32) * s, 'w_up': jax.random.normal(ks[3], (E, D, H), dtype=jnp.float32) * s, 'w_down': jax.random.normal(ks[4], (E, H, D), dtype=jnp.float32) * s, 'shgate_w': jax.random.normal(ks[5], (D,), dtype=jnp.float32) * s, 'shw_gate': jax.random.normal(ks[6], (D, HS), dtype=jnp.float32) * s, 'shw_up': jax.random.normal(ks[7], (D, HS), dtype=jnp.float32) * s, 'shw_down': jax.random.normal(ks[8], (HS, D), dtype=jnp.float32) * s}
    _L0_ffn_all = _L0_ffn_setup()
    _L0_ffn_in = {k: v for k, v in _L0_ffn_all.items() if k in ('gate_w', 'w_gate', 'w_up', 'w_down', 'shgate_w', 'shw_gate', 'shw_up', 'shw_down')}
    del _L0_ffn_all

    def _L1_xattn_setup():
        import jax, jax.numpy as jnp
        import numpy as np
        B_, L_, D_MODEL = (4, 256, 128)
        D_STATE, D_CONV, EXPAND = (16, 4, 2)
        D_INNER = EXPAND * D_MODEL
        DT_RANK = (D_MODEL + 15) // 16

        def silu(x):
            return x * jax.nn.sigmoid(x)
        key = jax.random.key(seed)
        ks = jax.random.split(key, 10)
        f32 = jnp.float32
        hidden_states = jax.random.normal(ks[0], (B_, L_, D_MODEL), dtype=f32)
        z = jax.random.normal(ks[1], (B_, D_INNER, L_), dtype=f32)
        in_proj_w = jax.random.normal(ks[2], (D_INNER, D_MODEL), dtype=f32) * 0.02
        conv_w = jax.random.normal(ks[3], (D_INNER, 1, D_CONV), dtype=f32) * 0.1
        conv_b = jax.random.normal(ks[4], (D_INNER,), dtype=f32) * 0.02
        x_proj_w = jax.random.normal(ks[5], (DT_RANK + 2 * D_STATE, D_INNER), dtype=f32) * 0.02
        dt_proj_w = jax.random.uniform(ks[6], (D_INNER, DT_RANK), dtype=f32, minval=-DT_RANK ** (-0.5), maxval=DT_RANK ** (-0.5))
        dt = jnp.exp(jax.random.uniform(ks[7], (D_INNER,), dtype=f32, minval=np.log(0.001), maxval=np.log(0.1)))
        dt_proj_b = jnp.log(jnp.expm1(dt))
        A_log = jnp.log(jnp.broadcast_to(jnp.arange(1, D_STATE + 1, dtype=f32), (D_INNER, D_STATE)))
        D = jnp.ones((D_INNER,), f32)
        return {'hidden_states': hidden_states, 'z': z, 'in_proj_w': in_proj_w, 'conv_w': conv_w, 'conv_b': conv_b, 'x_proj_w': x_proj_w, 'dt_proj_w': dt_proj_w, 'dt_proj_b': dt_proj_b, 'A_log': A_log, 'D': D}
    _L1_xattn_all = _L1_xattn_setup()
    _L1_xattn_in = {k: v for k, v in _L1_xattn_all.items() if k in ('in_proj_w', 'conv_w', 'conv_b', 'x_proj_w', 'dt_proj_w', 'dt_proj_b', 'A_log', 'D')}
    del _L1_xattn_all

    def _L1_ffn_setup():
        import jax, jax.numpy as jnp
        import numpy as np
        B, S, H, I = (1, 64, 256, 768)

        def _quantized_matmul(x, w, scale):
            wq = w.astype(jnp.float8_e4m3fn).astype(x.dtype)
            y = jnp.einsum('bsi,io->bso', x, wq)
            return y * scale
        key = jax.random.key(seed)
        ks = jax.random.split(key, 7)
        return {'x': jax.random.normal(ks[0], (B, S, H), dtype=jnp.float32), 'gate_w': jax.random.normal(ks[1], (H, I), dtype=jnp.float32) * 0.02, 'up_w': jax.random.normal(ks[2], (H, I), dtype=jnp.float32) * 0.02, 'down_w': jax.random.normal(ks[3], (I, H), dtype=jnp.float32) * 0.02, 'gate_scale': jax.random.uniform(ks[4], (I,), dtype=jnp.float32, minval=0.5, maxval=1.5), 'up_scale': jax.random.uniform(ks[5], (I,), dtype=jnp.float32, minval=0.5, maxval=1.5), 'down_scale': jax.random.uniform(ks[6], (H,), dtype=jnp.float32, minval=0.5, maxval=1.5)}
    _L1_ffn_all = _L1_ffn_setup()
    _L1_ffn_in = {k: v for k, v in _L1_ffn_all.items() if k in ('gate_w', 'up_w', 'down_w', 'gate_scale', 'up_scale', 'down_scale')}
    del _L1_ffn_all
    return {'x': x, 'ctx_1024': ctx_1024, 'mask_BxS2_bf1': mask_BxS2_bf1, 'L0_xattn_Wq': _L0_xattn_in['Wq'], 'L0_xattn_Wk': _L0_xattn_in['Wk'], 'L0_xattn_Wv': _L0_xattn_in['Wv'], 'L0_xattn_Wo': _L0_xattn_in['Wo'], 'L0_ffn_gate_w': _L0_ffn_in['gate_w'], 'L0_ffn_w_gate': _L0_ffn_in['w_gate'], 'L0_ffn_w_up': _L0_ffn_in['w_up'], 'L0_ffn_w_down': _L0_ffn_in['w_down'], 'L0_ffn_shgate_w': _L0_ffn_in['shgate_w'], 'L0_ffn_shw_gate': _L0_ffn_in['shw_gate'], 'L0_ffn_shw_up': _L0_ffn_in['shw_up'], 'L0_ffn_shw_down': _L0_ffn_in['shw_down'], 'L1_xattn_in_proj_w': _L1_xattn_in['in_proj_w'], 'L1_xattn_conv_w': _L1_xattn_in['conv_w'], 'L1_xattn_conv_b': _L1_xattn_in['conv_b'], 'L1_xattn_x_proj_w': _L1_xattn_in['x_proj_w'], 'L1_xattn_dt_proj_w': _L1_xattn_in['dt_proj_w'], 'L1_xattn_dt_proj_b': _L1_xattn_in['dt_proj_b'], 'L1_xattn_A_log': _L1_xattn_in['A_log'], 'L1_xattn_D': _L1_xattn_in['D'], 'L1_ffn_gate_w': _L1_ffn_in['gate_w'], 'L1_ffn_up_w': _L1_ffn_in['up_w'], 'L1_ffn_down_w': _L1_ffn_in['down_w'], 'L1_ffn_gate_scale': _L1_ffn_in['gate_scale'], 'L1_ffn_up_scale': _L1_ffn_in['up_scale'], 'L1_ffn_down_scale': _L1_ffn_in['down_scale']}

def reference(x, ctx_1024, mask_BxS2_bf1, L0_xattn_Wq, L0_xattn_Wk, L0_xattn_Wv, L0_xattn_Wo, L0_ffn_gate_w, L0_ffn_w_gate, L0_ffn_w_up, L0_ffn_w_down, L0_ffn_shgate_w, L0_ffn_shw_gate, L0_ffn_shw_up, L0_ffn_shw_down, L1_xattn_in_proj_w, L1_xattn_conv_w, L1_xattn_conv_b, L1_xattn_x_proj_w, L1_xattn_dt_proj_w, L1_xattn_dt_proj_b, L1_xattn_A_log, L1_xattn_D, L1_ffn_gate_w, L1_ffn_up_w, L1_ffn_down_w, L1_ffn_gate_scale, L1_ffn_up_scale, L1_ffn_down_scale):
    import jax
    import jax.numpy as jnp

    def _L0_xattn_ref(text_hidden, vision_tokens, vision_mask, Wq, Wk, Wv, Wo):
        import jax, jax.numpy as jnp
        import numpy as np
        N_HEADS = 16
        N_KV_HEADS = 8
        HEAD_DIM = 128
        D_TEXT = 256
        D_VISION = 128
        GROUPS = N_HEADS // N_KV_HEADS
        B, T_text, _ = text_hidden.shape
        T_vis = vision_tokens.shape[1]
        scale = jnp.float32(np.sqrt(HEAD_DIM))
        q = (text_hidden @ Wq).reshape(B, T_text, N_HEADS, HEAD_DIM).transpose(0, 2, 1, 3)
        k = (vision_tokens @ Wk).reshape(B, T_vis, N_KV_HEADS, HEAD_DIM).transpose(0, 2, 1, 3)
        v = (vision_tokens @ Wv).reshape(B, T_vis, N_KV_HEADS, HEAD_DIM).transpose(0, 2, 1, 3)
        k = jnp.repeat(k, GROUPS, axis=1)
        v = jnp.repeat(v, GROUPS, axis=1)
        scores = jnp.einsum('bhtd,bhsd->bhts', q, k) / scale
        mask = vision_mask[:, None, None, :]
        scores = jnp.where(mask, scores, -jnp.inf)
        attn = jax.nn.softmax(scores, axis=-1)
        attn = jnp.nan_to_num(attn, nan=0.0)
        out = jnp.einsum('bhts,bhsd->bhtd', attn, v)
        out = out.transpose(0, 2, 1, 3).reshape(B, T_text, N_HEADS * HEAD_DIM)
        return out @ Wo

    def _L0_ffn_ref(x, gate_w, w_gate, w_up, w_down, shgate_w, shw_gate, shw_up, shw_down):
        import jax, jax.numpy as jnp
        import numpy as np
        B, L, D = (2, 128, 256)
        E, K = (8, 2)
        H, HS = (176, 352)
        b, l, d = x.shape
        xf = x.reshape(-1, d)
        logits = jnp.einsum('td,ed->te', xf.astype(jnp.float32), gate_w)
        probs = jax.nn.softmax(logits.astype(jnp.float32), axis=-1)
        weights, indices = jax.lax.top_k(probs, K)
        weights = (weights / weights.sum(-1, keepdims=True)).astype(x.dtype)
        onehot = jax.nn.one_hot(indices, E, dtype=x.dtype)
        combine = jnp.einsum('tk,tke->te', weights, onehot)
        g = jnp.einsum('td,edh->teh', xf, w_gate)
        u = jnp.einsum('td,edh->teh', xf, w_up)
        h = jax.nn.silu(g) * u
        out = jnp.einsum('teh,ehd,te->td', h.astype(jnp.float32), w_down.astype(jnp.float32), combine.astype(jnp.float32))
        sgate = jax.nn.sigmoid(xf @ shgate_w)[:, None]
        sh = jax.nn.silu(xf @ shw_gate) * (xf @ shw_up) @ shw_down
        out = out + (sgate * sh).astype(jnp.float32)
        return out.astype(x.dtype).reshape(b, l, d)

    def _L1_xattn_ref(hidden_states, z, in_proj_w, conv_w, conv_b, x_proj_w, dt_proj_w, dt_proj_b, A_log, D):
        import jax, jax.numpy as jnp
        import numpy as np
        B_, L_, D_MODEL = (4, 256, 128)
        D_STATE, D_CONV, EXPAND = (16, 4, 2)
        D_INNER = EXPAND * D_MODEL
        DT_RANK = (D_MODEL + 15) // 16

        def silu(x):
            return x * jax.nn.sigmoid(x)
        Bsz, L, _ = hidden_states.shape
        d_inner, _, d_conv = conv_w.shape
        dt_rank = dt_proj_w.shape[1]
        d_state = A_log.shape[1]
        x = jnp.einsum('bld,ed->bel', hidden_states, in_proj_w)
        xc = jax.lax.conv_general_dilated(x, conv_w, window_strides=(1,), padding=[(d_conv - 1, 0)], feature_group_count=d_inner, dimension_numbers=('NCH', 'OIH', 'NCH'))
        x = silu(xc + conv_b[None, :, None])
        x_dbl = jnp.einsum('bdl,ed->bel', x, x_proj_w)
        dt_low, Bm, Cm = jnp.split(x_dbl, [dt_rank, dt_rank + d_state], axis=1)
        dt = jnp.einsum('brl,dr->bdl', dt_low, dt_proj_w)
        dt = jax.nn.softplus(dt + dt_proj_b[None, :, None])
        A = -jnp.exp(A_log)
        dt_t = jnp.moveaxis(dt, -1, 0)
        B_t = jnp.moveaxis(Bm, -1, 0)
        C_t = jnp.moveaxis(Cm, -1, 0)
        u_t = jnp.moveaxis(x, -1, 0)

        def step(state, inp):
            d, b, c, u = inp
            dA = jnp.exp(d[..., None] * A)
            state = state * dA + (d * u)[..., None] * b[:, None, :]
            y = jnp.einsum('bdn,bn->bd', state, c)
            return (state, y)
        state0 = jnp.zeros((Bsz, d_inner, d_state), x.dtype)
        _, ys = jax.lax.scan(step, state0, (dt_t, B_t, C_t, u_t))
        y = jnp.moveaxis(ys, 0, 2)
        y = y + D[None, :, None] * x
        y = y * silu(z)
        return jnp.swapaxes(y, 1, 2)

    def _L1_ffn_ref(x, gate_w, up_w, down_w, gate_scale, up_scale, down_scale):
        import jax, jax.numpy as jnp
        import numpy as np
        B, S, H, I = (1, 64, 256, 768)

        def _quantized_matmul(x, w, scale):
            wq = w.astype(jnp.float8_e4m3fn).astype(x.dtype)
            y = jnp.einsum('bsi,io->bso', x, wq)
            return y * scale
        gate = jax.nn.silu(_quantized_matmul(x, gate_w, gate_scale))
        up = _quantized_matmul(x, up_w, up_scale)
        fuse = gate * up
        return _quantized_matmul(fuse, down_w, down_scale)
    x = x + _L0_xattn_ref(_layernorm(x, axis=-1), ctx_1024, mask_BxS2_bf1, L0_xattn_Wq, L0_xattn_Wk, L0_xattn_Wv, L0_xattn_Wo)
    x = x + _L0_ffn_ref(_layernorm(x, axis=-1), L0_ffn_gate_w, L0_ffn_w_gate, L0_ffn_w_up, L0_ffn_w_down, L0_ffn_shgate_w, L0_ffn_shw_gate, L0_ffn_shw_up, L0_ffn_shw_down)
    x = x + _L1_xattn_ref(ctx_1024, _layernorm(x, axis=-1), L1_xattn_in_proj_w, L1_xattn_conv_w, L1_xattn_conv_b, L1_xattn_x_proj_w, L1_xattn_dt_proj_w, L1_xattn_dt_proj_b, L1_xattn_A_log, L1_xattn_D)
    x = x + _L1_ffn_ref(_layernorm(x, axis=-1), L1_ffn_gate_w, L1_ffn_up_w, L1_ffn_down_w, L1_ffn_gate_scale, L1_ffn_up_scale, L1_ffn_down_scale)
    return x

_drawn_inputs = setup_inputs


def setup_inputs(seed=0):
    import zlib

    import numpy as np

    out = dict(_drawn_inputs(seed))
    spreads = {'L1_xattn_D': (1.0, 0.6)}
    factors = {'L0_xattn_Wq': 8.0,
     'L0_xattn_Wk': 8.0,
     'L0_ffn_gate_w': 6.559,
     'L0_ffn_w_gate': 5.761,
     'L0_ffn_w_up': 5.706,
     'L0_ffn_w_down': 5.702,
     'L0_ffn_shgate_w': 8.0,
     'L0_ffn_shw_gate': 5.827,
     'L0_ffn_shw_up': 5.722,
     'L0_ffn_shw_down': 5.744,
     'L1_xattn_in_proj_w': 4.434,
     'L1_xattn_conv_w': 4.586,
     'L1_xattn_conv_b': 8.0,
     'L1_xattn_x_proj_w': 8.0,
     'L1_xattn_dt_proj_w': 8.0,
     'L1_xattn_dt_proj_b': 8.0,
     'L1_xattn_A_log': 8.0,
     'L1_ffn_gate_scale': 5.319,
     'L1_ffn_up_scale': 6.179,
     'L1_ffn_down_scale': 5.999}
    for name, (base, spread) in spreads.items():
        noise = np.random.default_rng([zlib.crc32(name.encode()), seed]).standard_normal(out[name].shape)
        drawn = base * np.exp(spread * noise) if base else spread * noise
        out[name] = jnp.asarray(drawn.astype(out[name].dtype))
    for name, factor in factors.items():
        out[name] = (out[name] * factor).astype(out[name].dtype)
    return out
```

```python
from contextlib import ExitStack

import concourse.bass as bass
from concourse import mybir

F32 = mybir.dt.float32
F32R = mybir.dt.float32r
U8 = mybir.dt.uint8
I32 = mybir.dt.int32
ALU = mybir.AluOpType
ACT = mybir.ActivationFunctionType
AX = mybir.AxisListType

P = 128
B, T, D = 4, 256, 256
C = 128
H, G = 16, 8
TT = T // P
DB = D // P
E, HE, HS = 8, 176, 352
J0 = -(-(E * HE + HS) // P)
HID1 = 768
J1 = HID1 // P
NS, RANK, TAPS = 16, 8, 4
ET = 2
PAIR = 2 * T
UNITS = B * G
FOLD_COLS = 2 * 2 * D + 2 * C
FFN_COLS = 2 * DB * P + D
EPS = 1e-5
MASKED = 1e30
LOG1P = [1.0000000039388743, 0.3333315796754004, 0.2001242686175179, 0.13980709417160408, 0.14087328632654456]

SMALL = [
    ("ident", P), ("in_w", ET * P), ("xp_w", ET * P), ("dt_w", ET * P), ("a_log", ET * NS),
    ("conv_w", ET * TAPS), ("conv_b", ET), ("dt_b", ET), ("d_skip", ET), ("g_scale", J1),
    ("u_scale", J1), ("route_w", DB * 10), ("lower", E * E), ("sel", NS),
]
SMALL_AT = {}
SMALL_COLS = 0
for _name, _n in SMALL:
    SMALL_AT[_name] = (SMALL_COLS, SMALL_COLS + _n)
    SMALL_COLS += _n


def timeline():
    steps = [("ctx", 0), ("ln", (0, 0)), ("prep", 0)]
    steps += [("fold", g) for g in range(G)]
    steps += [("ln", (0, 1)), ("scanB", 0), ("Q", 0)]
    v = 0
    for i in range(UNITS + 3):
        b, g = divmod(i, G)
        if i + 1 < UNITS:
            steps.append(("Q", i + 1))
        if i < UNITS:
            steps.append(("S", i))
        if i % 2 == 0 and v < NS:
            steps.append(("scanC", v))
        if 1 <= i <= UNITS:
            steps.append(("T", i - 1))
        if 2 <= i <= UNITS + 1:
            steps.append(("V", i - 2))
        if i < UNITS:
            steps.append(("N", i))
        if i >= 3:
            steps.append(("O", i - 3))
            if (i - 3) % G == G - 1:
                steps.append(("res", (i - 3) // G))
        if i % 2 == 0 and v < NS:
            v += 1
            if v < NS:
                steps.append(("scanB", v))
        if g == 5 and b in (0, 1):
            steps.append(("ln", (0, b + 2)))
        if g == 5 and b in (1, 2, 3):
            steps.append(("ln", (1, b - 1)))
        if i >= UNITS + 1:
            steps.append(("W", i - UNITS - 1))
    steps.append(("ln", (1, 3)))
    steps.append(("route", 0))
    nw, wq, v = 2, 0, NS
    f0 = 2 * J0
    for m in range(f0 + 2 * J1):
        k, j = (m // J0, m % J0) if m < f0 else (2 + (m - f0) // J1, (m - f0) % J1)
        steps.append(("G", m))
        if m >= 1:
            steps.append(("D", m - 1))
        if j == 0 and k >= 1:
            steps.append(("acc", k - 1))
        if m == 1:
            steps += [("route", 1), ("prep", 1), ("scanB", v)]
        elif 3 <= m and v < 2 * NS:
            steps.append(("scanC", v))
            v += 1
            if v < 2 * NS:
                steps.append(("scanB", v))
        if nw < f0:
            steps.append(("W", nw))
            nw += 1
        if m >= 15 and m % 2 == 1 and wq < J1:
            steps.append(("W1", wq))
            wq += 1
        if (k, j) in ((1, 2), (2, 2)):
            p = k - 1
            for b in (2 * p, 2 * p + 1):
                steps += [("gatey", b), ("ln", (3, b))]
    steps += [("D", f0 + 2 * J1 - 1), ("acc", 3)]
    return steps


STEPS = timeline()


def build_program(nc, x, ctx_n, ctx_t, fold_w, ffn_w, small, expert_sel, mask, down_scale, out):
    stack = ExitStack()
    with stack:
        def sb(name, shape, dt=F32):
            return stack.enter_context(nc.sbuf_tensor(name, shape, dt))

        def sem(name):
            return stack.enter_context(nc.semaphore(name))

        xs = sb("xs", [P, B * TT, D])
        cn = [sb(f"cn_{s}", [P, B * TT, C], F32R) for s in ("hi", "lo")]
        ct = [sb(f"ct_{s}", [P, B * T], F32R) for s in ("hi", "lo")]
        stage = sb("stage", [P, 2560])
        stage_fold = stage[:, :].rearrange("p (s n) -> p s n", s=2)
        stage_ffn = stage[:, 0:3 * FFN_COLS].rearrange("p (s n) -> p s n", s=3)
        mw = [sb(f"mw_{s}", [P, G * 512], F32R) for s in ("hi", "lo")]
        nw = [sb(f"nw_{s}", [P, G * 512], F32R) for s in ("hi", "lo")]
        xnt = [sb(f"xnt_{s}", [P, DB, B * T], F32R) for s in ("hi", "lo")]
        qt = [sb(f"qt_{s}", [P, 2, 512], F32R) for s in ("hi", "lo")]
        prob = sb("prob", [P, 4, 512])
        pt = [sb(f"pt_{s}", [P, TT, 2, T], F32R) for s in ("hi", "lo")]
        ot = [sb(f"ot_{s}", [P, 2, 512], F32R) for s in ("hi", "lo")]
        sm = sb("sm", [P, SMALL_COLS])
        mask_sb = sb("mask_sb", [P, B * T], U8)
        mask_bias = sb("mask_bias", [P, 2, T])
        mask_any = sb("mask_any", [P, B])
        dscale = sb("dscale", [P, D])
        s_max = sb("s_max", [P, 2, 4])
        s_bias = sb("s_bias", [P, 2, 4])
        s_sum = sb("s_sum", [P, 2, 4])
        s_inv = sb("s_inv", [P, 2, 4])
        xn = sb("xn", [P, TT, D])
        bn = sb("bn", [P, TT, 6])
        mv = sb("mv", [P, TT, 2])
        rstd = sb("rstd", [P, TT])
        neg_half = sb("neg_half", [P, TT])
        front = sb("front", [P, 4, 512])
        xc = front[:, 0:2, :]
        bb = front[:, 0:2, :]
        uu = front[:, 2:4, :]
        da = front[:, 2:4, :]
        dtt = sb("dtt", [P, ET, 512])
        dtu = sb("dtu", [P, ET, 512])
        ys = sb("ys", [P, ET, B * T])
        bc = sb("bc", [P, 512], F32R)
        dtl = sb("dtl", [RANK, 512])
        sel = sb("sel", [P, NS, P], F32R)
        ring = sb("ring", [P, 3, 512])
        acoef = sb("acoef", [P, ET, NS])
        lg = sb("lg", [P, 4, 10])
        ex = sb("ex", [P, 4, 10])
        r1 = sb("r1", [P, 4, 1])
        cmp_ = sb("cmp_", [P, FFN_COLS])
        gt, eq = (cmp_[:, a:a + 4 * E * E].rearrange("p (t e j) -> p t e j", t=4, e=E) for a in (0, 4 * E * E))
        rk = sb("rk", [P, 4, E])
        cm = sb("cm", [P, 4, 64])
        rw = [sb(f"rw_{s}", [P, DB * 10], F32R) for s in ("hi", "lo")]
        ucoef = sb("ucoef", [P, J1])
        gcoef = sb("gcoef", [P, J1])
        ysb = sb("ysb", [P, TT, D])
        in_split = [sb(f"in_split_{s}", [P, ET * P], F32R)[:, :] for s in ("hi", "lo")]
        q1c = cmp_[:, :]

        bank = [stack.enter_context(nc.psum_tensor(f"bank{i}", [P, 512], F32)) for i in range(8)]
        misc = bank[7]

        def small_(name):
            a, b = SMALL_AT[name]
            return sm[:, a:b]

        ident = small_("ident")
        in_w, xp_w = small_("in_w"), small_("xp_w")
        dt_w = small_("dt_w")[0:RANK, :]
        conv_w, conv_b, dt_b, d_skip = (small_(n) for n in ("conv_w", "conv_b", "dt_b", "d_skip"))

        wslot = [[w[:, s * FFN_COLS:(s + 1) * FFN_COLS] for s in range(3)] for w in mw]
        w1slot = [t[:, a:a + FFN_COLS] for t, a in ((mw[0], 2304), (mw[0], 3072), (mw[1], 2304), (mw[1], 3072), (nw[1], 2560), (nw[1], 3328))]
        hid = [[w[:, s * 512:(s + 1) * 512] for s in range(2)] for w in nw]
        esel = nw[0][0:64, 1024:1024 + J0 * P]
        combt = [nw[0][0:64, 2816:2816 + 512], nw[0][0:64, 3328:3328 + 512]]

        x_in, small_in, ctx_in, mask_in, esel_in, dsc_in = (sem(n) for n in ("x_in", "small_in", "ctx_in", "mask_in", "esel_in", "dsc_in"))
        fold_in = [sem(f"fold_in{i}") for i in range(2)]
        ffn_in = [sem(f"ffn_in{i}") for i in range(3)]
        out_done = sem("out_done")
        v_chain, g_const, q1_added = sem("v_chain"), sem("g_const"), sem("q1_added")
        misc_filled, misc_done = sem("misc_filled"), sem("misc_done")
        ctx_hi, ctx_lo = sem("ctx_hi"), sem("ctx_lo")
        m_filled, n_filled = sem("m_filled"), sem("n_filled")
        m_hi, m_lo, n_hi, n_lo = (sem(n) for n in ("m_hi", "m_lo", "n_hi", "n_lo"))
        mv_ready, rstd_ready = sem("mv_ready"), sem("rstd_ready")
        xn_ready, xt_hi = sem("xn_ready"), sem("xt_hi")
        q_filled, q_hi, q_lo = sem("q_filled"), sem("q_hi"), sem("q_lo")
        s_filled, s_masked, s_biased = sem("s_filled"), sem("s_masked"), sem("s_biased")
        p_exp, p_inv, p_norm = sem("p_exp"), sem("p_inv"), sem("p_norm")
        t_filled, t_hi, t_lo = sem("t_filled"), sem("t_hi"), sem("t_lo")
        v_filled, o_hi, o_lo, o_summed = (sem(n) for n in ("v_filled", "o_hi", "o_lo", "o_summed"))
        res_done = sem("res_done")
        mbias_ready = sem("mbias_ready")
        pre_tanh, pre_u, pre_bc_hi, pre_dtl, pre_na, pre_e, dt_ready, dtu_ready = (
            sem(n) for n in ("pre_tanh", "pre_u", "pre_bc_hi", "pre_dtl", "pre_na", "pre_e", "dt_ready", "dtu_ready"))
        a_exp, sel_ready = sem("a_exp"), sem("sel_ready")
        b_ready, da_ready, dbu_ready, scanned, hc_ready, y_added = (
            sem(n) for n in ("b_ready", "da_ready", "dbu_ready", "scanned", "hc_ready", "y_added"))
        yg_norm, yg_tanh, yg_ready = sem("yg_norm"), sem("yg_tanh"), sem("yg_ready")
        lg_ready, lg_exp, cm_ready, ct_hi = (sem(n) for n in ("lg_ready", "lg_exp", "cm_ready", "ct_hi"))
        w_hi, w_lo = sem("w_hi"), sem("w_lo")
        q1_scale, q1_round, w1_ready = sem("q1_scale"), sem("q1_round"), sem("w1_ready")
        g_filled, u_filled, c_filled = sem("g_filled"), sem("u_filled"), sem("c_filled")
        h_tanh, h_g, h_u, h_c, h_hi, h_lo = (sem(n) for n in ("h_tanh", "h_g", "h_u", "h_c", "h_hi", "h_lo"))
        d_done, acc_done, out_ready = sem("d_done"), sem("acc_done"), sem("out_ready")

        use = {}
        for kind, arg in STEPS:
            mine = {"ln": [("ln", arg)], "prep": [("in", arg, 0), ("in", arg, 1), ("xp", arg), ("dt", arg, 0), ("dt", arg, 1)],
                    "scanB": [("B", arg)], "scanC": [("C", arg)], "gatey": [("yt", arg)],
                    "route": [("lg", arg), ("cT", arg)]}.get(kind, [])
            for key in mine:
                use[key] = len(use)
        ln_no = {arg: n for n, arg in enumerate(a for k, a in STEPS if k == "ln")}

        F0 = 2 * J0
        ITEMS = F0 + 2 * J1

        def phase(m):
            return (m // J0, m % J0) if m < F0 else (2 + (m - F0) // J1, (m - F0) % J1)

        def acc_banks(k):
            return (bank[0], bank[1]) if k % 2 == 0 else (bank[5], bank[6])

        def last_item(k):
            return (J0, 2 * J0, F0 + J1, ITEMS)[k] - 1

        loads = [(k, a) for k, a in STEPS if k in ("fold", "W", "W1")]
        ffn_loads = [x for x in loads if x[0] != "fold"]
        ffn_slot = {key: (n % 3, n // 3 + 1) for n, key in enumerate(ffn_loads)}

        block = stack.enter_context(nc.Block())

        @block.sync
        def _(sp):
            sp.dma_start(xs[:, 0:TT, :], x.rearrange("(n p) d -> p n d", p=P)[:, 0:TT, :]).then_inc(x_in, 16)
            sp.dma_start(sm[:, :], small).then_inc(small_in, 16)
            sp.dma_start(prob[:, 0:2, :].rearrange("p a n -> p (a n)"), ctx_t).then_inc(ctx_in, 16)
            sp.dma_start(prob[:, 2:4, :].rearrange("p a n -> p (a n)").rearrange("p (n c) -> p n c", c=C),
                         ctx_n.rearrange("(n p) c -> p n c", p=P)).then_inc(ctx_in, 16)
            for g in range(2):
                sp.dma_start(stage_fold[:, g, :], fold_w[g]).then_inc(fold_in[g], 16)
            sp.dma_start(xs[:, TT:, :], x.rearrange("(n p) d -> p n d", p=P)[:, TT:, :]).then_inc(x_in, 16)
            sp.dma_start(mask_sb[:, :], mask.unsqueeze(0).to_broadcast([P, B * T])).then_inc(mask_in, 16)
            sp.dma_start(dscale[:, :], down_scale.unsqueeze(0).to_broadcast([P, D])).then_inc(dsc_in, 16)
            for g in range(2, G):
                sp.wait_ge(n_filled, g - 1)
                sp.dma_start(stage_fold[:, g % 2, :], fold_w[g]).then_inc(fold_in[g % 2], 16)
            for n, (kind, a) in enumerate(ffn_loads):
                if n == 0:
                    sp.wait_ge(n_filled, G)
                if n >= 3:
                    before, j = ffn_loads[n - 3]
                    sp.wait_ge(w_lo if before == "W" else w1_ready, j + 1)
                row = a % J0 if kind == "W" else J0 + a
                sp.dma_start(stage_ffn[:, n % 3, :], ffn_w[row]).then_inc(ffn_in[n % 3], 16)
            for b in range(B):
                sp.wait_ge(out_ready, b + 1)
                sp.dma_start(out.rearrange("(n p) d -> p n d", p=P)[:, b * TT:(b + 1) * TT, :],
                             xs[:, b * TT:(b + 1) * TT, :]).then_inc(out_done, 16)
            sp.wait_ge(out_done, 16 * B)

        @block.tensor
        def _(pe):
            def three(bank_ap, a, b, start, stop, skip=False):
                terms = [(a[0], b[0])]
                if b[1] is not None:
                    terms.append((a[0], b[1]))
                if a[1] is not None:
                    terms.append((a[1], b[0]))
                for n, (l, r) in enumerate(terms):
                    last = nc.tensor.matmul(bank_ap, l, r, start=start and n == 0, stop=stop and n == len(terms) - 1,
                                            skip_group_check=skip)
                return last

            def take_misc(key):
                if use[key]:
                    pe.wait_ge(misc_done, use[key])

            def fold(g):
                pe.wait_ge(fold_in[g % 2], 16 * (g // 2 + 1))
                wq = stage_fold[:, g % 2, 0:512]
                wo = stage_fold[:, g % 2, 512:1024]
                wk = stage_fold[:, g % 2, 1024:1152]
                wv = stage_fold[:, g % 2, 1152:1280]
                if g >= 2:
                    pe.wait_ge(m_lo, g - 1)
                for h in range(2):
                    for d in range(DB):
                        last = nc.tensor.matmul(bank[2 + g % 2][:, (h * DB + d) * P:(h * DB + d + 1) * P],
                                                wq[:, h * D + d * P:h * D + (d + 1) * P], wk, start=True, stop=True)
                last.then_inc(m_filled, 1)
                if g >= 2:
                    pe.wait_ge(n_lo, g - 1)
                nc.tensor.matmul(bank[4 + g % 2][:, :], wv, wo, start=True, stop=True).then_inc(n_filled, 1)

            def ln(arg):
                kind, b = arg
                pe.wait_ge(xn_ready, ln_no[arg] + 1)
                take_misc(("ln", arg))
                for d in range(DB):
                    for t in range(TT):
                        last = nc.tensor.transpose(misc[:, d * T + t * P:d * T + (t + 1) * P],
                                                   xn[:, t, d * P:(d + 1) * P], ident)
                last.then_inc(misc_filled, 1)

            def prep(p):
                pair = slice(p * PAIR, (p + 1) * PAIR)
                if p == 0:
                    pe.wait_ge(small_in, 16)
                    pe.wait_ge(ctx_lo, 1)
                    pe.wait_ge(ctx_in, 32)
                cth, ctl = ct[0][:, pair], ct[1][:, pair]
                for e in range(ET):
                    take_misc(("in", p, e))
                    if p == 0 and e == 0:
                        pe.wait_ge(sel_ready, 1)
                    w = [t[:, e * P:(e + 1) * P] for t in in_split]
                    three(misc[:, :], w, (cth, ctl), True, True).then_inc(misc_filled, 1)
                take_misc(("xp", p))
                pe.wait_ge(pre_u, 2 * p + 2)
                for e in range(ET):
                    last = nc.tensor.matmul(misc[:, :], xp_w[:, e * P:(e + 1) * P], uu[:, e, :], start=e == 0, stop=e == ET - 1)
                last.then_inc(misc_filled, 1)
                pe.wait_ge(pre_dtl, p + 1)
                for e in range(ET):
                    take_misc(("dt", p, e))
                    nc.tensor.matmul(misc[:, :], dt_w[:, e * P:(e + 1) * P], dtl[:, :], start=True, stop=True).then_inc(misc_filled, 1)

            def scan_b(v):
                take_misc(("B", v))
                nc.tensor.matmul(misc[:, :], sel[0:64, v % NS, :], bc[0:64, :], start=True, stop=True).then_inc(misc_filled, 1)

            def scan_c(v):
                take_misc(("C", v))
                nc.tensor.matmul(misc[:, :], sel[64:128, v % NS, :], bc[64:128, :], start=True, stop=True).then_inc(misc_filled, 1)

            def q_part(u):
                b, g = divmod(u, G)
                pe.wait_ge(misc_done, use[("ln", (0, b))] + 1)
                if u == 0:
                    pe.wait_ge(m_lo, G)
                else:
                    pe.wait_ge(q_lo, u)
                for h in range(2):
                    for d in range(DB):
                        at = g * 512 + (h * DB + d) * P
                        last = three(bank[1][:, h * T:(h + 1) * T], [w[:, at:at + P] for w in mw],
                                     [w[:, d, b * T:(b + 1) * T] for w in xnt], d == 0, d == DB - 1)
                last.then_inc(q_filled, 1)

            def s_part(u):
                b, g = divmod(u, G)
                pe.wait_ge(q_lo, u + 1)
                for h in range(2):
                    if u:
                        pe.wait_ge(s_masked, 2 * u - 1 + h)
                    for t in range(TT):
                        last = three(bank[2 + h][:, t * T:(t + 1) * T],
                                     [w[:, u % 2, h * T + t * P:h * T + (t + 1) * P] for w in qt],
                                     [w[:, b * T:(b + 1) * T] for w in ct], True, True)
                    last.then_inc(s_filled, 1)

            def t_part(u):
                pe.wait_ge(p_norm, u + 1)
                for h in range(2):
                    if u:
                        pe.wait_ge(t_lo, 2 * u - 1 + h)
                    elif h == 0:
                        pe.wait_ge(n_lo, G)
                    for t in range(TT):
                        for s in range(TT):
                            last = nc.tensor.transpose(bank[4 + h][:, s * T + t * P:s * T + (t + 1) * P],
                                                       prob[:, u % 2 * 2 + h, t * T + s * P:t * T + (s + 1) * P], ident)
                    last.then_inc(t_filled, 1)

            def v_part(u):
                b = u // G
                pe.wait_ge(t_lo, 2 * u + 2)
                if u:
                    pe.wait_ge(o_lo, u)
                for s in range(TT):
                    last = three(bank[6][:, :], [w[:, b * TT + s, :] for w in cn],
                                 [w[:, s, :, :].rearrange("p h t -> p (h t)") for w in pt], s == 0, s == TT - 1)
                last.then_inc(v_filled, 1)

            def o_part(u):
                b, g = divmod(u, G)
                pe.wait_ge(o_lo, u + 1)
                if g == 0 and b:
                    pe.wait_ge(res_done, b)
                for t in range(TT):
                    for h in range(2):
                        last = three(bank[0][:, t * D:(t + 1) * D],
                                     [w[:, u % 2, h * T + t * P:h * T + (t + 1) * P] for w in ot],
                                     [w[:, g * 512 + h * D:g * 512 + (h + 1) * D] for w in nw],
                                     g == 0 and t == 0 and h == 0, g == G - 1 and h == 1, skip=True)
                last.then_inc(o_summed, 1)

            def route(p):
                take_misc(("lg", p))
                pe.wait_ge(misc_done, use[("ln", (1, 2 * p + 1))] + 1)
                for t in range(4):
                    at = p * PAIR + t * P
                    for d in range(DB):
                        last = three(misc[:, t * 10:(t + 1) * 10], [w[:, d, at:at + P] for w in xnt],
                                     [w[:, d * 10:(d + 1) * 10] for w in rw], d == 0, d == DB - 1)
                last.then_inc(misc_filled, 1)
                take_misc(("cT", p))
                pe.wait_ge(cm_ready, p + 1)
                for t in range(4):
                    last = nc.tensor.transpose(misc[0:64, t * P:(t + 1) * P], cm[:, t, :], ident)
                last.then_inc(misc_filled, 1)

            def g_part(m):
                k, j = phase(m)
                p = k % 2
                if m < F0:
                    pe.wait_ge(w_lo, m + 1)
                    ws = [wslot[0][m % 3], wslot[1][m % 3]]
                    pe.wait_ge(misc_done, use[("ln", (1, 2 * p + 1))] + 1)
                else:
                    pe.wait_ge(w1_ready, j + 1)
                    ws = [w1slot[j], None]
                    pe.wait_ge(misc_done, use[("ln", (3, 2 * p + 1))] + 1)
                for n, (filled, read) in enumerate(((g_filled, h_g), (u_filled, h_u))):
                    if m:
                        pe.wait_ge(read, m)
                    else:
                        pe.wait_ge(s_masked, 2 * UNITS)
                    for d in range(DB):
                        at = n * DB * P + d * P
                        last = three(bank[2 + n][:, :], [w if w is None else w[:, at:at + P] for w in ws],
                                     [w[:, d, p * PAIR:(p + 1) * PAIR] for w in xnt], d == 0, d == DB - 1)
                    last.then_inc(filled, 1)
                if m < F0:
                    if m:
                        pe.wait_ge(h_c, m)
                    else:
                        pe.wait_ge(t_lo, 2 * UNITS)
                        pe.wait_ge(esel_in, 16)
                    pe.wait_ge(misc_done, use[("cT", p)] + 1)
                    nc.tensor.matmul(bank[4][:, :], esel[:, j * P:(j + 1) * P], combt[p], start=True, stop=True).then_inc(c_filled, 1)

            def d_part(m):
                k, j = phase(m)
                pe.wait_ge(h_lo, m + 1)
                down = 2 * DB * P
                if m < F0:
                    ws = [w[:, down:down + D] for w in (wslot[0][m % 3], wslot[1][m % 3])]
                else:
                    ws = [w1slot[j][:, down:down + D], None]
                if j == 0:
                    if k >= 2:
                        pe.wait_ge(acc_done, k - 1)
                    elif k == 1:
                        pe.wait_ge(o_lo, UNITS)
                    else:
                        pe.wait_ge(res_done, B)
                        pe.wait_ge(q_lo, UNITS)
                banks = acc_banks(k)
                n_items = J0 if k < 2 else J1
                for t in range(4):
                    last = three(banks[t // 2][:, t % 2 * D:(t % 2 + 1) * D],
                                 [w[m % 2][:, t * P:(t + 1) * P] for w in hid], ws,
                                 j == 0 and t % 2 == 0, j == n_items - 1, skip=True)
                last.then_inc(d_done, 1)

            def gatey(b):
                take_misc(("yt", b))
                pe.wait_ge(yg_ready, b + 1)
                for t in range(TT):
                    for e in range(ET):
                        last = nc.tensor.transpose(misc[:, t * D + e * P:t * D + (e + 1) * P], ysb[:, e, t * P:(t + 1) * P], ident)
                last.then_inc(misc_filled, 1)

            do = {"fold": fold, "ln": ln, "prep": prep, "scanB": scan_b, "scanC": scan_c, "Q": q_part, "S": s_part,
                  "T": t_part, "V": v_part, "O": o_part, "route": route, "G": g_part, "D": d_part, "gatey": gatey}
            for kind, a in STEPS:
                if kind in do:
                    do[kind](a)

        @block.scalar
        def _(act):
            def copy(dst, src, scale=1.0):
                return nc.scalar.activation(dst, src, ACT.Copy, scale=scale)

            def misc_ready(key):
                act.wait_ge(misc_filled, use[key] + 1)

            def ctx(_):
                act.wait_ge(ctx_in, 32)
                copy(ct[0][:, :], prob[:, 0:2, :].rearrange("p a n -> p (a n)"))
                copy(cn[0][:, :, :].rearrange("p n c -> p (n c)"),
                     prob[:, 2:4, :].rearrange("p a n -> p (a n)")).then_inc(ctx_hi, 1)
                act.wait_ge(small_in, 16)
                copy(in_split[0], in_w)
                copy(rw[0][:, :], small_("route_w"))
                nc.scalar.activation(acoef[:, :, :].rearrange("p e n -> p (e n)"), small_("a_log"), ACT.Exp).then_inc(a_exp, 1)

            def fold(g):
                act.wait_ge(m_filled, g + 1)
                copy(mw[0][:, g * 512:(g + 1) * 512], bank[2 + g % 2][:, :]).then_inc(m_hi, 1)
                act.wait_ge(n_filled, g + 1)
                copy(nw[0][:, g * 512:(g + 1) * 512], bank[4 + g % 2][:, :]).then_inc(n_hi, 1)

            def ln(arg):
                kind, b = arg
                if kind == 1:
                    act.wait_ge(q_filled, G * (b + 1))
                elif kind == 3:
                    act.wait_ge(g_filled, J0 * (b // 2 + 1))
                    act.wait_ge(u_filled, J0 * (b // 2 + 1))
                misc_ready(("ln", arg))
                copy(xnt[0][:, :, b * T:(b + 1) * T], misc[:, :].rearrange("p (d t) -> p d t", d=DB)).then_inc(xt_hi, 1)

            def prep(p):
                for e in range(ET):
                    act.wait_ge(misc_done, use[("in", p, e)] + 1)
                    nc.scalar.activation(dtu[:, e, :], xc[:, e, :], ACT.Tanh, scale=0.5).then_inc(pre_tanh, 1)
                misc_ready(("xp", p))
                copy(bc[:, :], misc[:, :], 0.5).then_inc(pre_bc_hi, 1)
                copy(dtl[:, :], misc[0:RANK, :], 0.5).then_inc(pre_dtl, 1)
                act.wait_ge(pre_na, p + 1)
                nc.scalar.activation(dtt[:, :, :], dtt[:, :, :], ACT.Exp).then_inc(pre_e, 1)

            def scan_b(v):
                p, n = divmod(v, NS)
                misc_ready(("B", v))
                if n >= 2:
                    act.wait_ge(dbu_ready, 2 * (v - 1))
                elif n == 0:
                    act.wait_ge(dtu_ready, p + 1)
                copy(bb[:, v % 2, :], misc[:, :]).then_inc(misc_done, 1)
                for e in range(ET):
                    if n:
                        act.wait_ge(scanned, 2 * v - 1 + e)
                    nc.scalar.activation(da[:, e, :].rearrange("p (b l) -> p b l", b=2)[:, :, 1:T],
                                         dtt[:, e, :].rearrange("p (b l) -> p b l", b=2)[:, :, 1:T], ACT.Exp,
                                         scale=acoef[:, e, n:n + 1]).then_inc(da_ready, 1)

            def q_part(u):
                act.wait_ge(q_filled, u + 1)
                if u >= 2:
                    act.wait_ge(s_filled, 2 * (u - 1))
                copy(qt[0][:, u % 2, :], bank[1][:, :]).then_inc(q_hi, 1)

            def s_part(u):
                for h in range(2):
                    act.wait_ge(s_biased, 2 * u + h + 1)
                    for t in range(TT):
                        i = 2 * h + t
                        s = prob[:, u % 2 * 2 + h, t * T:(t + 1) * T]
                        last = nc.scalar.activation(s, s, ACT.Exp, bias=s_bias[:, u % 2, i:i + 1], scale=float(P) ** -0.5,
                                                    accum_out=s_sum[:, u % 2, i:i + 1])
                    last.then_inc(p_exp, 1)

            def t_part(u):
                for h in range(2):
                    act.wait_ge(t_filled, 2 * u + h + 1)
                    if u and h == 0:
                        act.wait_ge(v_filled, u)
                    copy(pt[0][:, :, h, :], bank[4 + h][:, :].rearrange("p (s t) -> p s t", s=TT)).then_inc(t_hi, 1)

            def v_part(u):
                act.wait_ge(v_filled, u + 1)
                if u >= 2:
                    act.wait_ge(o_summed, u - 1)
                copy(ot[0][:, u % 2, :], bank[6][:, :]).then_inc(o_hi, 1)

            def route(p):
                act.wait_ge(lg_ready, p + 1)
                nc.scalar.activation(ex[:, :, 0:9], lg[:, :, 0:9], ACT.Exp).then_inc(lg_exp, 1)
                misc_ready(("cT", p))
                if p == 0:
                    act.wait_ge(o_summed, UNITS)
                copy(combt[p], misc[0:64, :]).then_inc(ct_hi, 1)

            def w_part(m):
                slot, times = ffn_slot[("W", m)]
                act.wait_ge(ffn_in[slot], 16 * times)
                if m == 0:
                    act.wait_ge(q_filled, UNITS)
                if m >= 3:
                    act.wait_ge(d_done, m - 2)
                copy(wslot[0][m % 3], stage_ffn[:, slot, :]).then_inc(w_hi, 1)

            def g_part(m):
                k, j = phase(m)
                act.wait_ge(g_filled, m + 1)
                if m >= 4:
                    act.wait_ge(h_lo, m - 3)
                if m < F0:
                    nc.scalar.activation(prob[:, m % 4, :], bank[2][:, :], ACT.Tanh, scale=0.5).then_inc(h_tanh, 1)
                else:
                    nc.scalar.activation(prob[:, m % 4, :], bank[2][:, :], ACT.Tanh, scale=gcoef[:, j:j + 1]).then_inc(h_tanh, 1)
                act.wait_ge(h_c, m + 1)
                if m >= 2:
                    act.wait_ge(d_done, m - 1)
                else:
                    act.wait_ge(o_summed, UNITS)
                copy(hid[0][m % 2], prob[:, m % 4, :]).then_inc(h_hi, 1)

            def gatey(b):
                act.wait_ge(yg_norm, b + 1)
                if b:
                    act.wait_ge(misc_filled, use[("yt", b - 1)] + 1)
                nc.scalar.activation(ysb[:, :, :], xn[:, :, :], ACT.Tanh, scale=0.5).then_inc(yg_tanh, 1)

            do = {"ctx": ctx, "fold": fold, "ln": ln, "prep": prep, "scanB": scan_b, "Q": q_part, "S": s_part, "T": t_part,
                  "V": v_part, "route": route, "W": w_part, "G": g_part, "gatey": gatey}
            for kind, a in STEPS:
                if kind in do:
                    do[kind](a)

        @block.vector
        def _(dve):
            v_ = nc.vector
            chain = [0]

            def link(ins):
                chain[0] += 1
                ins.then_inc(v_chain, 1)
                dve.wait_ge(v_chain, chain[0])

            def misc_ready(key):
                dve.wait_ge(misc_filled, use[key] + 1)

            def ctx(_):
                dve.wait_ge(ctx_hi, 1)
                v_.tensor_tensor(ct[1][:, :], prob[:, 0:2, :].rearrange("p a n -> p (a n)"), ct[0][:, :].bitcast(F32), ALU.subtract)
                v_.tensor_tensor(cn[1][:, :, :].rearrange("p n c -> p (n c)"), prob[:, 2:4, :].rearrange("p a n -> p (a n)"),
                                 cn[0][:, :, :].rearrange("p n c -> p (n c)").bitcast(F32), ALU.subtract).then_inc(ctx_lo, 1)
                dve.wait_ge(a_exp, 1)
                v_.tensor_tensor(rw[1][:, :], small_("route_w"), rw[0][:, :].bitcast(F32), ALU.subtract)
                a = acoef[:, :, :]
                v_.tensor_scalar(a, a, -1.0, None, ALU.mult)
                v_.tensor_scalar(gcoef[:, :], small_("g_scale"), 0.5, None, ALU.mult)
                v_.scalar_tensor_tensor(ucoef[:, :], small_("g_scale"), 0.5, small_("u_scale"), ALU.mult, ALU.mult)
                v_.memset(cm[:, :, :], 0.0)
                v_.tensor_tensor(in_split[1], in_w, in_split[0].bitcast(F32), ALU.subtract)
                v_.tensor_copy(sel[:, :, :], small_("sel").unsqueeze(2).to_broadcast([P, NS, P])).then_inc(sel_ready, 1)
                dve.wait_ge(mask_in, 16)
                v_.reduce_max(mask_any[:, :], mask_sb[:, :].rearrange("p (b t) -> p b t", b=B), AX.X)

            def fold(g):
                for w, b, hi, lo in ((mw, 2, m_hi, m_lo), (nw, 4, n_hi, n_lo)):
                    at = slice(g * 512, (g + 1) * 512)
                    dve.wait_ge(hi, g + 1)
                    v_.tensor_tensor(w[1][:, at], bank[b + g % 2][:, :], w[0][:, at].bitcast(F32), ALU.subtract).then_inc(lo, 1)

            def normalise(b, readers):
                for t in range(TT):
                    last = v_.bn_stats(bn[:, t, :], xs[:, b * TT + t, :])
                link(last)
                for t in range(TT):
                    last = v_.bn_aggr(mv[:, t, :], bn[:, t, :])
                link(last)
                v_.tensor_scalar(rstd[:, :].unsqueeze(2), mv[:, :, 1:2], EPS, None, ALU.add).then_inc(mv_ready, 1)
                normed[0] += 1
                dve.wait_ge(rstd_ready, normed[0])
                if readers:
                    dve.wait_ge(misc_filled, readers)
                for t in range(TT):
                    last = v_.tensor_scalar(xn[:, t, :], xs[:, b * TT + t, :], mv[:, t, 0:1], rstd[:, t:t + 1],
                                            ALU.subtract, ALU.mult)
                return last

            last_xn_use = [0]
            normed = [0]

            def ln(arg):
                kind, b = arg
                if kind == 0:
                    dve.wait_ge(x_in, 16 if b == 0 else 32)
                normalise(b, last_xn_use[0]).then_inc(xn_ready, 1)
                last_xn_use[0] = use[("ln", arg)] + 1
                dve.wait_ge(xt_hi, ln_no[arg] + 1)
                at = slice(b * T, (b + 1) * T)
                v_.tensor_tensor(xnt[1][:, :, at], misc[:, :].rearrange("p (d t) -> p d t", d=DB),
                                 xnt[0][:, :, at].bitcast(F32), ALU.subtract).then_inc(misc_done, 1)

            def prep(p):
                for e in range(ET):
                    misc_ready(("in", p, e))
                    if p and e == 0:
                        dve.wait_ge(scanned, 2 * NS)
                        dve.wait_ge(dbu_ready, 2 * NS)
                    w = conv_w[:, e * TAPS:(e + 1) * TAPS]
                    link(v_.tensor_scalar(xc[:, e, :], misc[:, :], w[:, TAPS - 1:TAPS], conv_b[:, e:e + 1], ALU.mult, ALU.add))
                    for back in range(1, TAPS):
                        o = xc[:, e, :].rearrange("p (b l) -> p b l", b=2)[:, :, back:T]
                        i = misc[:, :].rearrange("p (b l) -> p b l", b=2)[:, :, 0:T - back]
                        last = v_.scalar_tensor_tensor(o, i, w[:, TAPS - 1 - back:TAPS - back], o, ALU.mult, ALU.add)
                        if back < TAPS - 1:
                            link(last)
                    last.then_inc(misc_done, 1)
                for e in range(ET):
                    dve.wait_ge(pre_tanh, 2 * p + e + 1)
                    v_.scalar_tensor_tensor(uu[:, e, :], dtu[:, e, :], 1.0, xc[:, e, :], ALU.add, ALU.mult).then_inc(pre_u, 1)
                dve.wait_ge(pre_dtl, p + 1)
                for a in (32, 96):
                    last = v_.scalar_tensor_tensor(bc[a:a + 32, :], misc[a:a + 32, :], 0.5, bc[a:a + 32, :].bitcast(F32),
                                                   ALU.mult, ALU.subtract)
                last.then_inc(misc_done, 1)
                for e in range(ET):
                    misc_ready(("dt", p, e))
                    v_.tensor_scalar(xc[:, e, :], misc[:, :], dt_b[:, e:e + 1], None, ALU.add).then_inc(misc_done, 1)
                dve.wait_ge(misc_done, use[("dt", p, 1)] + 1)
                v_.scalar_tensor_tensor(dtt[:, :, :], xc[:, :, :], -1.0, xc[:, :, :], ALU.mult, ALU.min).then_inc(pre_na, 1)
                for e in range(ET):
                    v_.tensor_scalar(ys[:, e, p * PAIR:(p + 1) * PAIR], uu[:, e, :], d_skip[:, e:e + 1], 0.5, ALU.mult, ALU.mult)
                dve.wait_ge(pre_e, p + 1)
                link(v_.tensor_scalar(dtu[:, :, :], dtt[:, :, :], 2.0, None, ALU.add))
                link(v_.reciprocal(dtu[:, :, :], dtu[:, :, :]))
                link(v_.tensor_tensor(dtt[:, :, :], dtt[:, :, :], dtu[:, :, :], ALU.mult))
                if p:
                    dve.wait_ge(y_added, 2 * NS)
                z = ring[:, 0:2, :]
                link(v_.tensor_tensor(z, dtt[:, :, :], dtt[:, :, :], ALU.mult))
                link(v_.tensor_scalar(dtu[:, :, :], z, LOG1P[4], None, ALU.mult))
                for c in (3, 2, 1):
                    link(v_.scalar_tensor_tensor(dtu[:, :, :], dtu[:, :, :], LOG1P[c], z, ALU.add, ALU.mult))
                link(v_.scalar_tensor_tensor(dtu[:, :, :], dtu[:, :, :], LOG1P[0], dtt[:, :, :], ALU.add, ALU.mult))
                link(v_.tensor_scalar(xc[:, :, :], xc[:, :, :], 0.0, None, ALU.max))
                link(v_.scalar_tensor_tensor(dtt[:, :, :], dtu[:, :, :], 2.0, xc[:, :, :], ALU.mult, ALU.add))
                link(v_.scalar_tensor_tensor(dtu[:, :, :], dtt[:, :, :], 0.5, uu[:, :, :], ALU.mult, ALU.mult))
                v_.memset(da.rearrange("p e (b l) -> p (e b) l", b=2)[:, :, 0:1], 0.0).then_inc(dtu_ready, 1)

            def scan_c(v):
                for e in range(ET):
                    i = 2 * v + e
                    s = ring[:, i % 3, :]
                    dve.wait_ge(da_ready, i + 1)
                    dve.wait_ge(dbu_ready, i + 1)
                    v_.tensor_tensor_scan(s, da[:, e, :], s, 0.0, ALU.mult, ALU.add).then_inc(scanned, 1)
                misc_ready(("C", v))
                for e in range(ET):
                    i = 2 * v + e
                    s = ring[:, i % 3, :]
                    dve.wait_ge(scanned, i + 1)
                    v_.tensor_tensor(s, s, misc[:, :], ALU.mult).then_inc(hc_ready if e == 0 else misc_done, 1)

            def q_part(u):
                b, g = divmod(u, G)
                if g == 0:
                    if u == 0:
                        dve.wait_ge(mask_in, 16)
                    v_.tensor_scalar(mask_bias[:, b % 2, :], mask_sb[:, b * T:(b + 1) * T], 1.0, MASKED,
                                     ALU.subtract, ALU.mult).then_inc(mbias_ready, 1)
                dve.wait_ge(q_hi, u + 1)
                v_.tensor_tensor(qt[1][:, u % 2, :], bank[1][:, :], qt[0][:, u % 2, :].bitcast(F32), ALU.subtract).then_inc(q_lo, 1)

            def s_part(u):
                b, g = divmod(u, G)
                if g == 0:
                    dve.wait_ge(mbias_ready, b + 1)
                for h in range(2):
                    dve.wait_ge(s_filled, 2 * u + h + 1)
                    if u >= 2 and h == 0:
                        dve.wait_ge(t_filled, 2 * (u - 1))
                    if u == 0 and h == 0:
                        dve.wait_ge(ctx_lo, 1)
                    for t in range(TT):
                        i = 2 * h + t
                        last = v_.tensor_tensor_reduce(
                            out=prob[:, u % 2 * 2 + h, t * T:(t + 1) * T], in0=bank[2 + h][:, t * T:(t + 1) * T],
                            in1=mask_bias[:, b % 2, :], scale=1.0, scalar=-3.0e38, op0=ALU.add, op1=ALU.max,
                            accum_out=s_max[:, u % 2, i:i + 1])
                    last.then_inc(s_masked, 1)
                    dve.wait_ge(s_masked, 2 * u + h + 1)
                    v_.tensor_scalar(s_bias[:, u % 2, 2 * h:2 * h + 2], s_max[:, u % 2, 2 * h:2 * h + 2],
                                     -(float(P) ** -0.5), None, ALU.mult).then_inc(s_biased, 1)

            def t_part(u):
                for h in range(2):
                    dve.wait_ge(t_hi, 2 * u + h + 1)
                    v_.tensor_tensor(pt[1][:, :, h, :], bank[4 + h][:, :].rearrange("p (s t) -> p s t", s=TT),
                                     pt[0][:, :, h, :].bitcast(F32), ALU.subtract).then_inc(t_lo, 1)

            def n_part(u):
                b = u // G
                dve.wait_ge(p_exp, 2 * u + 2)
                link(v_.reciprocal(s_inv[:, u % 2, :], s_sum[:, u % 2, :]))
                v_.tensor_scalar(s_inv[:, u % 2, :], s_inv[:, u % 2, :], mask_any[:, b:b + 1], None, ALU.mult).then_inc(p_inv, 1)

            def v_part(u):
                dve.wait_ge(o_hi, u + 1)
                v_.tensor_tensor(ot[1][:, u % 2, :], bank[6][:, :], ot[0][:, u % 2, :].bitcast(F32), ALU.subtract).then_inc(o_lo, 1)

            def res(b):
                dve.wait_ge(o_summed, G * (b + 1))
                rows = xs[:, b * TT:(b + 1) * TT, :]
                v_.tensor_tensor(rows, rows, bank[0][:, :].rearrange("p (t d) -> p t d", t=TT), ALU.add).then_inc(res_done, 1)
                dve.wait_ge(res_done, b + 1)

            def route(p):
                misc_ready(("lg", p))
                v_.tensor_copy(lg[:, :, :], misc[:, 0:40].rearrange("p (t n) -> p t n", t=4)).then_inc(misc_done, 1)
                dve.wait_ge(misc_done, use[("lg", p)] + 1)
                L = lg[:, :, 0:E]
                a = L.unsqueeze(2).to_broadcast([P, 4, E, E])
                c = L.unsqueeze(3).to_broadcast([P, 4, E, E])
                v_.tensor_tensor(gt[:, :, :, :], a, c, ALU.is_gt)
                link(v_.tensor_tensor(eq[:, :, :, :], a, c, ALU.is_equal))
                low = small_("lower").unsqueeze(1).to_broadcast([P, 4, E * E])
                eqf = eq[:, :, :, :].rearrange("p t e j -> p t (e j)")
                link(v_.tensor_tensor(eqf, eqf, low, ALU.mult))
                link(v_.tensor_tensor(gt[:, :, :, :], gt[:, :, :, :], eq[:, :, :, :], ALU.add))
                link(v_.reduce_sum(rk[:, :, :], gt[:, :, :, :], AX.X))
                link(v_.tensor_scalar(rk[:, :, :], rk[:, :, :], 1.5, None, ALU.is_lt))
                link(v_.reduce_max(r1[:, :, :].rearrange("p t n -> p (t n)"), L, AX.X))
                link(v_.tensor_tensor(L, L, r1[:, :, :].to_broadcast([P, 4, E]), ALU.subtract))
                v_.tensor_scalar(lg[:, :, E:E + 1], lg[:, :, E:E + 1], -1.0, None, ALU.mult).then_inc(lg_ready, 1)
                dve.wait_ge(lg_exp, p + 1)
                W = ex[:, :, 0:E]
                link(v_.tensor_tensor(W, W, rk[:, :, :], ALU.mult))
                link(v_.reduce_sum(r1[:, :, :].rearrange("p t n -> p (t n)"), W, AX.X))
                link(v_.reciprocal(r1[:, :, :], r1[:, :, :]))
                link(v_.tensor_tensor(W, W, r1[:, :, :].to_broadcast([P, 4, E]), ALU.mult))
                S = ex[:, :, E:E + 1]
                link(v_.tensor_scalar(S, S, 1.0, None, ALU.add))
                link(v_.reciprocal(S, S))
                v_.tensor_scalar(cm[:, :, 0:E + 1], ex[:, :, 0:E + 1], 0.5, None, ALU.mult)
                v_.tensor_scalar(cm[:, :, 32:32 + E + 1], ex[:, :, 0:E + 1], 0.5, None, ALU.mult).then_inc(cm_ready, 1)
                dve.wait_ge(ct_hi, p + 1)
                v_.tensor_tensor(combt[p][32:64, :], misc[32:64, :], combt[p][32:64, :].bitcast(F32), ALU.subtract).then_inc(misc_done, 1)

            def g_part(m):
                k, j = phase(m)
                t = prob[:, m % 4, :]
                dve.wait_ge(h_tanh, m + 1)
                v_.scalar_tensor_tensor(t, t, 1.0, bank[2][:, :], ALU.add, ALU.mult).then_inc(h_g, 1)
                dve.wait_ge(u_filled, m + 1)
                dve.wait_ge(h_g, m + 1)
                v_.tensor_tensor(t, t, bank[3][:, :], ALU.mult).then_inc(h_u, 1)
                dve.wait_ge(h_u, m + 1)
                if m < F0:
                    dve.wait_ge(c_filled, m + 1)
                    v_.tensor_tensor(t, t, bank[4][:, :], ALU.mult).then_inc(h_c, 1)
                else:
                    v_.tensor_scalar(t, t, ucoef[:, j:j + 1], None, ALU.mult).then_inc(h_c, 1)

            def w1_part(j):
                slot, times = ffn_slot[("W1", j)]
                dve.wait_ge(ffn_in[slot], 16 * times)
                w = stage_ffn[:, slot, :]
                link(v_.tensor_scalar(q1c[:, :].bitcast(I32), w.bitcast(I32), 0x7F800000, None, ALU.bitwise_and))
                v_.tensor_scalar(q1c[:, :], q1c[:, :], 2.0 ** -6, 1.5 * 2.0 ** 20, ALU.max, ALU.mult).then_inc(q1_scale, 1)
                dve.wait_ge(q1_round, j + 1)
                link(v_.scalar_tensor_tensor(q1c[:, :], w, -1.0, w, ALU.mult, ALU.max))
                link(v_.tensor_scalar(q1c[:, :], q1c[:, :], -448.0, 0.0, ALU.add, ALU.max))
                link(v_.tensor_scalar(q1c[:, :], q1c[:, :], 3.0e38, None, ALU.mult))
                if j == 0:
                    dve.wait_ge(q_filled, UNITS)
                    dve.wait_ge(o_summed, UNITS)
                v_.scalar_tensor_tensor(w1slot[j], q1c[:, :], 0.0, w, ALU.mult, ALU.add).then_inc(w1_ready, 1)
                dve.wait_ge(w1_ready, j + 1)

            def acc(k):
                p = k % 2
                dve.wait_ge(d_done, last_item(k) + 1)
                for n, bk in enumerate(acc_banks(k)):
                    rows = xs[:, p * 4 + 2 * n:p * 4 + 2 * n + 2, :]
                    sums = bk[:, :].rearrange("p (t d) -> p t d", t=2)
                    if k < 2:
                        last = v_.tensor_tensor(rows, rows, sums, ALU.add)
                    else:
                        if k == 2 and n == 0:
                            dve.wait_ge(dsc_in, 16)
                        for t in range(2):
                            last = v_.tensor_tensor(xn[:, t, :], sums[:, t, :], dscale[:, :], ALU.mult)
                        link(last)
                        v_.tensor_tensor(rows, rows, xn[:, :, :], ALU.add).then_inc(out_ready, 1)
                        dve.wait_ge(out_ready, 2 * p + n + 1)
                if k < 2:
                    last.then_inc(acc_done, 1)
                    dve.wait_ge(acc_done, k + 1)

            def gatey(b):
                normalise(b, last_xn_use[0]).then_inc(yg_norm, 1)
                dve.wait_ge(yg_norm, b + 1)
                dve.wait_ge(yg_tanh, b + 1)
                link(v_.scalar_tensor_tensor(ysb[:, :, :], ysb[:, :, :], 1.0, xn[:, :, :], ALU.add, ALU.mult))
                dve.wait_ge(y_added, 2 * NS * (b // 2 + 1))
                for e in range(ET):
                    last = v_.tensor_tensor(ysb[:, e, :], ysb[:, e, :], ys[:, e, b * T:(b + 1) * T], ALU.mult)
                last.then_inc(yg_ready, 1)
                misc_ready(("yt", b))
                rows = xs[:, b * TT:(b + 1) * TT, :]
                v_.scalar_tensor_tensor(rows, misc[:, :].rearrange("p (t d) -> p t d", t=TT), 0.5, rows, ALU.mult, ALU.add).then_inc(misc_done, 1)
                dve.wait_ge(misc_done, use[("yt", b)] + 1)

            do = {"ctx": ctx, "fold": fold, "ln": ln, "prep": prep, "scanC": scan_c, "Q": q_part, "S": s_part, "T": t_part,
                  "N": n_part, "V": v_part, "res": res, "route": route, "G": g_part, "W1": w1_part, "acc": acc, "gatey": gatey}
            for kind, a in STEPS:
                if kind in do:
                    do[kind](a)

        @block.gpsimd
        def _(pool):
            gp = nc.gpsimd

            def n_part(u):
                s = prob[:, u % 2 * 2:u % 2 * 2 + 2, :].rearrange("p h (t s) -> p (h t) s", t=TT)
                pool.wait_ge(p_inv, u + 1)
                gp.tensor_tensor(s, s, s_inv[:, u % 2, :].unsqueeze(2).to_broadcast([P, 4, T]), ALU.mult).then_inc(p_norm, 1)

            def scan_b(v):
                pool.wait_ge(misc_done, use[("B", v)] + 1)
                if v % NS == 0:
                    pool.wait_ge(dtu_ready, v // NS + 1)
                for e in range(ET):
                    i = 2 * v + e
                    if i >= 3:
                        pool.wait_ge(y_added, i - 2)
                    gp.tensor_tensor(ring[:, i % 3, :], dtu[:, e, :], bb[:, v % 2, :], ALU.mult).then_inc(dbu_ready, 1)

            def scan_c(v):
                p = v // NS
                for e in range(ET):
                    i = 2 * v + e
                    y = ys[:, e, p * PAIR:(p + 1) * PAIR]
                    if e == 0:
                        pool.wait_ge(hc_ready, v + 1)
                    else:
                        pool.wait_ge(misc_done, use[("C", v)] + 1)
                    if i >= 2:
                        pool.wait_ge(y_added, i - 1)
                    gp.tensor_tensor(y, y, ring[:, i % 3, :], ALU.add).then_inc(y_added, 1)

            def esel_load():
                pool.wait_ge(o_summed, UNITS)
                gp.dma_start(esel, expert_sel).then_inc(esel_in, 16)

            normed = [0]
            gp.memset(neg_half[:, :], -0.5).then_inc(g_const, 1)
            pool.wait_ge(g_const, 1)

            def rstd_part(_):
                normed[0] += 1
                pool.wait_ge(mv_ready, normed[0])
                gp.tensor_tensor(rstd[:, :], rstd[:, :], neg_half[:, :], ALU.pow).then_inc(rstd_ready, 1)

            def w_part(m):
                slot, times = ffn_slot[("W", m)]
                pool.wait_ge(w_hi, m + 1)
                if m == 0:
                    pool.wait_ge(q_filled, UNITS)
                if m >= 3:
                    pool.wait_ge(d_done, m - 2)
                gp.tensor_tensor(wslot[1][m % 3], stage_ffn[:, slot, :], wslot[0][m % 3].bitcast(F32), ALU.subtract).then_inc(w_lo, 1)

            def w1_part(j):
                slot, _ = ffn_slot[("W1", j)]
                w = stage_ffn[:, slot, :]
                pool.wait_ge(q1_scale, j + 1)
                gp.tensor_tensor(w, w, q1c[:, :], ALU.add).then_inc(q1_added, 1)
                pool.wait_ge(q1_added, j + 1)
                gp.tensor_tensor(w, w, q1c[:, :], ALU.subtract).then_inc(q1_round, 1)

            def g_part(m):
                pool.wait_ge(h_hi, m + 1)
                gp.tensor_tensor(hid[1][m % 2], prob[:, m % 4, :], hid[0][m % 2].bitcast(F32), ALU.subtract).then_inc(h_lo, 1)

            do = {"ln": rstd_part, "gatey": rstd_part, "N": n_part, "scanB": scan_b, "scanC": scan_c, "W": w_part, "W1": w1_part, "G": g_part}
            loaded = False
            for kind, a in STEPS:
                if kind == "route" and not loaded:
                    esel_load()
                    loaded = True
                if kind in do:
                    do[kind](a)


def kernel(x, ctx_1024, mask_BxS2_bf1, L0_xattn_Wq, L0_xattn_Wk, L0_xattn_Wv, L0_xattn_Wo, L0_ffn_gate_w, L0_ffn_w_gate,
           L0_ffn_w_up, L0_ffn_w_down, L0_ffn_shgate_w, L0_ffn_shw_gate, L0_ffn_shw_up, L0_ffn_shw_down,
           L1_xattn_in_proj_w, L1_xattn_conv_w, L1_xattn_conv_b, L1_xattn_x_proj_w, L1_xattn_dt_proj_w,
           L1_xattn_dt_proj_b, L1_xattn_A_log, L1_xattn_D, L1_ffn_gate_w, L1_ffn_up_w, L1_ffn_down_w,
           L1_ffn_gate_scale, L1_ffn_up_scale, L1_ffn_down_scale):
    import concourse.bacc as bacc
    import numpy as np
    from concourse.bass_utils import run_bass_kernel_spmd

    f32 = np.float32

    def blocks(w):
        n = w.shape[0] // P
        return w.reshape(n, P, -1).transpose(1, 0, 2).reshape(P, -1)

    ctx = np.ascontiguousarray(ctx_1024).reshape(B * T, C)
    wq = np.asarray(L0_xattn_Wq).reshape(D, G, 2, P)
    wk = np.asarray(L0_xattn_Wk).reshape(C, G, P)
    wv = np.asarray(L0_xattn_Wv).reshape(C, G, P)
    wo = np.asarray(L0_xattn_Wo).reshape(G, 2, P, D)
    fold_w = np.concatenate([
        wq.transpose(1, 3, 2, 0).reshape(G, P, 2 * D), wo.transpose(0, 2, 1, 3).reshape(G, P, 2 * D),
        wk.transpose(1, 2, 0), wv.transpose(1, 2, 0)], axis=2)

    pad = J0 * P - E * HE - HS
    wide = lambda w, s: np.concatenate([np.asarray(w).transpose(1, 0, 2).reshape(D, E * HE), np.asarray(s), np.zeros((D, pad), f32)], axis=1)
    down0 = np.concatenate([np.asarray(L0_ffn_w_down).reshape(E * HE, D), np.asarray(L0_ffn_shw_down), np.zeros((pad, D), f32)])

    def tiles(gate, up, down):
        n = down.shape[0] // P
        cut = lambda w: w.reshape(DB, P, n, P).transpose(2, 1, 0, 3).reshape(n, P, DB * P)
        return np.concatenate([cut(gate), cut(up), down.reshape(n, P, D)], axis=2)

    ffn_w = np.concatenate([
        tiles(wide(L0_ffn_w_gate, L0_ffn_shw_gate), wide(L0_ffn_w_up, L0_ffn_shw_up), down0),
        tiles(np.asarray(L1_ffn_gate_w), np.asarray(L1_ffn_up_w), np.asarray(L1_ffn_down_w))])

    xp = np.asarray(L1_xattn_x_proj_w)
    xp_t = np.zeros((ET * P, P), f32)
    for at in (0, 32):
        xp_t[:, at:at + RANK + NS] = xp[:RANK + NS].T
    for at in (64, 96):
        xp_t[:, at + RANK:at + RANK + NS] = xp[RANK + NS:].T
    dt_w = np.zeros((P, ET * P), f32)
    dt_w[:RANK] = np.asarray(L1_xattn_dt_proj_w).T
    route = np.zeros((D, 10), f32)
    route[:, :E] = np.asarray(L0_ffn_gate_w).T
    route[:, E] = np.asarray(L0_ffn_shgate_w)
    lower = np.broadcast_to((np.arange(E)[None, :] < np.arange(E)[:, None]).astype(f32).reshape(1, E * E), (P, E * E))
    sel = np.zeros((P, NS), f32)
    for at in (0, 32, 64, 96):
        sel[at + RANK + np.arange(NS), np.arange(NS)] = 1
    expert_sel = np.zeros((64, J0 * P), f32)
    for e in range(E + 1):
        expert_sel[[e, 32 + e], e * HE:(e * HE + (HE if e < E else HS))] = 1
    parts = {
        "ident": np.eye(P, dtype=f32), "in_w": np.asarray(L1_xattn_in_proj_w).T, "xp_w": blocks(xp_t), "dt_w": dt_w,
        "a_log": blocks(np.asarray(L1_xattn_A_log)), "conv_w": blocks(np.asarray(L1_xattn_conv_w).reshape(ET * P, TAPS)),
        "conv_b": blocks(np.asarray(L1_xattn_conv_b)[:, None]), "dt_b": blocks(np.asarray(L1_xattn_dt_proj_b)[:, None]),
        "d_skip": blocks(np.asarray(L1_xattn_D)[:, None]), "g_scale": blocks(np.asarray(L1_ffn_gate_scale)[:, None]),
        "u_scale": blocks(np.asarray(L1_ffn_up_scale)[:, None]), "route_w": blocks(route), "lower": lower, "sel": sel,
    }
    small = np.concatenate([parts[n] for n, _ in SMALL], axis=1)

    arrays = {
        "x": np.asarray(x).reshape(B * T, D), "ctx_n": ctx, "ctx_t": ctx.T, "fold_w": fold_w, "ffn_w": ffn_w, "small": small,
        "expert_sel": expert_sel, "mask": np.asarray(mask_BxS2_bf1).reshape(B * T).view(np.uint8),
        "down_scale": np.asarray(L1_ffn_down_scale),
    }
    nc = bacc.Bacc("TRN2", target_bir_lowering=False, num_devices=1)
    args, given = [], {}
    for name, a in arrays.items():
        given[f"in_{name}"] = a = np.ascontiguousarray(a)
        args.append(nc.dram_tensor(f"in_{name}", a.shape, mybir.dt.from_np(a.dtype), kind="ExternalInput").ap())
    out = nc.dram_tensor("out", (B * T, D), F32, kind="ExternalOutput").ap()
    build_program(nc, *args, out)
    r = run_bass_kernel_spmd(nc, [given], core_ids=[0])
    return r.results[0]["out"].reshape(B, T, D)
```

```python
from contextlib import ExitStack

import concourse.bass as bass
from concourse import mybir

F32 = mybir.dt.float32
F32R = mybir.dt.float32r
U8 = mybir.dt.uint8
I32 = mybir.dt.int32
ALU = mybir.AluOpType
ACT = mybir.ActivationFunctionType
AX = mybir.AxisListType

P = 128
B, T, D = 4, 256, 256
C = 128
H, G = 16, 8
TT = T // P
DB = D // P
E, HE, HS = 8, 176, 352
J0 = -(-(E * HE + HS) // P)
HID1 = 768
J1 = HID1 // P
NS, RANK, TAPS = 16, 8, 4
ET = 2
PAIR = 2 * T
UNITS = B * G
FOLD_COLS = 2 * 2 * D + 2 * C
FFN_COLS = 2 * DB * P + D
START = (0, 0, 0, 0, 0, 1, 1, 1)
SOFT = 4
WSLOTS = 5
W_AT = ((0, 30), (1, 31), (2, 32), (3, 33), (4, 34))
PREP_BEFORE = 8
LAST_SCAN = UNITS - 1
EPS = 1e-5
MASKED = 1e30
LOG1P = [0.9999999705406568, -0.49999501516786626, 0.3331927134249427, -0.2484436989243044, 0.19111431080478863,
         -0.13674769705383674, 0.07836166801762622, -0.02958850739253811, 0.005253457797007794]

SMALL = [
    ("ident", P), ("in_w", ET * P), ("xp_w", ET * P), ("dt_w", ET * P), ("a_log", ET * NS),
    ("conv_w", ET * TAPS), ("conv_b", ET), ("dt_b", ET), ("d_skip", ET), ("g_scale", J1),
    ("u_scale", J1), ("route_w", DB * 10), ("lower", E * E), ("sel", NS),
]
SMALL_AT = {}
SMALL_COLS = 0
for _name, _n in SMALL:
    SMALL_AT[_name] = (SMALL_COLS, SMALL_COLS + _n)
    SMALL_COLS += _n


def ffn_items():
    order = START + (1, 0) * (J0 - 3 - START.count(0)) + (0, 0, 0)
    order += (1,) * (J0 - order.count(1))
    items = [(k, order[:m].count(k)) for m, k in enumerate(order)]
    return items + [(k, j) for k in (2, 3) for j in range(J1)]


ITEMS = ffn_items()
LAST = [max(m for m, (k, _) in enumerate(ITEMS) if k == phase) for phase in range(4)]


GATE_AT = ((24, ("rows", 0)), (27, ("gate", 0)), (28, ("gexp", 0)), (28, ("gate2", 0)), (30, ("esel", 0)), (UNITS, ("comb", 0)))
SCAN_ITEMS = (6, 8, 10, 12, 14, 16, 17, 18, 19, 20, 21, 22, 23)
ROUND_ITEMS = (7, 8, 9, 11, 12, 13, 15, 16, 17, 19, 20, 21)


def tail_steps(a, b, gaps):
    return [
        ([], [("stat", (2, a)), ("stat", (2, b))]),
        ([], [("ynorm", a)]),
        ([("ytanh", a)], [("ymul", a), ("ynorm", b)]),
        ([("ytanh", b)], [("yt", a), ("ymul", b), ("stat", (3, a))]),
        ([], [("norm", (3, a)), ("yt", b), ("stat", (3, b))] + ([] if gaps else [("ln", (3, a)), ("norm", (3, b)), ("ln", (3, b))])),
        ([], [("ln", (3, a)), ("norm", (3, b)), ("ln", (3, b))] if gaps else []),
    ]


def timeline():
    norm = lambda kind, b: [("stat", (kind, b)), ("norm", (kind, b)), ("ln", (kind, b))]
    prep_steps = lambda p: [
        [("conv", (p, 0))], [("silu", (p, 0))], [("conv", (p, 1))], [("silu", (p, 1))], [("xp", p)],
        [("dt", (p, 0))], [("dt", (p, 1)), ("abs", p)], []] + [[("soft", (p, n // 2))] if n % 2 == 0 else [] for n in range(2 * SOFT - 1)]
    first = prep_steps(0)
    steps = [("stat", (0, 0)), ("ctx", 0), ("norm", (0, 0)), ("fold", 0), ("setup", 0), ("ln", (0, 0)), ("fold", 1)]
    for g in range(2, max(G, 2 + PREP_BEFORE)):
        steps += first.pop(0) if g < 2 + PREP_BEFORE else []
        steps += [("fold", g)] if g < G else []
        steps += {5: [("stat", (0, 1))], 6: [("norm", (0, 1))], 7: [("ln", (0, 1))]}.get(g, [])
    steps += [("Q", 0), ("R", 0)]

    beside = {}
    for b in (2, 3):
        for n, step in enumerate(norm(0, b)):
            beside.setdefault((b - 1) * G - 5 + n, []).append(step)
    for b in (0, 1, 2):
        for n, step in enumerate(norm(1, b)):
            beside.setdefault((b + 1) * G + 5 + n, []).append(step)
    for i, step in GATE_AT + tuple((i, ("W", j)) for j, i in W_AT):
        beside.setdefault(i, []).append(step)

    v, prep = 0, first + [[("scanB", 0)]]
    for i in range(UNITS + 4):
        steps += [("Q", i + 1)] if i + 1 < UNITS else []
        steps += [("S", i)] if i < UNITS else []
        steps += [("R", i + 1)] if i + 1 < UNITS else []
        steps += [("E", i)] if i < UNITS else []
        now = not prep and i <= LAST_SCAN
        steps += [("scanC", v)] if now else prep.pop(0) if prep else []
        steps += [("T", i - 2)] if 2 <= i <= UNITS + 1 else []
        steps += [("V", i - 3)] if 3 <= i <= UNITS + 2 else []
        steps += [("I", i)] if i < UNITS else []
        if i >= 4:
            steps.append(("O", i - 4))
            if (i - 4) % G == G - 1:
                steps.append(("res", (i - 4) // G))
        if now:
            v += 1
            if v == NS:
                prep = prep_steps(1) + [[("scanB", v)]]
            else:
                steps.append(("scanB", v))
        elif prep:
            steps += prep.pop(0)
        steps += [("N", i)] if i < UNITS else []
        steps += [("sum", v - 1)] if now else []
        steps += beside.pop(i, [])
        m = i - UNITS
        steps += [("c", m - 1)] if m >= 1 else []
        steps += [("G", m)] if 0 <= m <= 2 else []
        steps += [("H", m - 1)] if m >= 1 else []
    steps += [("stat", (1, 3)), ("norm", (1, 3))]
    assert not beside and not prep, (beside, prep)

    after = {3: [("ln", (1, 3)), ("rows", 1)], 4: [("gate", 1), ("gexp", 1), ("gate2", 1)]}
    inside = {5: [("comb", 1)]}
    for p in range(2):
        for n, (i, a) in enumerate(tail_steps(2 * p, 2 * p + 1, p)):
            inside[LAST[p] + 1 + n] = i
            after[LAST[p] + 1 + n] = a
    down, rounds, pending, sums = 0, 0, [], []
    for m in range(3, len(ITEMS)):
        flush = m - 1 in LAST[:2]
        steps += [("H", m - 1)] if flush and m > 3 else []
        steps += [("G", m)] + pending + inside.get(m, [])
        steps += [("H", m - 1)] if not flush and m > 3 else []
        steps += [("c", m)] + sums
        pending, sums = [], []
        if m in SCAN_ITEMS and v < 2 * NS:
            steps.append(("scanC", v))
            v += 1
            pending = [("scanB", v)] if v < 2 * NS else [("sum", v - 1)]
            sums = [("sum", v - 1)] if v < 2 * NS else []
        while down <= m - 2 or down < m and flush:
            steps.append(("D", down))
            if ITEMS[down][0] == 1 and ITEMS[down][1] + WSLOTS < J0:
                steps.append(("W", ITEMS[down][1] + WSLOTS))
            if down in LAST:
                steps += [("acc", (LAST.index(down), n)) for n in range(2)]
            down += 1
        steps += after.get(m, [])
        if m in ROUND_ITEMS:
            steps.append(("W1" if rounds % 2 == 0 else "W1b", rounds // 2))
            rounds += 1
    assert v == 2 * NS and rounds == 2 * J1, (v, rounds)
    m = len(ITEMS) - 1
    steps += [("H", m), ("D", m - 1), ("D", m), ("acc", (3, 0)), ("acc", (3, 1))]
    return steps


STEPS = timeline()


def build_program(nc, x, ctx_n, ctx_t, fold_w, ffn_w, small, expert_sel, mask, down_scale, out):
    stack = ExitStack()
    with stack:
        def sb(name, shape, dt=F32):
            return stack.enter_context(nc.sbuf_tensor(name, shape, dt))

        def sem(name):
            return stack.enter_context(nc.semaphore(name))

        xs = sb("xs", [P, B * TT, D])
        cn = [sb(f"cn_{s}", [P, B * TT, C], F32R) for s in ("hi", "lo")]
        ct = [sb(f"ct_{s}", [P, B * T], F32R) for s in ("hi", "lo")]
        stage = sb("stage", [P, 2560])
        stage_fold = stage[:, :].rearrange("p (s n) -> p s n", s=2)
        stage_ffn = stage[:, 0:3 * FFN_COLS].rearrange("p (s n) -> p s n", s=3)
        mw = [sb(f"mw_{s}", [P, G * 512], F32R) for s in ("hi", "lo")]
        nw = [sb(f"nw_{s}", [P, G * 512], F32R) for s in ("hi", "lo")]
        xnt = [sb(f"xnt_{s}", [P, DB, B * T], F32R) for s in ("hi", "lo")]
        qt = [sb(f"qt_{s}", [P, 2, 512], F32R) for s in ("hi", "lo")]
        prob = sb("prob", [P, 4, 512])
        probs = [prob[:, 0:2, :], prob[:, 2:4, :], stage[:, 1536:2560].rearrange("p (h n) -> p h n", h=2)]
        pt = [sb(f"pt_{s}", [P, TT, 2, T], F32R) for s in ("hi", "lo")]
        ot = [sb(f"ot_{s}", [P, 2, 512], F32R) for s in ("hi", "lo")]
        sm = sb("sm", [P, SMALL_COLS])
        mask_sb = sb("mask_sb", [P, B * T], U8)
        mask_bias = sb("mask_bias", [P, 2, T])
        mask_any = sb("mask_any", [P, B])
        dscale = sb("dscale", [P, D])
        s_min = sb("s_min", [P, 3, 4])
        dhalf = sb("dhalf", [P, ET])
        neg_ident = sb("neg_ident", [P, P], F32R)
        s_sum = sb("s_sum", [P, 3, 4])
        s_inv = sb("s_inv", [P, 3, 4])
        xn = sb("xn", [P, TT, D])
        bn = sb("bn", [P, 2, TT, 6])
        mv = sb("mv", [P, 2, TT, 2])
        rstd = sb("rstd", [P, 2, TT])
        neg_half = sb("neg_half", [P, TT])
        front = sb("front", [P, 4, 512])
        xc = front[:, 0:2, :]
        bb = front[:, 0:2, :]
        uu = front[:, 2:4, :]
        da = front[:, 2:4, :]
        dtt = sb("dtt", [P, ET, 512])
        dtu = sb("dtu", [P, ET, 512])
        ys = sb("ys", [P, ET, B * T])
        bc = sb("bc", [P, 512], F32R)
        sel = sb("sel", [P, NS, P], F32R)
        ring = sb("ring", [P, 4, 512])
        acoef = sb("acoef", [P, ET, NS])
        lg = sb("lg", [P, 4, 10])
        ex = sb("ex", [P, 4, 10])
        r1 = sb("r1", [P, 4, 1])
        cmp_ = sb("cmp_", [P, FFN_COLS])
        dtl = cmp_[0:RANK, 0:512]
        lg_rows = cmp_[0:10, 0:512]
        gt, eq = (cmp_[:, a:a + 4 * E * E].rearrange("p (t e j) -> p t e j", t=4, e=E) for a in (0, 4 * E * E))
        rk = sb("rk", [P, 4, E])
        cm = sb("cm", [P, 4, 64])
        rw = [sb(f"rw_{s}", [P, DB * 10], F32R) for s in ("hi", "lo")]
        ucoef = sb("ucoef", [P, J1])
        gcoef = sb("gcoef", [P, J1])
        ysb = mask_bias
        in_split = [sb(f"in_split_{s}", [P, ET * P], F32R)[:, :] for s in ("hi", "lo")]
        q1c = cmp_[:, :]

        bank = [stack.enter_context(nc.psum_tensor(f"bank{i}", [P, 512], F32)) for i in range(8)]
        misc = bank[7]

        def small_(name):
            a, b = SMALL_AT[name]
            return sm[:, a:b]

        ident = small_("ident")
        in_w, xp_w = small_("in_w"), small_("xp_w")
        dt_w = small_("dt_w")[0:RANK, :]
        conv_w, conv_b, dt_b, d_skip = (small_(n) for n in ("conv_w", "conv_b", "dt_b", "d_skip"))

        wslot = [[w[:, s * FFN_COLS:(s + 1) * FFN_COLS] for s in range(WSLOTS)] for w in mw]
        w1slot = [nw[1][:, 512 + n * FFN_COLS:512 + (n + 1) * FFN_COLS] for n in range(2)]
        w1slot += [t[:, :, :, :].rearrange("p s h t -> p (s h t)")[:, 0:FFN_COLS] for t in pt]
        w1slot += [t[:, :, :].rearrange("p h t -> p (h t)")[:, 0:FFN_COLS] for t in ot]
        esel = nw[0][0:64, 0:J0 * P]
        combt = [nw[0][0:64, J0 * P:J0 * P + 512], nw[1][0:64, 0:512]]
        HID_AT = J0 * P + 512
        hid = [[w[:, HID_AT + s * 512:HID_AT + (s + 1) * 512] for s in range(3)] for w in nw]

        def nw_free(cols):
            return UNITS - G + -(-cols // 512)

        x0_in, x_in, small_in, ctx_in, ctx_n_in, mask_in, esel_in, dsc_in = (sem(n) for n in ("x0_in", "x_in", "small_in", "ctx_in", "ctx_n_in", "mask_in", "esel_in", "dsc_in"))
        fold_in = [sem(f"fold_in{i}") for i in range(2)]
        ffn_in = [sem(f"ffn_in{i}") for i in range(3)]
        out_done = sem("out_done")
        a_chain, v_chain, g_const, q1_added = sem("a_chain"), sem("v_chain"), sem("g_const"), sem("q1_added")
        misc_filled, misc_done = sem("misc_filled"), sem("misc_done")
        ctx_hi, ctx_lo = sem("ctx_hi"), sem("ctx_lo")
        in_w_hi, in_w_split, ctx_n_hi, coef_ready = (sem(n) for n in ("in_w_hi", "in_w_split", "ctx_n_hi", "coef_ready"))
        m_filled, n_filled = sem("m_filled"), sem("n_filled")
        m_hi, m_lo, n_hi, n_lo = (sem(n) for n in ("m_hi", "m_lo", "n_hi", "n_lo"))
        mv_ready, rstd_ready = sem("mv_ready"), sem("rstd_ready")
        xn_ready, xt_hi = sem("xn_ready"), sem("xt_hi")
        q_filled, q_hi, q_lo = sem("q_filled"), sem("q_hi"), sem("q_lo")
        s_filled, s_masked, q_left = sem("s_filled"), sem("s_masked"), sem("q_left")
        p_exp, p_inv, p_norm = sem("p_exp"), sem("p_inv"), sem("p_norm")
        t_filled, t_hi, t_lo = sem("t_filled"), sem("t_hi"), sem("t_lo")
        v_filled, o_hi, o_lo, o_summed = (sem(n) for n in ("v_filled", "o_hi", "o_lo", "o_summed"))
        res_done = sem("res_done")
        mbias_ready = sem("mbias_ready")
        pre_tanh, pre_u, pre_bc_hi, pre_dtl, pre_na, pre_e, dt_ready, dtu_ready = (
            sem(n) for n in ("pre_tanh", "pre_u", "pre_bc_hi", "pre_dtl", "pre_na", "pre_e", "dt_ready", "dtu_ready"))
        a_exp, setup_done = sem("a_exp"), sem("setup_done")
        b_ready, da_ready, dbu_ready, scanned, hc_ready, y_added = (
            sem(n) for n in ("b_ready", "da_ready", "dbu_ready", "scanned", "hc_ready", "y_added"))
        yg_norm, yg_tanh, yg_ready = sem("yg_norm"), sem("yg_tanh"), sem("yg_ready")
        lg_ready, lg_exp, cm_ready, ct_hi = (sem(n) for n in ("lg_ready", "lg_exp", "cm_ready", "ct_hi"))
        w_hi, w_lo_first, w_lo = sem("w_hi"), sem("w_lo_first"), sem("w_lo")
        q1_scale, q1_round, w1_ready = sem("q1_scale"), sem("q1_round"), sem("w1_ready")
        g_filled, u_filled, c_filled = sem("g_filled"), sem("u_filled"), sem("c_filled")
        h_tanh, h_g, h_u, h_c, h_hi, h_lo = (sem(n) for n in ("h_tanh", "h_g", "h_u", "h_c", "h_hi", "h_lo"))
        d_done, acc_done, out_ready = sem("d_done"), sem("acc_done"), sem("out_ready")

        use = {}
        for kind, arg in STEPS:
            mine = {"ln": [("ln", arg)], "conv": [("in",) + arg] if kind == "conv" else [], "xp": [("xp", arg)], "dt": [("dt",) + arg] if kind == "dt" else [],
                    "scanB": [("B", arg)], "scanC": [("C", arg)], "yt": [("yt", arg)], "rows": [("rows", arg)], "gate": [("lg", arg)], "comb": [("cT", arg)]}.get(kind, [])
            for key in mine:
                use[key] = len(use)
        ln_no = {arg: n for n, arg in enumerate(a for k, a in STEPS if k == "ln")}
        stat_no = {arg: n for n, arg in enumerate(a for k, a in STEPS if k == "stat")}

        def w_split(j):
            return (w_lo_first, j + 1) if j < WSLOTS else (w_lo, j + 1 - WSLOTS)

        def gate_bank(m):
            return bank[4 if ITEMS[m][0] >= 2 and m % 2 else 2]

        def fold_banks(g):
            return bank[1 + g % 3], bank[4 + g % 3]

        def acc_banks(k):
            return (bank[0], bank[1]) if k % 2 == 0 else (bank[5], bank[6])

        ffn_loads = [x for x in STEPS if x[0] in ("W", "W1")]
        ffn_slot = {key: (n % 3, n // 3 + 1) for n, key in enumerate(ffn_loads)}

        first_fp8 = LAST[1] + 1
        block = stack.enter_context(nc.Block())

        @block.sync
        def _(sp):
            sp.dma_start(xs[:, 0:TT, :], x.rearrange("(n p) d -> p n d", p=P)[:, 0:TT, :]).then_inc(x0_in, 16)
            sp.dma_start(prob[:, 0:2, :].rearrange("p a n -> p (a n)"), ctx_t).then_inc(ctx_in, 16)
            for g in range(2):
                sp.dma_start(stage_fold[:, g, :], fold_w[g]).then_inc(fold_in[g], 16)
                if g == 0:
                    sp.dma_start(sm[:, :], small).then_inc(small_in, 16)
            sp.dma_start(prob[:, 2:4, :].rearrange("p a n -> p (a n)").rearrange("p (n c) -> p n c", c=C),
                         ctx_n.rearrange("(n p) c -> p n c", p=P)).then_inc(ctx_n_in, 16)
            sp.dma_start(xs[:, TT:, :], x.rearrange("(n p) d -> p n d", p=P)[:, TT:, :]).then_inc(x_in, 16)
            sp.dma_start(mask_sb[:, :], mask.unsqueeze(0).to_broadcast([P, B * T])).then_inc(mask_in, 16)
            sp.dma_start(dscale[:, :], down_scale.unsqueeze(0).to_broadcast([P, D])).then_inc(dsc_in, 16)
            for g in range(2, G):
                sp.wait_ge(n_filled, g - 1)
                sp.dma_start(stage_fold[:, g % 2, :], fold_w[g]).then_inc(fold_in[g % 2], 16)
            for n, (kind, a) in enumerate(ffn_loads):
                if n == 0:
                    sp.wait_ge(n_filled, G)
                if n == 2:
                    sp.wait_ge(t_filled, 2 * (UNITS - 2))
                if n >= 3:
                    before, j = ffn_loads[n - 3]
                    sp.wait_ge(*(w_split(j) if before == "W" else (w1_ready, j + 1)))
                row = a % J0 if kind == "W" else J0 + a
                sp.dma_start(stage_ffn[:, n % 3, :], ffn_w[row]).then_inc(ffn_in[n % 3], 16)
            for b in range(B):
                sp.wait_ge(out_ready, b + 1)
                sp.dma_start(out.rearrange("(n p) d -> p n d", p=P)[:, b * TT:(b + 1) * TT, :],
                             xs[:, b * TT:(b + 1) * TT, :]).then_inc(out_done, 16)
            sp.wait_ge(out_done, 16 * B)

        @block.tensor
        def _(pe):
            def three(bank_ap, a, b, start, stop, skip=False):
                terms = [(a[0], b[0])]
                if b[1] is not None:
                    terms.append((a[0], b[1]))
                if a[1] is not None:
                    terms.append((a[1], b[0]))
                for n, (l, r) in enumerate(terms):
                    last = nc.tensor.matmul(bank_ap, l, r, start=start and n == 0, stop=stop and n == len(terms) - 1,
                                            skip_group_check=skip)
                return last

            def take_misc(key):
                if use[key]:
                    pe.wait_ge(misc_done, use[key])

            def fold(g):
                pe.wait_ge(fold_in[g % 2], 16 * (g // 2 + 1))
                wq = stage_fold[:, g % 2, 0:512]
                wo = stage_fold[:, g % 2, 512:1024]
                wk = stage_fold[:, g % 2, 1024:1152]
                wv = stage_fold[:, g % 2, 1152:1280]
                m_bank, n_bank = fold_banks(g)
                if g >= 3:
                    pe.wait_ge(m_lo, g - 2)
                for h in range(2):
                    for d in range(DB):
                        last = nc.tensor.matmul(m_bank[:, (h * DB + d) * P:(h * DB + d + 1) * P],
                                                wq[:, h * D + d * P:h * D + (d + 1) * P], wk, start=True, stop=True)
                last.then_inc(m_filled, 1)
                if g >= 3:
                    pe.wait_ge(n_lo, g - 2)
                nc.tensor.matmul(n_bank[:, :], wv, wo, start=True, stop=True).then_inc(n_filled, 1)

            def ln(arg):
                kind, b = arg
                if ln_no[arg] == 0:
                    pe.wait_ge(small_in, 16)
                pe.wait_ge(xn_ready, ln_no[arg] + 1)
                take_misc(("ln", arg))
                for d in range(DB):
                    for t in range(TT):
                        last = nc.tensor.transpose(misc[:, d * T + t * P:d * T + (t + 1) * P],
                                                   xn[:, t, d * P:(d + 1) * P], ident)
                last.then_inc(misc_filled, 1)

            def conv(arg):
                p, e = arg
                pair = slice(p * PAIR, (p + 1) * PAIR)
                if p == 0 and e == 0:
                    pe.wait_ge(ctx_lo, 1)
                    pe.wait_ge(in_w_split, 1)
                take_misc(("in", p, e))
                w = [t[:, e * P:(e + 1) * P] for t in in_split]
                three(misc[:, :], w, (ct[0][:, pair], ct[1][:, pair]), True, True).then_inc(misc_filled, 1)

            def xp(p):
                take_misc(("xp", p))
                pe.wait_ge(pre_u, 2 * p + 2)
                for e in range(ET):
                    last = nc.tensor.matmul(misc[:, :], xp_w[:, e * P:(e + 1) * P], uu[:, e, :], start=e == 0, stop=e == ET - 1)
                last.then_inc(misc_filled, 1)

            def dt_part(arg):
                p, e = arg
                pe.wait_ge(pre_dtl, p + 1)
                take_misc(("dt", p, e))
                nc.tensor.matmul(misc[:, :], dt_w[:, e * P:(e + 1) * P], dtl, start=True, stop=True).then_inc(misc_filled, 1)

            def scan_b(v):
                take_misc(("B", v))
                if v == 0:
                    pe.wait_ge(setup_done, 1)
                nc.tensor.matmul(misc[:, :], sel[0:64, v % NS, :], bc[0:64, :], start=True, stop=True).then_inc(misc_filled, 1)

            def scan_c(v):
                take_misc(("C", v))
                nc.tensor.matmul(misc[:, :], sel[64:128, v % NS, :], bc[64:128, :], start=True, stop=True).then_inc(misc_filled, 1)

            def q_part(u):
                b, g = divmod(u, G)
                pe.wait_ge(misc_done, use[("ln", (0, b))] + 1)
                if u == 0:
                    pe.wait_ge(m_lo, G)
                else:
                    pe.wait_ge(q_lo, u)
                for h in range(2):
                    for d in range(DB):
                        at = g * 512 + (h * DB + d) * P
                        last = three(bank[1][:, h * T:(h + 1) * T], [w[:, at:at + P] for w in mw],
                                     [w[:, d, b * T:(b + 1) * T] for w in xnt], h == 0 and d == 0, d == DB - 1, skip=True)
                last.then_inc(q_filled, 1)

            def r_part(u):
                pe.wait_ge(q_hi, u + 1)
                if u == 0:
                    pe.wait_ge(setup_done, 1)
                nc.tensor.matmul(bank[1][:, :], neg_ident[:, :], qt[0][:, u % 2, :], start=False, stop=True,
                                 skip_group_check=True).then_inc(q_left, 1)

            def s_part(u):
                b, g = divmod(u, G)
                pe.wait_ge(q_lo, u + 1)
                for h in range(2):
                    if u:
                        pe.wait_ge(s_masked, 2 * u - 1 + h)
                    for t in range(TT):
                        last = three(bank[2 + h][:, t * T:(t + 1) * T],
                                     [w[:, u % 2, h * T + t * P:h * T + (t + 1) * P] for w in qt],
                                     [w[:, b * T:(b + 1) * T] for w in ct], True, True)
                    last.then_inc(s_filled, 1)

            def t_part(u):
                pe.wait_ge(p_norm, u + 1)
                for h in range(2):
                    if u:
                        pe.wait_ge(t_lo, 2 * u - 1 + h)
                    elif h == 0:
                        pe.wait_ge(n_lo, G)
                    for t in range(TT):
                        for s in range(TT):
                            last = nc.tensor.transpose(bank[4 + h][:, s * T + t * P:s * T + (t + 1) * P],
                                                       probs[u % 3][:, h, t * T + s * P:t * T + (s + 1) * P], ident)
                    last.then_inc(t_filled, 1)

            def v_part(u):
                b = u // G
                pe.wait_ge(t_lo, 2 * u + 2)
                if u == 0:
                    pe.wait_ge(setup_done, 1)
                if u:
                    pe.wait_ge(o_lo, u)
                for s in range(TT):
                    last = three(bank[6][:, :], [w[:, b * TT + s, :] for w in cn],
                                 [w[:, s, :, :].rearrange("p h t -> p (h t)") for w in pt], s == 0, s == TT - 1)
                last.then_inc(v_filled, 1)

            def o_part(u):
                b, g = divmod(u, G)
                pe.wait_ge(o_lo, u + 1)
                if g == 0 and b:
                    pe.wait_ge(res_done, b)
                for t in range(TT):
                    for h in range(2):
                        last = three(bank[0][:, t * D:(t + 1) * D],
                                     [w[:, u % 2, h * T + t * P:h * T + (t + 1) * P] for w in ot],
                                     [w[:, g * 512 + h * D:g * 512 + (h + 1) * D] for w in nw],
                                     g == 0 and t == 0 and h == 0, g == G - 1 and h == 1, skip=True)
                last.then_inc(o_summed, 1)

            def rows_part(p):
                take_misc(("rows", p))
                pe.wait_ge(misc_done, use[("ln", (1, 2 * p + 1))] + 1)
                if p == 0:
                    pe.wait_ge(setup_done, 1)
                for d in range(DB):
                    last = three(misc[0:10, :], [w[:, d * 10:(d + 1) * 10] for w in rw],
                                 [w[:, d, p * PAIR:(p + 1) * PAIR] for w in xnt], d == 0, d == DB - 1)
                last.then_inc(misc_filled, 1)

            def gate(p):
                take_misc(("lg", p))
                for t in range(4):
                    last = nc.tensor.transpose(misc[:, t * 10:(t + 1) * 10], lg_rows[:, t * P:(t + 1) * P], ident[0:10, 0:10])
                last.then_inc(misc_filled, 1)

            def comb(p):
                take_misc(("cT", p))
                pe.wait_ge(cm_ready, p + 1)
                for t in range(4):
                    last = nc.tensor.transpose(misc[0:64, t * P:(t + 1) * P], cm[:, t, :], ident)
                last.then_inc(misc_filled, 1)

            def g_part(m):
                k, j = ITEMS[m]
                p = k % 2
                if k < 2:
                    pe.wait_ge(*w_split(j))
                    ws = [w[j % WSLOTS] for w in wslot]
                    pe.wait_ge(misc_done, use[("ln", (1, 2 * p + 1))] + 1)
                else:
                    pe.wait_ge(w1_ready, j + 1)
                    ws = [w1slot[j], None]
                    pe.wait_ge(misc_done, use[("ln", (3, 2 * p + 1))] + 1)
                for n, (filled, read) in enumerate(((g_filled, h_g), (u_filled, h_u))):
                    bk = bank[3] if n else gate_bank(m)
                    if n == 0 and m == first_fp8 + 1:
                        pe.wait_ge(h_c, m - 1)
                    elif n == 0 and m > first_fp8 + 1:
                        pe.wait_ge(h_g, m - 1)
                    elif m:
                        pe.wait_ge(read, m)
                    else:
                        pe.wait_ge(s_masked, 2 * UNITS)
                    for d in range(DB):
                        at = n * DB * P + d * P
                        last = three(bk[:, :], [w if w is None else w[:, at:at + P] for w in ws],
                                     [w[:, d, p * PAIR:(p + 1) * PAIR] for w in xnt], d == 0, d == DB - 1)
                    last.then_inc(filled, 1)

            def c_part(m):
                k, j = ITEMS[m]
                p = k % 2
                if k < 2:
                    if m:
                        pe.wait_ge(h_c, m)
                    else:
                        pe.wait_ge(t_lo, 2 * UNITS)
                        pe.wait_ge(esel_in, 16)
                    pe.wait_ge(misc_done, use[("cT", p)] + 1)
                    nc.tensor.matmul(bank[4][:, :], esel[:, j * P:(j + 1) * P], combt[p], start=True, stop=True).then_inc(c_filled, 1)

            def d_part(m):
                k, j = ITEMS[m]
                pe.wait_ge(h_lo, m + 1)
                down = 2 * DB * P
                if k < 2:
                    ws = [w[j % WSLOTS][:, down:down + D] for w in wslot]
                else:
                    ws = [w1slot[j][:, down:down + D], None]
                if j == 0:
                    if k >= 2:
                        pe.wait_ge(acc_done, 2 * (k - 1))
                    elif k == 1:
                        pe.wait_ge(o_lo, UNITS)
                    else:
                        pe.wait_ge(res_done, B)
                        pe.wait_ge(q_lo, UNITS)
                banks = acc_banks(k)
                n_items = J0 if k < 2 else J1
                for t in range(4):
                    last = three(banks[t // 2][:, t % 2 * D:(t % 2 + 1) * D],
                                 [w[m % 3][:, t * P:(t + 1) * P] for w in hid], ws,
                                 j == 0 and t % 2 == 0, j == n_items - 1, skip=True)
                last.then_inc(d_done, 1)

            def yt(b):
                take_misc(("yt", b))
                pe.wait_ge(yg_ready, b + 1)
                for t in range(TT):
                    for e in range(ET):
                        last = nc.tensor.transpose(misc[:, t * D + e * P:t * D + (e + 1) * P], ysb[:, e, t * P:(t + 1) * P], ident)
                last.then_inc(misc_filled, 1)

            do = {"fold": fold, "ln": ln, "conv": conv, "xp": xp, "dt": dt_part, "scanB": scan_b, "scanC": scan_c, "Q": q_part, "S": s_part,
                  "R": r_part, "T": t_part, "V": v_part, "O": o_part, "rows": rows_part, "gate": gate, "comb": comb, "G": g_part, "c": c_part, "D": d_part, "yt": yt}
            for kind, a in STEPS:
                if kind in do:
                    do[kind](a)

        @block.scalar
        def _(act):
            def copy(dst, src, scale=1.0):
                return nc.scalar.activation(dst, src, ACT.Copy, scale=scale)

            def misc_ready(key):
                act.wait_ge(misc_filled, use[key] + 1)

            def ctx(_):
                act.wait_ge(ctx_in, 16)
                copy(ct[0][:, :], prob[:, 0:2, :].rearrange("p a n -> p (a n)")).then_inc(ctx_hi, 1)

            def setup(_):
                act.wait_ge(small_in, 16)
                copy(in_split[0], in_w).then_inc(in_w_hi, 1)
                copy(rw[0][:, :], small_("route_w"))
                nc.scalar.activation(acoef[:, :, :].rearrange("p e n -> p (e n)"), small_("a_log"), ACT.Exp).then_inc(a_exp, 1)
                act.wait_ge(ctx_n_in, 16)
                copy(cn[0][:, :, :].rearrange("p n c -> p (n c)"),
                     prob[:, 2:4, :].rearrange("p a n -> p (a n)")).then_inc(ctx_n_hi, 1)

            def fold(g):
                act.wait_ge(m_filled, g + 1)
                copy(mw[0][:, g * 512:(g + 1) * 512], fold_banks(g)[0][:, :]).then_inc(m_hi, 1)
                act.wait_ge(n_filled, g + 1)
                copy(nw[0][:, g * 512:(g + 1) * 512], fold_banks(g)[1][:, :]).then_inc(n_hi, 1)

            def ln(arg):
                kind, b = arg
                if kind == 1:
                    act.wait_ge(q_filled, G * (b + 1))
                elif kind == 3:
                    act.wait_ge(u_filled, LAST[b // 2] + 1)
                misc_ready(("ln", arg))
                copy(xnt[0][:, :, b * T:(b + 1) * T], misc[:, :].rearrange("p (d t) -> p d t", d=DB)).then_inc(xt_hi, 1)

            def link(ins):
                chain[0] += 1
                ins.then_inc(a_chain, 1)
                act.wait_ge(a_chain, chain[0])

            chain = [0]

            def silu(arg):
                p, e = arg
                act.wait_ge(misc_done, use[("in", p, e)] + 1)
                nc.scalar.activation(dtu[:, e, :], xc[:, e, :], ACT.Tanh, scale=0.5).then_inc(pre_tanh, 1)

            def xp(p):
                misc_ready(("xp", p))
                copy(bc[:, :], misc[:, :], 0.5)
                copy(dtl, misc[0:RANK, :], 0.5).then_inc(pre_dtl, 1)
                for e in range(ET):
                    act.wait_ge(pre_u, 2 * p + 2)
                    if p == 0 and e == 0:
                        act.wait_ge(coef_ready, 1)
                    nc.scalar.activation(ys[:, e, p * PAIR:(p + 1) * PAIR], uu[:, e, :], ACT.Copy, scale=dhalf[:, e:e + 1])

            def dt_part(arg):
                p, e = arg
                misc_ready(("dt", p, e))
                nc.scalar.activation(xc[:, e, :], misc[:, :], ACT.Identity, bias=dt_b[:, e:e + 1]).then_inc(misc_done, 1)

            def abs_part(p):
                act.wait_ge(misc_done, use[("dt", p, 1)] + 1)
                link(nc.scalar.activation(dtt[:, :, :], xc[:, :, :], ACT.Abs))
                nc.scalar.activation(dtt[:, :, :], dtt[:, :, :], ACT.Exp, scale=-1.0)
                nc.scalar.activation(xc[:, :, :], xc[:, :, :], ACT.Relu).then_inc(pre_e, 1)

            def scan_b(v):
                p, n = divmod(v, NS)
                misc_ready(("B", v))
                if n >= 2:
                    act.wait_ge(dbu_ready, 2 * (v - 1))
                elif n == 0:
                    act.wait_ge(dtu_ready, p + 1)
                copy(bb[:, v % 2, :], misc[:, :]).then_inc(misc_done, 1)
                for e in range(ET):
                    if n:
                        act.wait_ge(scanned, 2 * v - 1 + e)
                    nc.scalar.activation(da[:, e, :].rearrange("p (b l) -> p b l", b=2)[:, :, 1:T],
                                         dtt[:, e, :].rearrange("p (b l) -> p b l", b=2)[:, :, 1:T], ACT.Exp,
                                         scale=acoef[:, e, n:n + 1]).then_inc(da_ready, 1)

            def q_part(u):
                act.wait_ge(q_filled, u + 1)
                if u >= 2:
                    act.wait_ge(s_filled, 2 * (u - 1))
                copy(qt[0][:, u % 2, :], bank[1][:, :]).then_inc(q_hi, 1)

            def r_part(u):
                act.wait_ge(q_left, u + 1)
                copy(qt[1][:, u % 2, :], bank[1][:, :]).then_inc(q_lo, 1)

            def e_part(u):
                for h in range(2):
                    act.wait_ge(s_masked, 2 * u + h + 1)
                    for t in range(TT):
                        i = 2 * h + t
                        s = probs[u % 3][:, h, t * T:(t + 1) * T]
                        last = nc.scalar.activation(s, s, ACT.Exp, bias=s_min[:, u % 3, i:i + 1], scale=-1.0,
                                                    accum_out=s_sum[:, u % 3, i:i + 1])
                    last.then_inc(p_exp, 1)

            def t_part(u):
                for h in range(2):
                    act.wait_ge(t_filled, 2 * u + h + 1)
                    if u and h == 0:
                        act.wait_ge(v_filled, u)
                    copy(pt[0][:, :, h, :], bank[4 + h][:, :].rearrange("p (s t) -> p s t", s=TT)).then_inc(t_hi, 1)

            def v_part(u):
                act.wait_ge(v_filled, u + 1)
                if u >= 2:
                    act.wait_ge(o_summed, u - 1)
                copy(ot[0][:, u % 2, :], bank[6][:, :]).then_inc(o_hi, 1)

            def rows_part(p):
                misc_ready(("rows", p))
                copy(lg_rows, misc[0:10, :]).then_inc(misc_done, 1)

            def gexp(p):
                act.wait_ge(lg_ready, p + 1)
                nc.scalar.activation(ex[:, :, 0:9], lg[:, :, 0:9], ACT.Exp).then_inc(lg_exp, 1)

            def comb(p):
                misc_ready(("cT", p))
                if p == 1:
                    act.wait_ge(o_summed, nw_free(512))
                else:
                    act.wait_ge(o_summed, nw_free(J0 * P + 512))
                copy(combt[p], misc[0:64, :]).then_inc(ct_hi, 1)

            def w_part(m):
                slot, times = ffn_slot[("W", m)]
                act.wait_ge(ffn_in[slot], 16 * times)
                if m < WSLOTS:
                    act.wait_ge(q_filled, UNITS - G + -(-(m + 1) * FFN_COLS // 512))
                if m >= WSLOTS:
                    act.wait_ge(d_done, ITEMS.index((1, m - WSLOTS)) + 1)
                copy(wslot[0][m % WSLOTS], stage_ffn[:, slot, :]).then_inc(w_hi, 1)

            def g_part(m):
                k, j = ITEMS[m]
                act.wait_ge(g_filled, m + 1)
                if m >= 4:
                    act.wait_ge(h_lo, m - 3)
                if k < 2:
                    nc.scalar.activation(prob[:, m % 4, :], bank[2][:, :], ACT.Tanh, scale=0.5).then_inc(h_tanh, 1)
                else:
                    nc.scalar.activation(prob[:, m % 4, :], gate_bank(m)[:, :], ACT.Tanh, scale=gcoef[:, j:j + 1]).then_inc(h_tanh, 1)

            def hi_part(m):
                act.wait_ge(h_c, m + 1)
                if m >= 3:
                    act.wait_ge(d_done, m - 2)
                else:
                    act.wait_ge(o_summed, nw_free(HID_AT + 512 * (m + 1)))
                copy(hid[0][m % 3], prob[:, m % 4, :]).then_inc(h_hi, 1)

            def ytanh(b):
                act.wait_ge(yg_norm, b + 1)
                if b:
                    act.wait_ge(misc_filled, use[("yt", b - 1)] + 1)
                nc.scalar.activation(ysb[:, :, :], xn[:, :, :], ACT.Tanh, scale=0.5).then_inc(yg_tanh, 1)

            do = {"ctx": ctx, "setup": setup, "fold": fold, "ln": ln, "silu": silu, "xp": xp, "dt": dt_part, "abs": abs_part, "scanB": scan_b, "Q": q_part, "R": r_part, "E": e_part, "T": t_part,
                  "V": v_part, "rows": rows_part, "gexp": gexp, "comb": comb, "W": w_part, "G": g_part, "H": hi_part, "ytanh": ytanh}
            for kind, a in STEPS:
                if kind in do:
                    do[kind](a)

        @block.vector
        def _(dve):
            v_ = nc.vector
            chain = [0]

            def link(ins):
                chain[0] += 1
                ins.then_inc(v_chain, 1)
                dve.wait_ge(v_chain, chain[0])

            def misc_ready(key):
                dve.wait_ge(misc_filled, use[key] + 1)

            def ctx(_):
                dve.wait_ge(ctx_hi, 1)
                v_.tensor_tensor(ct[1][:, :], prob[:, 0:2, :].rearrange("p a n -> p (a n)"), ct[0][:, :].bitcast(F32), ALU.subtract).then_inc(ctx_lo, 1)

            def setup(_):
                dve.wait_ge(a_exp, 1)
                a = acoef[:, :, :]
                v_.tensor_scalar(a, a, -1.0, None, ALU.mult)
                v_.tensor_scalar(gcoef[:, :], small_("g_scale"), 0.5, None, ALU.mult)
                v_.scalar_tensor_tensor(ucoef[:, :], small_("g_scale"), 0.5, small_("u_scale"), ALU.mult, ALU.mult)
                v_.tensor_scalar(dhalf[:, :], d_skip, 0.5, None, ALU.mult).then_inc(coef_ready, 1)

            def fold(g):
                for w, bk, hi, lo in zip((mw, nw), fold_banks(g), (m_hi, n_hi), (m_lo, n_lo)):
                    at = slice(g * 512, (g + 1) * 512)
                    dve.wait_ge(hi, g + 1)
                    v_.tensor_tensor(w[1][:, at], bk[:, :], w[0][:, at].bitcast(F32), ALU.subtract).then_inc(lo, 1)

            def stat(arg):
                kind, b = arg
                if kind == 0:
                    dve.wait_ge(x_in if b else x0_in, 16)
                for t in range(TT):
                    last = v_.bn_stats(bn[:, b % 2, t, :], xs[:, b * TT + t, :])
                link(last)
                for t in range(TT):
                    last = v_.bn_aggr(mv[:, b % 2, t, :], bn[:, b % 2, t, :])
                link(last)
                v_.tensor_scalar(rstd[:, b % 2, :].unsqueeze(2), mv[:, b % 2, :, 1:2], EPS, None, ALU.add).then_inc(mv_ready, 1)

            def normalise(arg):
                kind, b = arg
                dve.wait_ge(rstd_ready, stat_no[arg] + 1)
                if xn_use[0]:
                    dve.wait_ge(misc_filled, xn_use[0])
                for t in range(TT):
                    last = v_.tensor_scalar(xn[:, t, :], xs[:, b * TT + t, :], mv[:, b % 2, t, 0:1], rstd[:, b % 2, t:t + 1],
                                            ALU.subtract, ALU.mult)
                return last

            xn_use = [0]

            def norm(arg):
                normalise(arg).then_inc(xn_ready, 1)
                xn_use[0] = use[("ln", arg)] + 1

            def ln(arg):
                kind, b = arg
                dve.wait_ge(xt_hi, ln_no[arg] + 1)
                at = slice(b * T, (b + 1) * T)
                v_.tensor_tensor(xnt[1][:, :, at], misc[:, :].rearrange("p (d t) -> p d t", d=DB),
                                 xnt[0][:, :, at].bitcast(F32), ALU.subtract).then_inc(misc_done, 1)

            def conv(arg):
                p, e = arg
                misc_ready(("in", p, e))
                if p and e == 0:
                    dve.wait_ge(scanned, 2 * NS)
                    dve.wait_ge(dbu_ready, 2 * NS)
                w = conv_w[:, e * TAPS:(e + 1) * TAPS]
                link(v_.tensor_scalar(xc[:, e, :], misc[:, :], w[:, TAPS - 1:TAPS], conv_b[:, e:e + 1], ALU.mult, ALU.add))
                for back in range(1, TAPS):
                    o = xc[:, e, :].rearrange("p (b l) -> p b l", b=2)[:, :, back:T]
                    i = misc[:, :].rearrange("p (b l) -> p b l", b=2)[:, :, 0:T - back]
                    last = v_.scalar_tensor_tensor(o, i, w[:, TAPS - 1 - back:TAPS - back], o, ALU.mult, ALU.add)
                    if back < TAPS - 1:
                        link(last)
                last.then_inc(misc_done, 1)

            def silu(arg):
                p, e = arg
                dve.wait_ge(pre_tanh, 2 * p + e + 1)
                v_.scalar_tensor_tensor(uu[:, e, :], dtu[:, e, :], 1.0, xc[:, e, :], ALU.add, ALU.mult).then_inc(pre_u, 1)

            def xp(p):
                dve.wait_ge(pre_dtl, p + 1)
                for a in (32, 96):
                    last = v_.scalar_tensor_tensor(bc[a:a + 32, :], misc[a:a + 32, :], 0.5, bc[a:a + 32, :].bitcast(F32),
                                                   ALU.mult, ALU.subtract)
                last.then_inc(misc_done, 1)

            def softplus(arg):
                p, n = arg
                if n == 0:
                    dve.wait_ge(pre_e, p + 1)
                for c in LOG1P[::-1][3 * n:3 * n + 3]:
                    if c == LOG1P[-1]:
                        link(v_.tensor_scalar(dtu[:, :, :], dtt[:, :, :], c, None, ALU.mult))
                    else:
                        link(v_.scalar_tensor_tensor(dtu[:, :, :], dtu[:, :, :], c, dtt[:, :, :], ALU.add, ALU.mult))
                if n == SOFT - 1:
                    link(v_.tensor_tensor(dtt[:, :, :], dtu[:, :, :], xc[:, :, :], ALU.add))
                    link(v_.scalar_tensor_tensor(dtu[:, :, :], dtt[:, :, :], 0.5, uu[:, :, :], ALU.mult, ALU.mult))
                    v_.memset(da.rearrange("p e (b l) -> p (e b) l", b=2)[:, :, 0:1], 0.0).then_inc(dtu_ready, 1)

            def scan_c(v):
                for e in range(ET):
                    i = 2 * v + e
                    s = ring[:, i % 4, :]
                    dve.wait_ge(da_ready, i + 1)
                    dve.wait_ge(dbu_ready, i + 1)
                    v_.tensor_tensor_scan(s, da[:, e, :], s, 0.0, ALU.mult, ALU.add).then_inc(scanned, 1)
                misc_ready(("C", v))
                for e in range(ET):
                    i = 2 * v + e
                    s = ring[:, i % 4, :]
                    dve.wait_ge(scanned, i + 1)
                    v_.tensor_tensor(s, s, misc[:, :], ALU.mult).then_inc(hc_ready if e == 0 else misc_done, 1)

            def q_part(u):
                b, g = divmod(u, G)
                if g == 0:
                    if u == 0:
                        dve.wait_ge(mask_in, 16)
                        v_.reduce_max(mask_any[:, :], mask_sb[:, :].rearrange("p (b t) -> p b t", b=B), AX.X)
                    v_.tensor_scalar(mask_bias[:, b % 2, :], mask_sb[:, b * T:(b + 1) * T], 1.0, MASKED,
                                     ALU.subtract, ALU.mult).then_inc(mbias_ready, 1)

            def s_part(u):
                b, g = divmod(u, G)
                if g == 0:
                    dve.wait_ge(mbias_ready, b + 1)
                for h in range(2):
                    dve.wait_ge(s_filled, 2 * u + h + 1)
                    if u >= 3 and h == 0:
                        dve.wait_ge(t_filled, 2 * (u - 2))
                    if u == 2 and h == 0:
                        dve.wait_ge(n_filled, G)
                    if u == 1 and h == 0:
                        dve.wait_ge(setup_done, 1)
                    for t in range(TT):
                        i = 2 * h + t
                        last = v_.tensor_tensor_reduce(
                            out=probs[u % 3][:, h, t * T:(t + 1) * T], in0=bank[2 + h][:, t * T:(t + 1) * T],
                            in1=mask_bias[:, b % 2, :], scale=-(float(P) ** -0.5), scalar=3.0e38, op0=ALU.add, op1=ALU.min,
                            accum_out=s_min[:, u % 3, i:i + 1])
                    last.then_inc(s_masked, 1)

            def t_part(u):
                for h in range(2):
                    dve.wait_ge(t_hi, 2 * u + h + 1)
                    v_.tensor_tensor(pt[1][:, :, h, :], bank[4 + h][:, :].rearrange("p (s t) -> p s t", s=TT),
                                     pt[0][:, :, h, :].bitcast(F32), ALU.subtract).then_inc(t_lo, 1)

            def i_part(u):
                b = u // G
                dve.wait_ge(p_exp, 2 * u + 2)
                link(v_.reciprocal(s_inv[:, u % 3, :], s_sum[:, u % 3, :]))
                v_.tensor_scalar(s_inv[:, u % 3, :], s_inv[:, u % 3, :], mask_any[:, b:b + 1], None, ALU.mult).then_inc(p_inv, 1)

            def v_part(u):
                dve.wait_ge(o_hi, u + 1)
                v_.tensor_tensor(ot[1][:, u % 2, :], bank[6][:, :], ot[0][:, u % 2, :].bitcast(F32), ALU.subtract).then_inc(o_lo, 1)

            def res(b):
                dve.wait_ge(o_summed, G * (b + 1))
                rows = xs[:, b * TT:(b + 1) * TT, :]
                v_.tensor_tensor(rows, rows, bank[0][:, :].rearrange("p (t d) -> p t d", t=TT), ALU.add).then_inc(res_done, 1)
                dve.wait_ge(res_done, b + 1)

            def gate(p):
                misc_ready(("lg", p))
                v_.tensor_copy(lg[:, :, :], misc[:, 0:40].rearrange("p (t n) -> p t n", t=4)).then_inc(misc_done, 1)
                dve.wait_ge(misc_done, use[("lg", p)] + 1)
                L = lg[:, :, 0:E]
                a = L.unsqueeze(2).to_broadcast([P, 4, E, E])
                c = L.unsqueeze(3).to_broadcast([P, 4, E, E])
                v_.tensor_tensor(gt[:, :, :, :], a, c, ALU.is_gt)
                link(v_.tensor_tensor(eq[:, :, :, :], a, c, ALU.is_equal))
                low = small_("lower").unsqueeze(1).to_broadcast([P, 4, E * E])
                eqf = eq[:, :, :, :].rearrange("p t e j -> p t (e j)")
                link(v_.tensor_tensor(eqf, eqf, low, ALU.mult))
                link(v_.tensor_tensor(gt[:, :, :, :], gt[:, :, :, :], eq[:, :, :, :], ALU.add))
                link(v_.reduce_sum(rk[:, :, :], gt[:, :, :, :], AX.X))
                link(v_.tensor_scalar(rk[:, :, :], rk[:, :, :], 1.5, None, ALU.is_lt))
                link(v_.reduce_max(r1[:, :, :].rearrange("p t n -> p (t n)"), L, AX.X))
                link(v_.tensor_tensor(L, L, r1[:, :, :].to_broadcast([P, 4, E]), ALU.subtract))
                v_.tensor_scalar(lg[:, :, E:E + 1], lg[:, :, E:E + 1], -1.0, None, ALU.mult).then_inc(lg_ready, 1)

            def gate2(p):
                dve.wait_ge(lg_exp, p + 1)
                W = ex[:, :, 0:E]
                link(v_.tensor_tensor(W, W, rk[:, :, :], ALU.mult))
                link(v_.reduce_sum(r1[:, :, :].rearrange("p t n -> p (t n)"), W, AX.X))
                link(v_.reciprocal(r1[:, :, :], r1[:, :, :]))
                link(v_.tensor_tensor(W, W, r1[:, :, :].to_broadcast([P, 4, E]), ALU.mult))
                S = ex[:, :, E:E + 1]
                link(v_.tensor_scalar(S, S, 1.0, None, ALU.add))
                link(v_.reciprocal(S, S))
                v_.tensor_scalar(cm[:, :, 0:E + 1], ex[:, :, 0:E + 1], 0.5, None, ALU.mult)
                v_.tensor_scalar(cm[:, :, 32:32 + E + 1], ex[:, :, 0:E + 1], 0.5, None, ALU.mult).then_inc(cm_ready, 1)

            def comb(p):
                dve.wait_ge(ct_hi, p + 1)
                v_.tensor_tensor(combt[p][32:64, :], misc[32:64, :], combt[p][32:64, :].bitcast(F32), ALU.subtract).then_inc(misc_done, 1)

            def g_part(m):
                k, j = ITEMS[m]
                t = prob[:, m % 4, :]
                dve.wait_ge(h_tanh, m + 1)
                v_.scalar_tensor_tensor(t, t, 1.0, gate_bank(m)[:, :], ALU.add, ALU.mult).then_inc(h_g, 1)
                dve.wait_ge(u_filled, m + 1)
                dve.wait_ge(h_g, m + 1)
                v_.tensor_tensor(t, t, bank[3][:, :], ALU.mult).then_inc(h_u, 1)

            def c_part(m):
                k, j = ITEMS[m]
                t = prob[:, m % 4, :]
                dve.wait_ge(h_u, m + 1)
                if k < 2:
                    dve.wait_ge(c_filled, m + 1)
                    v_.tensor_tensor(t, t, bank[4][:, :], ALU.mult).then_inc(h_c, 1)
                else:
                    v_.tensor_scalar(t, t, ucoef[:, j:j + 1], None, ALU.mult).then_inc(h_c, 1)

            def w_part(m):
                if m < WSLOTS:
                    dve.wait_ge(w_hi, m + 1)
                    v_.tensor_tensor(wslot[1][m], stage_ffn[:, ffn_slot[("W", m)][0], :], wslot[0][m].bitcast(F32), ALU.subtract).then_inc(w_lo_first, 1)

            def w1_part(j):
                slot, times = ffn_slot[("W1", j)]
                dve.wait_ge(ffn_in[slot], 16 * times)
                w = stage_ffn[:, slot, :]
                link(v_.tensor_scalar(q1c[:, :].bitcast(I32), w.bitcast(I32), 0x7F800000, None, ALU.bitwise_and))
                link(v_.tensor_scalar(q1c[:, :], q1c[:, :], 2.0 ** -6, 1.5 * 2.0 ** 20, ALU.max, ALU.mult))
                link(v_.tensor_tensor(w, w, q1c[:, :], ALU.add))

            def w1b_part(j):
                slot, times = ffn_slot[("W1", j)]
                w = stage_ffn[:, slot, :]
                link(v_.tensor_tensor(w, w, q1c[:, :], ALU.subtract))
                link(v_.tensor_scalar(q1c[:, :], w, 7.3e35, 0.0, ALU.mult, ALU.mult))
                if j == 0:
                    dve.wait_ge(o_summed, UNITS)
                v_.tensor_tensor(w1slot[j], q1c[:, :], w, ALU.add).then_inc(w1_ready, 1)
                dve.wait_ge(w1_ready, j + 1)

            def acc(arg):
                k, n = arg
                p = k % 2
                dve.wait_ge(d_done, LAST[k] + 1)
                rows = xs[:, p * 4 + 2 * n:p * 4 + 2 * n + 2, :]
                sums = acc_banks(k)[n][:, :].rearrange("p (t d) -> p t d", t=2)
                if k < 2:
                    v_.tensor_tensor(rows, rows, sums, ALU.add).then_inc(acc_done, 1)
                    dve.wait_ge(acc_done, 2 * k + n + 1)
                else:
                    if k == 2 and n == 0:
                        dve.wait_ge(dsc_in, 16)
                    for t in range(2):
                        last = v_.tensor_tensor(xn[:, t, :], sums[:, t, :], dscale[:, :], ALU.mult)
                    link(last)
                    v_.tensor_tensor(rows, rows, xn[:, :, :], ALU.add).then_inc(out_ready, 1)
                    dve.wait_ge(out_ready, 2 * p + n + 1)

            def ynorm(b):
                normalise((2, b)).then_inc(yg_norm, 1)

            def ymul(b):
                dve.wait_ge(yg_tanh, b + 1)
                link(v_.scalar_tensor_tensor(ysb[:, :, :], ysb[:, :, :], 1.0, xn[:, :, :], ALU.add, ALU.mult))
                dve.wait_ge(y_added, 2 * NS * (b // 2 + 1))
                for e in range(ET):
                    last = v_.tensor_tensor(ysb[:, e, :], ysb[:, e, :], ys[:, e, b * T:(b + 1) * T], ALU.mult)
                last.then_inc(yg_ready, 1)

            def yt(b):
                misc_ready(("yt", b))
                rows = xs[:, b * TT:(b + 1) * TT, :]
                v_.scalar_tensor_tensor(rows, misc[:, :].rearrange("p (t d) -> p t d", t=TT), 0.5, rows, ALU.mult, ALU.add).then_inc(misc_done, 1)
                dve.wait_ge(misc_done, use[("yt", b)] + 1)

            do = {"ctx": ctx, "setup": setup, "fold": fold, "stat": stat, "norm": norm, "ln": ln, "conv": conv, "silu": silu, "xp": xp, "soft": softplus, "scanC": scan_c, "Q": q_part, "S": s_part, "T": t_part,
                  "I": i_part, "V": v_part, "res": res, "gate": gate, "gate2": gate2, "comb": comb, "G": g_part, "c": c_part, "W": w_part, "W1": w1_part, "W1b": w1b_part, "acc": acc,
                  "ynorm": ynorm, "ymul": ymul, "yt": yt}
            for kind, a in STEPS:
                if kind in do:
                    do[kind](a)

        @block.gpsimd
        def _(pool):
            gp = nc.gpsimd

            def setup(_):
                lower = lambda dst, src, hi: gp.tensor_tensor(dst, src, hi.bitcast(F32), ALU.subtract)
                pool.wait_ge(in_w_hi, 1)
                lower(in_split[1], in_w, in_split[0]).then_inc(in_w_split, 1)
                gp.tensor_scalar(neg_ident[:, :], ident, -1.0, None, ALU.mult)
                gp.memset(cm[:, :, :], 0.0)
                gp.tensor_copy(sel[:, :, :], small_("sel").unsqueeze(2).to_broadcast([P, NS, P]))
                pool.wait_ge(a_exp, 1)
                lower(rw[1][:, :], small_("route_w"), rw[0][:, :])
                pool.wait_ge(ctx_n_hi, 1)
                lower(cn[1][:, :, :].rearrange("p n c -> p (n c)"), prob[:, 2:4, :].rearrange("p a n -> p (a n)"),
                      cn[0][:, :, :].rearrange("p n c -> p (n c)")).then_inc(setup_done, 1)

            def n_part(u):
                s = probs[u % 3].rearrange("p h (t s) -> p (h t) s", t=TT)
                pool.wait_ge(p_inv, u + 1)
                gp.tensor_tensor(s, s, s_inv[:, u % 3, :].unsqueeze(2).to_broadcast([P, 4, T]), ALU.mult).then_inc(p_norm, 1)

            def product(v, e):
                i = 2 * v + e
                if i >= 4:
                    pool.wait_ge(y_added, i - 3)
                gp.tensor_tensor(ring[:, i % 4, :], dtu[:, e, :], bb[:, v % 2, :], ALU.mult).then_inc(dbu_ready, 1)

            def add(v, e):
                i = 2 * v + e
                p = v // NS
                y = ys[:, e, p * PAIR:(p + 1) * PAIR]
                if e == 0:
                    pool.wait_ge(hc_ready, v + 1)
                else:
                    pool.wait_ge(misc_done, use[("C", v)] + 1)
                if i >= 2:
                    pool.wait_ge(y_added, i - 1)
                gp.tensor_tensor(y, y, ring[:, i % 4, :], ALU.add).then_inc(y_added, 1)

            def scan_b(v):
                pool.wait_ge(misc_done, use[("B", v)] + 1)
                if v % NS == 0:
                    pool.wait_ge(dtu_ready, v // NS + 1)
                for e in range(ET):
                    product(v, e)

            def sum_part(v):
                for e in range(ET):
                    add(v, e)

            def esel_load(_):
                pool.wait_ge(o_summed, nw_free(J0 * P))
                gp.dma_start(esel, expert_sel).then_inc(esel_in, 16)

            gp.memset(neg_half[:, :], -0.5).then_inc(g_const, 1)
            pool.wait_ge(g_const, 1)

            def rstd_part(arg):
                pool.wait_ge(mv_ready, stat_no[arg] + 1)
                gp.tensor_tensor(rstd[:, arg[1] % 2, :], rstd[:, arg[1] % 2, :], neg_half[:, :], ALU.pow).then_inc(rstd_ready, 1)

            def w_part(m):
                if m < WSLOTS:
                    return
                slot, times = ffn_slot[("W", m)]
                pool.wait_ge(w_hi, m + 1)
                gp.tensor_tensor(wslot[1][m % WSLOTS], stage_ffn[:, slot, :], wslot[0][m % WSLOTS].bitcast(F32), ALU.subtract).then_inc(w_lo, 1)

            def lo_part(m):
                pool.wait_ge(h_hi, m + 1)
                gp.tensor_tensor(hid[1][m % 3], prob[:, m % 4, :], hid[0][m % 3].bitcast(F32), ALU.subtract).then_inc(h_lo, 1)

            do = {"setup": setup, "esel": esel_load, "stat": rstd_part, "N": n_part, "scanB": scan_b, "sum": sum_part, "W": w_part, "H": lo_part}
            for kind, a in STEPS:
                if kind in do:
                    do[kind](a)


def kernel(x, ctx_1024, mask_BxS2_bf1, L0_xattn_Wq, L0_xattn_Wk, L0_xattn_Wv, L0_xattn_Wo, L0_ffn_gate_w, L0_ffn_w_gate,
           L0_ffn_w_up, L0_ffn_w_down, L0_ffn_shgate_w, L0_ffn_shw_gate, L0_ffn_shw_up, L0_ffn_shw_down,
           L1_xattn_in_proj_w, L1_xattn_conv_w, L1_xattn_conv_b, L1_xattn_x_proj_w, L1_xattn_dt_proj_w,
           L1_xattn_dt_proj_b, L1_xattn_A_log, L1_xattn_D, L1_ffn_gate_w, L1_ffn_up_w, L1_ffn_down_w,
           L1_ffn_gate_scale, L1_ffn_up_scale, L1_ffn_down_scale):
    import concourse.bacc as bacc
    import numpy as np
    from concourse.bass_utils import run_bass_kernel_spmd

    f32 = np.float32

    def blocks(w):
        n = w.shape[0] // P
        return w.reshape(n, P, -1).transpose(1, 0, 2).reshape(P, -1)

    ctx = np.ascontiguousarray(ctx_1024).reshape(B * T, C)
    wq = np.asarray(L0_xattn_Wq).reshape(D, G, 2, P)
    wk = np.asarray(L0_xattn_Wk).reshape(C, G, P)
    wv = np.asarray(L0_xattn_Wv).reshape(C, G, P)
    wo = np.asarray(L0_xattn_Wo).reshape(G, 2, P, D)
    fold_w = np.concatenate([
        wq.transpose(1, 3, 2, 0).reshape(G, P, 2 * D), wo.transpose(0, 2, 1, 3).reshape(G, P, 2 * D),
        wk.transpose(1, 2, 0), wv.transpose(1, 2, 0)], axis=2)

    pad = J0 * P - E * HE - HS
    wide = lambda w, s: np.concatenate([np.asarray(w).transpose(1, 0, 2).reshape(D, E * HE), np.asarray(s), np.zeros((D, pad), f32)], axis=1)
    down0 = np.concatenate([np.asarray(L0_ffn_w_down).reshape(E * HE, D), np.asarray(L0_ffn_shw_down), np.zeros((pad, D), f32)])

    def tiles(gate, up, down):
        n = down.shape[0] // P
        cut = lambda w: w.reshape(DB, P, n, P).transpose(2, 1, 0, 3).reshape(n, P, DB * P)
        return np.concatenate([cut(gate), cut(up), down.reshape(n, P, D)], axis=2)

    ffn_w = np.concatenate([
        tiles(wide(L0_ffn_w_gate, L0_ffn_shw_gate), wide(L0_ffn_w_up, L0_ffn_shw_up), down0),
        tiles(np.asarray(L1_ffn_gate_w), np.asarray(L1_ffn_up_w), np.asarray(L1_ffn_down_w))])

    xp = np.asarray(L1_xattn_x_proj_w)
    xp_t = np.zeros((ET * P, P), f32)
    for at in (0, 32):
        xp_t[:, at:at + RANK + NS] = xp[:RANK + NS].T
    for at in (64, 96):
        xp_t[:, at + RANK:at + RANK + NS] = xp[RANK + NS:].T
    dt_w = np.zeros((P, ET * P), f32)
    dt_w[:RANK] = np.asarray(L1_xattn_dt_proj_w).T
    route = np.zeros((D, 10), f32)
    route[:, :E] = np.asarray(L0_ffn_gate_w).T
    route[:, E] = np.asarray(L0_ffn_shgate_w)
    lower = np.broadcast_to((np.arange(E)[None, :] < np.arange(E)[:, None]).astype(f32).reshape(1, E * E), (P, E * E))
    sel = np.zeros((P, NS), f32)
    for at in (0, 32, 64, 96):
        sel[at + RANK + np.arange(NS), np.arange(NS)] = 1
    expert_sel = np.zeros((64, J0 * P), f32)
    for e in range(E + 1):
        expert_sel[[e, 32 + e], e * HE:(e * HE + (HE if e < E else HS))] = 1
    parts = {
        "ident": np.eye(P, dtype=f32), "in_w": np.asarray(L1_xattn_in_proj_w).T, "xp_w": blocks(xp_t), "dt_w": dt_w,
        "a_log": blocks(np.asarray(L1_xattn_A_log)), "conv_w": blocks(np.asarray(L1_xattn_conv_w).reshape(ET * P, TAPS)),
        "conv_b": blocks(np.asarray(L1_xattn_conv_b)[:, None]), "dt_b": blocks(np.asarray(L1_xattn_dt_proj_b)[:, None]),
        "d_skip": blocks(np.asarray(L1_xattn_D)[:, None]), "g_scale": blocks(np.asarray(L1_ffn_gate_scale)[:, None]),
        "u_scale": blocks(np.asarray(L1_ffn_up_scale)[:, None]), "route_w": blocks(route), "lower": lower, "sel": sel,
    }
    small = np.concatenate([parts[n] for n, _ in SMALL], axis=1)

    arrays = {
        "x": np.asarray(x).reshape(B * T, D), "ctx_n": ctx, "ctx_t": ctx.T, "fold_w": fold_w, "ffn_w": ffn_w, "small": small,
        "expert_sel": expert_sel, "mask": np.asarray(mask_BxS2_bf1).reshape(B * T).view(np.uint8),
        "down_scale": np.asarray(L1_ffn_down_scale),
    }
    nc = bacc.Bacc("TRN2", target_bir_lowering=False, num_devices=1)
    args, given = [], {}
    for name, a in arrays.items():
        given[f"in_{name}"] = a = np.ascontiguousarray(a)
        args.append(nc.dram_tensor(f"in_{name}", a.shape, mybir.dt.from_np(a.dtype), kind="ExternalInput").ap())
    out = nc.dram_tensor("out", (B * T, D), F32, kind="ExternalOutput").ap()
    build_program(nc, *args, out)
    r = run_bass_kernel_spmd(nc, [given], core_ids=[0])
    return r.results[0]["out"].reshape(B, T, D)
```

```python
from contextlib import ExitStack

import concourse.bass as bass
from concourse import mybir

F32 = mybir.dt.float32
F32R = mybir.dt.float32r
U8 = mybir.dt.uint8
I32 = mybir.dt.int32
ALU = mybir.AluOpType
ACT = mybir.ActivationFunctionType
AX = mybir.AxisListType

P = 128
B, T, D = 4, 256, 256
C = 128
G = 8
TT = T // P
DB = D // P
E, HE, HS = 8, 176, 352
J0 = -(-(E * HE + HS) // P)
HID1 = 768
J1 = HID1 // P
NS, RANK, TAPS = 16, 8, 4
XP = RANK + 2 * NS
BC_SLOTS = 3
ET = 2
PAIR = 2 * T
UNITS = B * G
FFN_COLS = 2 * DB * P + D
START = (0, 0, 0, 0, 0, 1, 1, 1)
SOFT = 3
WSLOTS = 5
W_VECTOR = ()
HID_VECTOR = (1, 25, 27, 33, 39)
W_AT = ((0, 28), (1, 31), (2, 31), (3, 32), (4, 33))
LAST_SCAN = 32
EPS = 1e-5
MASKED = 1e30
LOG1P = [0.9999999705406568, -0.49999501516786626, 0.3331927134249427, -0.2484436989243044, 0.19111431080478863,
         -0.13674769705383674, 0.07836166801762622, -0.02958850739253811, 0.005253457797007794]

SMALL = [
    ("ident", P), ("in_w", ET * P), ("xp_w", ET * P), ("dt_w", ET * P), ("a_log", ET * NS),
    ("conv_w", ET * TAPS), ("conv_b", ET), ("dt_b", ET), ("d_skip", ET), ("g_scale", J1),
    ("u_scale", J1), ("route_w", DB * 10), ("lower", E * E), ("xp_scale", 1),
]
SMALL_AT = {}
SMALL_COLS = 0
for _name, _n in SMALL:
    SMALL_AT[_name] = (SMALL_COLS, SMALL_COLS + _n)
    SMALL_COLS += _n


def ffn_items():
    order = START + (1, 0) * (J0 - 3 - START.count(0)) + (0, 0, 0)
    order += (1,) * (J0 - order.count(1))
    items = [(k, order[:m].count(k)) for m, k in enumerate(order)]
    return items + [(k, j) for k in (2, 3) for j in range(J1)]


ITEMS = ffn_items()
LAST = [max(m for m, (k, _) in enumerate(ITEMS) if k == phase) for phase in range(4)]


GATE_AT = (
    (27, ("gate", 0)), (26, ("rows", 0)), (28, ("gexp", 0)), (28, ("gate2", 0)), (30, ("esel", 0)), (32, ("comb", 0)),
)
NORM_BEFORE = (-6, -4, -2)
NORM_AFTER = (5, 6, 7)
SCAN_ITEMS = (5, 8, 11, 12, 14, 16, 17, 18, 19, 20, 21, 22, 26)
ROUND_ITEMS = (6, 7, 9, 10, 11, 13, 15, 16, 18, 19, 20, 22)


PREP = (
    (("conv", 0),), (("silu", 0),), (("conv", 1),), (("silu", 1),), (("xp", None),), (("dt", 0),), (("dt", 1), ("abs", None)),
    (), (("soft", 0),), (), (("soft", 1),), (), (("soft", 2),), (("dt_end", None),),
)
START_STEPS = (
    ("ctx", 0), ("stat", (0, 0)), ("norm", (0, 0)), ("ln", (0, 0)), ("setup", 0), ("fold", 0), ("fold", 1),
    ("conv", (0, 0)), ("silu", (0, 0)), ("fold", 2), ("fold", 3), ("conv", (0, 1)), ("silu", (0, 1)), ("fold", 4),
    ("fold", 5), ("stat", (0, 1)), ("xp", 0), ("fold", 6), ("norm", (0, 1)), ("dt", (0, 0)), ("fold", 7),
    ("dt", (0, 1)), ("Q", 0), ("R", 0), ("ln", (0, 1)), ("abs", 0),
)
FFN_AT = (
    (3, "after", ("ln", (1, 3))), (4, "inside", ("gate", 1)), (3, "after", ("rows", 1)),
    (4, "after", ("gate2", 1)), (4, "after", ("gexp", 1)), (23, "after", ("stat", (2, 0))),
    (5, "inside", ("comb", 1)), (23, "after", ("stat", (2, 1))), (24, "inside", ("ytanh", 0)),
    (24, "after", ("ymul", 0)), (23, "after", ("ynorm", 0)), (24, "after", ("ynorm", 1)),
    (25, "inside", ("yt", 0)), (25, "inside", ("ytanh", 1)), (25, "after", ("ymul", 1)),
    (25, "inside", ("stat", (3, 0))), (26, "after", ("stat", (3, 1))), (26, "after", ("norm", (3, 0))),
    (26, "inside", ("yt", 1)), (27, "inside", ("norm", (3, 1))), (28, "after", ("stat", (2, 2))),
    (27, "inside", ("ln", (3, 0))), (27, "after", ("ln", (3, 1))), (28, "after", ("stat", (2, 3))),
    (29, "after", ("ynorm", 2)), (29, "after", ("ymul", 2)), (29, "after", ("ytanh", 2)),
    (29, "after", ("ynorm", 3)), (30, "after", ("ymul", 3)), (30, "after", ("ytanh", 3)),
    (30, "after", ("yt", 2)), (31, "after", ("norm", (3, 2))), (30, "after", ("stat", (3, 2))),
    (31, "after", ("yt", 3)), (32, "inside", ("norm", (3, 3))), (31, "after", ("stat", (3, 3))),
    (33, "after", ("ln", (3, 3))), (32, "after", ("ln", (3, 2))),
)


ATTENTION_ORDER = {
    "pe": ("Q", "E", "S", "I", "R", "middle", "H", "T", "V", "O", "c", "N", "sum", "G", "beside", "end"),
    "act": ("Q", "R", "S", "E", "T", "I", "V", "middle", "end", "O", "beside", "sum", "c", "N", "G", "H"),
    "dve": ("R", "S", "E", "middle", "Q", "T", "V", "I", "sum", "end", "beside", "c", "O", "N", "G", "H"),
    "pool": ("middle", "I", "Q", "E", "R", "c", "T", "end", "V", "sum", "S", "O", "N", "G", "H", "beside"),
}
FFN_ORDER = {
    "pe": ("G", "inside", "c", "H first", "D", "scanB", "scanC", "sum", "H", "after", "round"),
    "act": ("c", "scanC", "H first", "G", "H", "round", "scanB", "D", "inside", "sum", "after"),
    "dve": ("H first", "G", "inside", "scanB", "c", "H", "sum", "scanC", "D", "round", "after"),
    "pool": ("scanB", "inside", "G", "H", "sum", "round", "H first", "after", "D", "scanC", "c"),
}


def timeline():
    norm = lambda kind, b: [("stat", (kind, b)), ("norm", (kind, b)), ("ln", (kind, b))]
    prep_steps = lambda p: [[(kind, p if n is None else (p, n)) for kind, n in more] for more in PREP]
    first = [[step for step in more if step not in START_STEPS] for more in prep_steps(0)]
    while not first[0]:
        first.pop(0)
    steps = list(START_STEPS)

    beside = {}
    for b in (2, 3):
        for n, step in enumerate(norm(0, b)):
            beside.setdefault((b - 1) * G + NORM_BEFORE[n], []).append(step)
    for b in (0, 1, 2):
        for n, step in enumerate(norm(1, b)):
            beside.setdefault((b + 1) * G + NORM_AFTER[n], []).append(step)
    for i, step in GATE_AT + tuple((i, ("W", j)) for j, i in W_AT):
        beside.setdefault(i, []).append(step)

    plan = [("start", {"all": steps})]
    v, prep = 0, first + [[("scanB", 0)]]
    for i in range(UNITS + 4):
        now = not prep and i <= LAST_SCAN
        part = {
            "Q": [("Q", i + 1)] if i + 1 < UNITS else [],
            "S": [("S", i)] if i < UNITS else [],
            "R": [("R", i + 1)] if i + 1 < UNITS else [],
            "E": [("E", i)] if i < UNITS else [],
            "middle": [("scanC", v)] if now else prep.pop(0) if prep else [],
            "T": [("T", i - 2)] if 2 <= i <= UNITS + 1 else [],
            "V": [("V", i - 3)] if 3 <= i <= UNITS + 2 else [],
            "I": [("I", i)] if i < UNITS else [],
            "O": ([("O", i - 4)] if i >= 4 else []) + ([("res", (i - 4) // G)] if i >= 4 and (i - 4) % G == G - 1 else []),
            "N": [("N", i)] if i < UNITS else [],
            "sum": [("sum", v)] if now else [],
            "beside": beside.pop(i, []),
        }
        if now:
            v += 1
            part["end"] = [("scanB", v)] if v != NS else []
            prep = prep_steps(1) + [[("scanB", v)]] if v == NS else []
        else:
            part["end"] = prep.pop(0) if prep else []
        m = i - UNITS
        part["c"] = [("c", m - 1)] if m >= 1 else []
        part["G"] = [("G", m)] if 0 <= m <= 2 else []
        part["H"] = [("H", m - 1)] if m >= 1 else []
        plan.append(("attention", part))
    plan.append(("start", {"all": [("stat", (1, 3)), ("norm", (1, 3))]}))
    assert not beside and not prep, (beside, prep)

    at = {}
    for m, place, step in FFN_AT:
        at.setdefault((m, place), []).append(step)
    down, rounds, pending, sums = 0, 0, [], []
    for m in range(3, len(ITEMS)):
        flush = m - 1 in LAST[:2]
        part = {
            "H first": [("H", m - 1)] if flush and m > 3 else [],
            "G": [("G", m)],
            "scanB": pending,
            "inside": at.pop((m, "inside"), []),
            "H": [("H", m - 1)] if not flush and m > 3 else [],
            "c": [("c", m)],
            "sum": sums,
            "scanC": [], "D": [], "round": [],
            "after": at.pop((m, "after"), []),
        }
        pending, sums = [], []
        if m in SCAN_ITEMS and v < 2 * NS:
            part["scanC"] = [("scanC", v)]
            v += 1
            pending = [("scanB", v)] if v < 2 * NS else [("sum", v - 1)]
            sums = [("sum", v - 1)] if v < 2 * NS else []
        while down <= m - 2 or down < m and flush:
            part["D"].append(("D", down))
            if ITEMS[down][0] == 1 and ITEMS[down][1] + WSLOTS < J0:
                part["D"].append(("W", ITEMS[down][1] + WSLOTS))
            if down in LAST:
                part["D"] += [("acc", (LAST.index(down), n)) for n in range(2)]
            down += 1
        if m in ROUND_ITEMS:
            part["round"].append(("W1" if rounds % 2 == 0 else "W1b", rounds // 2))
            rounds += 1
        plan.append(("ffn", part))
    assert v == 2 * NS and rounds == 2 * J1 and not at, (v, rounds, at)
    m = len(ITEMS) - 1
    plan.append(("start", {"all": [("H", m), ("D", m - 1), ("D", m), ("acc", (3, 0)), ("acc", (3, 1))]}))
    return plan


def order(engine):
    names = {"start": ("all",), "attention": ATTENTION_ORDER[engine], "ffn": FFN_ORDER[engine]}
    return [step for kind, part in timeline() for name in names[kind] for step in part[name]]


STEPS = order("pe")


def build_program(nc, x, ctx_n, ctx_t, fold_w, ffn_w, small, expert_sel, mask, down_scale, bc_rows, out):
    stack = ExitStack()
    with stack:
        def sb(name, shape, dt=F32):
            return stack.enter_context(nc.sbuf_tensor(name, shape, dt))

        def sem(name):
            return stack.enter_context(nc.semaphore(name))

        xs = sb("xs", [P, B * TT, D])
        cn = [sb(f"cn_{s}", [P, B * TT, C], F32R) for s in ("hi", "lo")]
        ct = [sb(f"ct_{s}", [P, B * T], F32R) for s in ("hi", "lo")]
        stage = sb("stage", [P, 2560])
        stage_fold = stage[:, :].rearrange("p (s n) -> p s n", s=2)
        stage_ffn = stage[:, 0:3 * FFN_COLS].rearrange("p (s n) -> p s n", s=3)
        mw = [sb(f"mw_{s}", [P, G * 512], F32R) for s in ("hi", "lo")]
        nw = [sb(f"nw_{s}", [P, G * 512], F32R) for s in ("hi", "lo")]
        xnt = [sb(f"xnt_{s}", [P, DB, B * T], F32R) for s in ("hi", "lo")]
        qt = [sb(f"qt_{s}", [P, 2, 512], F32R) for s in ("hi", "lo")]
        prob = sb("prob", [P, 4, 512])
        probs = [prob[:, 0:2, :], prob[:, 2:4, :], stage[:, 1536:2560].rearrange("p (h n) -> p h n", h=2)]
        pt = [sb(f"pt_{s}", [P, TT, 2, T], F32R) for s in ("hi", "lo")]
        ot = [sb(f"ot_{s}", [P, 2, 512], F32R) for s in ("hi", "lo")]
        sm = sb("sm", [P, SMALL_COLS])
        mask_sb = sb("mask_sb", [P, B * T], U8)
        mask_bias = sb("mask_bias", [P, 2, T])
        mask_any = sb("mask_any", [P, B])
        dscale = sb("dscale", [P, D])
        s_min = sb("s_min", [P, 3, 4])
        dhalf = sb("dhalf", [P, ET])
        neg_ident = sb("neg_ident", [P, P], F32R)
        s_sum = sb("s_sum", [P, 3, 4])
        s_inv = sb("s_inv", [P, 3, 4])
        xn = sb("xn", [P, TT, D])
        bn = sb("bn", [P, 2, TT, 6])
        mv = sb("mv", [P, 2, TT, 2])
        rstd = sb("rstd", [P, 2, TT])
        neg_half = sb("neg_half", [P, TT])
        front = sb("front", [P, 4, 512])
        xc = front[:, 0:2, :]
        uu = front[:, 2:4, :]
        da = front[:, 2:4, :]
        dtt = sb("dtt", [P, ET, 512])
        dtu = sb("dtu", [P, ET, 512])
        ys = sb("ys", [P, ET, B * T])
        xp_rows = sb("xp_rows", [XP, 512])
        bc = [t[:, :, :] for t in (sb("bc0", [P, 2, 512]), sb("bc1", [P, 2, 512]), xc)]
        ring = sb("ring", [P, 2, ET, 512])
        acoef = sb("acoef", [P, ET, NS])
        lg = sb("lg", [P, 4, 10])
        ex = sb("ex", [P, 4, 10])
        r1 = sb("r1", [P, 4, 1])
        cmp_ = sb("cmp_", [P, FFN_COLS])
        lg_rows = cmp_[0:10, 0:512]
        gt, eq = (cmp_[:, a:a + 4 * E * E].rearrange("p (t e j) -> p t e j", t=4, e=E) for a in (0, 4 * E * E))
        rk = sb("rk", [P, 4, E])
        cm = sb("cm", [P, 4, 64])
        rw = [sb(f"rw_{s}", [P, DB * 10], F32R) for s in ("hi", "lo")]
        ucoef = sb("ucoef", [P, J1])
        gcoef = sb("gcoef", [P, J1])
        ysb = mask_bias
        in_split = [sb(f"in_split_{s}", [P, ET * P], F32R)[:, :] for s in ("hi", "lo")]
        q1c = cmp_[:, :]

        bank = [stack.enter_context(nc.psum_tensor(f"bank{i}", [P, 512], F32)) for i in range(8)]
        misc = bank[7]

        def small_(name):
            a, b = SMALL_AT[name]
            return sm[:, a:b]

        ident = small_("ident")
        in_w, xp_w = small_("in_w"), small_("xp_w")
        dt_w = small_("dt_w")[0:RANK, :]
        conv_w, conv_b, dt_b, d_skip = (small_(n) for n in ("conv_w", "conv_b", "dt_b", "d_skip"))

        wslot = [[w[:, s * FFN_COLS:(s + 1) * FFN_COLS] for s in range(WSLOTS)] for w in mw]
        w1slot = [nw[1][:, 512 + n * FFN_COLS:512 + (n + 1) * FFN_COLS] for n in range(2)]
        w1slot += [t[:, :, :, :].rearrange("p s h t -> p (s h t)")[:, 0:FFN_COLS] for t in pt]
        w1slot += [t[:, :, :].rearrange("p h t -> p (h t)")[:, 0:FFN_COLS] for t in ot]
        esel = nw[0][0:64, 0:J0 * P]
        combt = [nw[0][0:64, J0 * P:J0 * P + 512], nw[1][0:64, 0:512]]
        HID_AT = J0 * P + 512
        hid = [[w[:, HID_AT + s * 512:HID_AT + (s + 1) * 512] for s in range(3)] for w in nw]

        def nw_free(cols):
            return UNITS - G + -(-cols // 512)

        x0_in, x_in, small_in, ctx_in, ctx_n_in, mask_in, esel_in, dsc_in = (sem(n) for n in ("x0_in", "x_in", "small_in", "ctx_in", "ctx_n_in", "mask_in", "esel_in", "dsc_in"))
        fold_in = [sem(f"fold_in{i}") for i in range(2)]
        ffn_in = [sem(f"ffn_in{i}") for i in range(3)]
        out_done = sem("out_done")
        a_chain, v_chain, g_const = sem("a_chain"), sem("v_chain"), sem("g_const")
        misc_filled, misc_done = sem("misc_filled"), sem("misc_done")
        ctx_hi, ctx_lo = sem("ctx_hi"), sem("ctx_lo")
        in_w_hi, in_w_split, ctx_n_hi, coef_ready = (sem(n) for n in ("in_w_hi", "in_w_split", "ctx_n_hi", "coef_ready"))
        m_filled, n_filled = sem("m_filled"), sem("n_filled")
        m_hi, m_lo, n_hi, n_lo = (sem(n) for n in ("m_hi", "m_lo", "n_hi", "n_lo"))
        mv_ready, rstd_ready = sem("mv_ready"), sem("rstd_ready")
        xn_ready, xt_hi = sem("xn_ready"), sem("xt_hi")
        q_filled, q_hi, q_lo = sem("q_filled"), sem("q_hi"), sem("q_lo")
        s_filled, s_masked, q_left = sem("s_filled"), sem("s_masked"), sem("q_left")
        p_exp, p_inv, p_norm = sem("p_exp"), sem("p_inv"), sem("p_norm")
        t_filled, t_hi, t_lo = sem("t_filled"), sem("t_hi"), sem("t_lo")
        v_filled, o_hi, o_lo, o_summed = (sem(n) for n in ("v_filled", "o_hi", "o_lo", "o_summed"))
        res_done = sem("res_done")
        mbias_ready = sem("mbias_ready")
        pre_tanh, pre_u, pre_e, log_ready, dt_parts, dtu_ready = (
            sem(n) for n in ("pre_tanh", "pre_u", "pre_e", "log_ready", "dt_parts", "dtu_ready"))
        a_exp, setup_done = sem("a_exp"), sem("setup_done")
        da_ready, dbu_ready, scanned, times_c, y_added = (
            sem(n) for n in ("da_ready", "dbu_ready", "scanned", "times_c", "y_added"))
        rows_out = sem("rows_out")
        bc_in = [sem(f"bc_in{i}") for i in range(BC_SLOTS)]
        yg_norm, yg_tanh, yg_ready = sem("yg_norm"), sem("yg_tanh"), sem("yg_ready")
        lg_ready, lg_exp, cm_ready, ct_hi = (sem(n) for n in ("lg_ready", "lg_exp", "cm_ready", "ct_hi"))
        w_hi, w_lo_vector, w_lo_pool = sem("w_hi"), sem("w_lo_vector"), sem("w_lo_pool")
        w1_ready = sem("w1_ready")
        g_filled, u_filled, c_filled = sem("g_filled"), sem("u_filled"), sem("c_filled")
        h_tanh, h_g, h_u, h_c, h_hi, h_lo_vector, h_lo_pool = (
            sem(n) for n in ("h_tanh", "h_g", "h_u", "h_c", "h_hi", "h_lo_vector", "h_lo_pool"))
        d_done, acc_done, out_ready = sem("d_done"), sem("acc_done"), sem("out_ready")

        use = {}
        for kind, arg in STEPS:
            mine = {"ln": [("ln", arg)], "conv": [("in",) + arg] if kind == "conv" else [], "xp": [("xp", arg)], "dt": [("dt",) + arg] if kind == "dt" else [],
                    "yt": [("yt", arg)], "rows": [("rows", arg)], "gate": [("lg", arg)], "comb": [("cT", arg)]}.get(kind, [])
            for key in mine:
                use[key] = len(use)
        ln_no = {arg: n for n, arg in enumerate(a for k, a in STEPS if k == "ln")}
        stat_no = {arg: n for n, arg in enumerate(a for k, a in STEPS if k == "stat")}

        def w_split(j):
            ours = [i for i in range(j + 1) if (i in W_VECTOR) == (j in W_VECTOR)]
            return w_lo_vector if j in W_VECTOR else w_lo_pool, len(ours)

        def hid_split(m):
            ours = [i for i in range(m + 1) if (i in HID_VECTOR) == (m in HID_VECTOR)]
            return h_lo_vector if m in HID_VECTOR else h_lo_pool, len(ours)

        def gate_bank(m):
            return bank[4 if ITEMS[m][0] >= 2 and m % 2 else 2]

        def fold_banks(g):
            return bank[1 + g % 3], bank[4 + g % 3]

        def acc_banks(k):
            return (bank[0], bank[1]) if k % 2 == 0 else (bank[5], bank[6])

        ffn_loads = [x for x in STEPS if x[0] in ("W", "W1")]
        ffn_slot = {key: (n % 3, n // 3 + 1) for n, key in enumerate(ffn_loads)}

        first_fp8 = LAST[1] + 1
        block = stack.enter_context(nc.Block())

        @block.sync
        def _(sp):
            sp.dma_start(xs[:, 0:TT, :], x.rearrange("(n p) d -> p n d", p=P)[:, 0:TT, :]).then_inc(x0_in, 16)
            sp.dma_start(prob[:, 0:2, :].rearrange("p a n -> p (a n)"), ctx_t).then_inc(ctx_in, 16)
            for g in range(2):
                sp.dma_start(stage_fold[:, g, :], fold_w[g]).then_inc(fold_in[g], 16)
                if g == 0:
                    sp.dma_start(sm[:, :], small).then_inc(small_in, 16)
            sp.dma_start(prob[:, 2:4, :].rearrange("p a n -> p (a n)").rearrange("p (n c) -> p n c", c=C),
                         ctx_n.rearrange("(n p) c -> p n c", p=P)).then_inc(ctx_n_in, 16)
            sp.dma_start(xs[:, TT:, :], x.rearrange("(n p) d -> p n d", p=P)[:, TT:, :]).then_inc(x_in, 16)
            sp.dma_start(mask_sb[:, :], mask.unsqueeze(0).to_broadcast([P, B * T])).then_inc(mask_in, 16)
            sp.dma_start(dscale[:, :], down_scale.unsqueeze(0).to_broadcast([P, D])).then_inc(dsc_in, 16)
            for g in range(2, G):
                sp.wait_ge(n_filled, g - 1)
                sp.dma_start(stage_fold[:, g % 2, :], fold_w[g]).then_inc(fold_in[g % 2], 16)

            def ffn_load(n):
                if n >= len(ffn_loads):
                    return
                if n == 0:
                    sp.wait_ge(n_filled, G)
                if n == 2:
                    sp.wait_ge(t_filled, 2 * (UNITS - 2))
                if n >= 3:
                    before, j = ffn_loads[n - 3]
                    sp.wait_ge(*(w_split(j) if before == "W" else (w1_ready, j + 1)))
                kind, a = ffn_loads[n]
                row = a % J0 if kind == "W" else J0 + a
                sp.dma_start(stage_ffn[:, n % 3, :], ffn_w[row]).then_inc(ffn_in[n % 3], 16)

            def bc_load(v):
                if v % BC_SLOTS == BC_SLOTS - 1:
                    sp.wait_ge(dtu_ready, v // NS + 1)
                sp.dma_start(bc[v % BC_SLOTS], bc_rows[v].unsqueeze(0).to_broadcast([P, 2, 512])).then_inc(bc_in[v % BC_SLOTS], 16)

            for kind, a in order("dve"):
                if kind == "xp":
                    sp.wait_ge(misc_done, use[("xp", a)] + 1)
                    for n in range(2):
                        sp.dma_start(bc_rows[a * NS:(a + 1) * NS, n, :], xp_rows[RANK + n * NS:RANK + (n + 1) * NS, :]).then_inc(rows_out, 16)
                    sp.wait_ge(rows_out, 32 * (a + 1))
                    for v in range(a * NS, a * NS + BC_SLOTS):
                        if v >= BC_SLOTS:
                            sp.wait_ge(times_c, v - BC_SLOTS + 1)
                        bc_load(v)
                elif kind == "scanC" and a % NS + BC_SLOTS < NS:
                    sp.wait_ge(times_c, a + 1)
                    bc_load(a + BC_SLOTS)
                elif (kind, a) == ("T", UNITS - G):
                    ffn_load(0)
                    ffn_load(1)
                elif (kind, a) == ("T", UNITS - 3):
                    ffn_load(2)
                elif kind in ("W", "W1b"):
                    ffn_load(ffn_loads.index((kind[:2] if kind != "W" else "W", a)) + 3)
            for b in range(B):
                sp.wait_ge(out_ready, b + 1)
                sp.dma_start(out.rearrange("(n p) d -> p n d", p=P)[:, b * TT:(b + 1) * TT, :],
                             xs[:, b * TT:(b + 1) * TT, :]).then_inc(out_done, 16)
            sp.wait_ge(out_done, 16 * B)

        @block.tensor
        def _(pe):
            def three(bank_ap, a, b, start, stop, skip=False):
                terms = [(a[0], b[0])]
                if b[1] is not None:
                    terms.append((a[0], b[1]))
                if a[1] is not None:
                    terms.append((a[1], b[0]))
                for n, (l, r) in enumerate(terms):
                    last = nc.tensor.matmul(bank_ap, l, r, start=start and n == 0, stop=stop and n == len(terms) - 1,
                                            skip_group_check=skip)
                return last

            def take_misc(key):
                if use[key]:
                    pe.wait_ge(misc_done, use[key])

            def fold(g):
                pe.wait_ge(fold_in[g % 2], 16 * (g // 2 + 1))
                wq = stage_fold[:, g % 2, 0:512]
                wo = stage_fold[:, g % 2, 512:1024]
                wk = stage_fold[:, g % 2, 1024:1152]
                wv = stage_fold[:, g % 2, 1152:1280]
                m_bank, n_bank = fold_banks(g)
                if g >= 3:
                    pe.wait_ge(m_lo, g - 2)
                for h in range(2):
                    for d in range(DB):
                        last = nc.tensor.matmul(m_bank[:, (h * DB + d) * P:(h * DB + d + 1) * P],
                                                wq[:, h * D + d * P:h * D + (d + 1) * P], wk, start=True, stop=True)
                last.then_inc(m_filled, 1)
                if g >= 3:
                    pe.wait_ge(n_lo, g - 2)
                nc.tensor.matmul(n_bank[:, :], wv, wo, start=True, stop=True).then_inc(n_filled, 1)

            def ln(arg):
                kind, b = arg
                if ln_no[arg] == 0:
                    pe.wait_ge(small_in, 16)
                pe.wait_ge(xn_ready, ln_no[arg] + 1)
                take_misc(("ln", arg))
                for d in range(DB):
                    for t in range(TT):
                        last = nc.tensor.transpose(misc[:, d * T + t * P:d * T + (t + 1) * P],
                                                   xn[:, t, d * P:(d + 1) * P], ident)
                last.then_inc(misc_filled, 1)

            def conv(arg):
                p, e = arg
                pair = slice(p * PAIR, (p + 1) * PAIR)
                if p == 0 and e == 0:
                    pe.wait_ge(ctx_lo, 1)
                    pe.wait_ge(in_w_split, 1)
                take_misc(("in", p, e))
                w = [t[:, e * P:(e + 1) * P] for t in in_split]
                three(misc[:, :], w, (ct[0][:, pair], ct[1][:, pair]), True, True).then_inc(misc_filled, 1)

            def xp(p):
                take_misc(("xp", p))
                pe.wait_ge(pre_u, 2 * p + 2)
                for e in range(ET):
                    last = nc.tensor.matmul(misc[0:XP, :], xp_w[:, e * P:e * P + XP], uu[:, e, :], start=e == 0, stop=e == ET - 1)
                last.then_inc(misc_filled, 1)

            def dt_part(arg):
                p, e = arg
                take_misc(("dt", p, e))
                nc.tensor.matmul(misc[:, :], dt_w[:, e * P:(e + 1) * P], xp_rows[0:RANK, :], start=True, stop=True).then_inc(misc_filled, 1)

            def q_part(u):
                b, g = divmod(u, G)
                pe.wait_ge(misc_done, use[("ln", (0, b))] + 1)
                if u == 0:
                    pe.wait_ge(m_lo, G)
                else:
                    pe.wait_ge(q_lo, u)
                for h in range(2):
                    for d in range(DB):
                        at = g * 512 + (h * DB + d) * P
                        last = three(bank[1][:, h * T:(h + 1) * T], [w[:, at:at + P] for w in mw],
                                     [w[:, d, b * T:(b + 1) * T] for w in xnt], h == 0 and d == 0, d == DB - 1, skip=True)
                last.then_inc(q_filled, 1)

            def r_part(u):
                pe.wait_ge(q_hi, u + 1)
                if u == 0:
                    pe.wait_ge(setup_done, 1)
                nc.tensor.matmul(bank[1][:, :], neg_ident[:, :], qt[0][:, u % 2, :], start=False, stop=True,
                                 skip_group_check=True).then_inc(q_left, 1)

            def s_part(u):
                b, g = divmod(u, G)
                pe.wait_ge(q_lo, u + 1)
                for h in range(2):
                    if u:
                        pe.wait_ge(s_masked, 2 * u - 1 + h)
                    for t in range(TT):
                        last = three(bank[2 + h][:, t * T:(t + 1) * T],
                                     [w[:, u % 2, h * T + t * P:h * T + (t + 1) * P] for w in qt],
                                     [w[:, b * T:(b + 1) * T] for w in ct], True, True)
                    last.then_inc(s_filled, 1)

            def t_part(u):
                pe.wait_ge(p_norm, u + 1)
                for h in range(2):
                    if u:
                        pe.wait_ge(t_lo, 2 * u - 1 + h)
                    elif h == 0:
                        pe.wait_ge(n_lo, G)
                    for t in range(TT):
                        for s in range(TT):
                            last = nc.tensor.transpose(bank[4 + h][:, s * T + t * P:s * T + (t + 1) * P],
                                                       probs[u % 3][:, h, t * T + s * P:t * T + (s + 1) * P], ident)
                    last.then_inc(t_filled, 1)

            def v_part(u):
                b = u // G
                pe.wait_ge(t_lo, 2 * u + 2)
                if u == 0:
                    pe.wait_ge(setup_done, 1)
                if u:
                    pe.wait_ge(o_lo, u)
                for s in range(TT):
                    last = three(bank[6][:, :], [w[:, b * TT + s, :] for w in cn],
                                 [w[:, s, :, :].rearrange("p h t -> p (h t)") for w in pt], s == 0, s == TT - 1)
                last.then_inc(v_filled, 1)

            def o_part(u):
                b, g = divmod(u, G)
                pe.wait_ge(o_lo, u + 1)
                if g == 0 and b:
                    pe.wait_ge(res_done, b)
                for t in range(TT):
                    for h in range(2):
                        last = three(bank[0][:, t * D:(t + 1) * D],
                                     [w[:, u % 2, h * T + t * P:h * T + (t + 1) * P] for w in ot],
                                     [w[:, g * 512 + h * D:g * 512 + (h + 1) * D] for w in nw],
                                     g == 0 and t == 0 and h == 0, g == G - 1 and h == 1, skip=True)
                last.then_inc(o_summed, 1)

            def rows_part(p):
                take_misc(("rows", p))
                pe.wait_ge(misc_done, use[("ln", (1, 2 * p + 1))] + 1)
                if p == 0:
                    pe.wait_ge(setup_done, 1)
                for d in range(DB):
                    last = three(misc[0:10, :], [w[:, d * 10:(d + 1) * 10] for w in rw],
                                 [w[:, d, p * PAIR:(p + 1) * PAIR] for w in xnt], d == 0, d == DB - 1)
                last.then_inc(misc_filled, 1)

            def gate(p):
                take_misc(("lg", p))
                for t in range(4):
                    last = nc.tensor.transpose(misc[:, t * 10:(t + 1) * 10], lg_rows[:, t * P:(t + 1) * P], ident[0:10, 0:10])
                last.then_inc(misc_filled, 1)

            def comb(p):
                take_misc(("cT", p))
                pe.wait_ge(cm_ready, p + 1)
                for t in range(4):
                    last = nc.tensor.transpose(misc[0:64, t * P:(t + 1) * P], cm[:, t, :], ident)
                last.then_inc(misc_filled, 1)

            def g_part(m):
                k, j = ITEMS[m]
                p = k % 2
                if k < 2:
                    pe.wait_ge(*w_split(j))
                    ws = [w[j % WSLOTS] for w in wslot]
                    pe.wait_ge(misc_done, use[("ln", (1, 2 * p + 1))] + 1)
                else:
                    pe.wait_ge(w1_ready, j + 1)
                    ws = [w1slot[j], None]
                    pe.wait_ge(misc_done, use[("ln", (3, 2 * p + 1))] + 1)
                for n, (filled, read) in enumerate(((g_filled, h_g), (u_filled, h_u))):
                    bk = bank[3] if n else gate_bank(m)
                    if n == 0 and m == first_fp8 + 1:
                        pe.wait_ge(h_c, m - 1)
                    elif n == 0 and m > first_fp8 + 1:
                        pe.wait_ge(h_g, m - 1)
                    elif m:
                        pe.wait_ge(read, m)
                    else:
                        pe.wait_ge(s_masked, 2 * UNITS)
                    for d in range(DB):
                        at = n * DB * P + d * P
                        last = three(bk[:, :], [w if w is None else w[:, at:at + P] for w in ws],
                                     [w[:, d, p * PAIR:(p + 1) * PAIR] for w in xnt], d == 0, d == DB - 1)
                    last.then_inc(filled, 1)

            def c_part(m):
                k, j = ITEMS[m]
                p = k % 2
                if k < 2:
                    if m:
                        pe.wait_ge(h_c, m)
                    else:
                        pe.wait_ge(t_lo, 2 * UNITS)
                        pe.wait_ge(esel_in, 16)
                    pe.wait_ge(misc_done, use[("cT", p)] + 1)
                    nc.tensor.matmul(bank[4][:, :], esel[:, j * P:(j + 1) * P], combt[p], start=True, stop=True).then_inc(c_filled, 1)

            def d_part(m):
                k, j = ITEMS[m]
                pe.wait_ge(*hid_split(m))
                down = 2 * DB * P
                if k < 2:
                    ws = [w[j % WSLOTS][:, down:down + D] for w in wslot]
                else:
                    ws = [w1slot[j][:, down:down + D], None]
                if j == 0:
                    if k >= 2:
                        pe.wait_ge(acc_done, 2 * (k - 1))
                    elif k == 1:
                        pe.wait_ge(o_lo, UNITS)
                    else:
                        pe.wait_ge(res_done, B)
                        pe.wait_ge(q_lo, UNITS)
                banks = acc_banks(k)
                n_items = J0 if k < 2 else J1
                for t in range(4):
                    last = three(banks[t // 2][:, t % 2 * D:(t % 2 + 1) * D],
                                 [w[m % 3][:, t * P:(t + 1) * P] for w in hid], ws,
                                 j == 0 and t % 2 == 0, j == n_items - 1, skip=True)
                last.then_inc(d_done, 1)

            def yt(b):
                take_misc(("yt", b))
                pe.wait_ge(yg_ready, b + 1)
                for t in range(TT):
                    for e in range(ET):
                        last = nc.tensor.transpose(misc[:, t * D + e * P:t * D + (e + 1) * P], ysb[:, e, t * P:(t + 1) * P], ident)
                last.then_inc(misc_filled, 1)

            do = {"fold": fold, "ln": ln, "conv": conv, "xp": xp, "dt": dt_part, "Q": q_part, "S": s_part,
                  "R": r_part, "T": t_part, "V": v_part, "O": o_part, "rows": rows_part, "gate": gate, "comb": comb, "G": g_part, "c": c_part, "D": d_part, "yt": yt}
            for kind, a in order("pe"):
                if kind in do:
                    do[kind](a)

        @block.scalar
        def _(act):
            def copy(dst, src, scale=1.0):
                return nc.scalar.activation(dst, src, ACT.Copy, scale=scale)

            def misc_ready(key):
                act.wait_ge(misc_filled, use[key] + 1)

            def ctx(_):
                act.wait_ge(ctx_in, 16)
                copy(ct[0][:, :], prob[:, 0:2, :].rearrange("p a n -> p (a n)")).then_inc(ctx_hi, 1)

            def setup(_):
                act.wait_ge(small_in, 16)
                copy(in_split[0], in_w).then_inc(in_w_hi, 1)
                copy(rw[0][:, :], small_("route_w"))
                nc.scalar.activation(acoef[:, :, :].rearrange("p e n -> p (e n)"), small_("a_log"), ACT.Exp).then_inc(a_exp, 1)
                act.wait_ge(ctx_n_in, 16)
                copy(cn[0][:, :, :].rearrange("p n c -> p (n c)"),
                     prob[:, 2:4, :].rearrange("p a n -> p (a n)")).then_inc(ctx_n_hi, 1)

            def fold(g):
                act.wait_ge(m_filled, g + 1)
                copy(mw[0][:, g * 512:(g + 1) * 512], fold_banks(g)[0][:, :]).then_inc(m_hi, 1)
                act.wait_ge(n_filled, g + 1)
                copy(nw[0][:, g * 512:(g + 1) * 512], fold_banks(g)[1][:, :]).then_inc(n_hi, 1)

            def ln(arg):
                kind, b = arg
                if kind == 1:
                    act.wait_ge(q_filled, G * (b + 1))
                elif kind == 3:
                    act.wait_ge(u_filled, LAST[b // 2] + 1)
                misc_ready(("ln", arg))
                copy(xnt[0][:, :, b * T:(b + 1) * T], misc[:, :].rearrange("p (d t) -> p d t", d=DB)).then_inc(xt_hi, 1)

            def link(ins):
                chain[0] += 1
                ins.then_inc(a_chain, 1)
                act.wait_ge(a_chain, chain[0])

            chain = [0]

            def silu(arg):
                p, e = arg
                act.wait_ge(misc_done, use[("in", p, e)] + 1)
                nc.scalar.activation(dtu[:, e, :], xc[:, e, :], ACT.Tanh, scale=0.5).then_inc(pre_tanh, 1)

            def xp(p):
                misc_ready(("xp", p))
                if p:
                    act.wait_ge(rows_out, 32 * p)
                nc.scalar.activation(xp_rows[:, :], misc[0:XP, :], ACT.Copy, scale=small_("xp_scale")[0:XP, :]).then_inc(misc_done, 1)
                for e in range(ET):
                    act.wait_ge(pre_u, 2 * p + 2)
                    if p == 0 and e == 0:
                        act.wait_ge(coef_ready, 1)
                    nc.scalar.activation(ys[:, e, p * PAIR:(p + 1) * PAIR], uu[:, e, :], ACT.Copy, scale=dhalf[:, e:e + 1])

            def dt_part(arg):
                p, e = arg
                misc_ready(("dt", p, e))
                nc.scalar.activation(xc[:, e, :], misc[:, :], ACT.Identity, bias=dt_b[:, e:e + 1]).then_inc(misc_done, 1)

            def abs_part(p):
                act.wait_ge(misc_done, use[("dt", p, 1)] + 1)
                link(nc.scalar.activation(dtt[:, :, :], xc[:, :, :], ACT.Abs))
                nc.scalar.activation(dtt[:, :, :], dtt[:, :, :], ACT.Exp, scale=-1.0)
                nc.scalar.activation(xc[:, :, :], xc[:, :, :], ACT.Relu).then_inc(pre_e, 1)

            def scan_b(v):
                p, n = divmod(v, NS)
                if n == 0:
                    act.wait_ge(dtu_ready, p + 1)
                for e in range(ET):
                    if n and e == 0:
                        act.wait_ge(scanned, v)
                    nc.scalar.activation(da[:, e, :].rearrange("p (b l) -> p b l", b=2)[:, :, 1:T],
                                         dtt[:, e, :].rearrange("p (b l) -> p b l", b=2)[:, :, 1:T], ACT.Exp,
                                         scale=acoef[:, e, n:n + 1]).then_inc(da_ready, 1)

            def q_part(u):
                act.wait_ge(q_filled, u + 1)
                if u >= 2:
                    act.wait_ge(s_filled, 2 * (u - 1))
                copy(qt[0][:, u % 2, :], bank[1][:, :]).then_inc(q_hi, 1)

            def r_part(u):
                act.wait_ge(q_left, u + 1)
                copy(qt[1][:, u % 2, :], bank[1][:, :]).then_inc(q_lo, 1)

            def e_part(u):
                for h in range(2):
                    act.wait_ge(s_masked, 2 * u + h + 1)
                    for t in range(TT):
                        i = 2 * h + t
                        s = probs[u % 3][:, h, t * T:(t + 1) * T]
                        last = nc.scalar.activation(s, s, ACT.Exp, bias=s_min[:, u % 3, i:i + 1], scale=-1.0,
                                                    accum_out=s_sum[:, u % 3, i:i + 1])
                    last.then_inc(p_exp, 1)

            def t_part(u):
                for h in range(2):
                    act.wait_ge(t_filled, 2 * u + h + 1)
                    if u and h == 0:
                        act.wait_ge(v_filled, u)
                    copy(pt[0][:, :, h, :], bank[4 + h][:, :].rearrange("p (s t) -> p s t", s=TT)).then_inc(t_hi, 1)

            def v_part(u):
                act.wait_ge(v_filled, u + 1)
                if u >= 2:
                    act.wait_ge(o_summed, u - 1)
                copy(ot[0][:, u % 2, :], bank[6][:, :]).then_inc(o_hi, 1)

            def rows_part(p):
                misc_ready(("rows", p))
                copy(lg_rows, misc[0:10, :]).then_inc(misc_done, 1)

            def gexp(p):
                act.wait_ge(lg_ready, p + 1)
                nc.scalar.activation(ex[:, :, 0:9], lg[:, :, 0:9], ACT.Exp).then_inc(lg_exp, 1)

            def comb(p):
                misc_ready(("cT", p))
                if p == 1:
                    act.wait_ge(o_summed, nw_free(512))
                else:
                    act.wait_ge(o_summed, nw_free(J0 * P + 512))
                copy(combt[p], misc[0:64, :]).then_inc(ct_hi, 1)

            def w_part(m):
                slot, times = ffn_slot[("W", m)]
                act.wait_ge(ffn_in[slot], 16 * times)
                if m < WSLOTS:
                    act.wait_ge(q_filled, UNITS - G + -(-(m + 1) * FFN_COLS // 512))
                if m >= WSLOTS:
                    act.wait_ge(d_done, ITEMS.index((1, m - WSLOTS)) + 1)
                copy(wslot[0][m % WSLOTS], stage_ffn[:, slot, :]).then_inc(w_hi, 1)

            def g_part(m):
                k, j = ITEMS[m]
                act.wait_ge(g_filled, m + 1)
                if m >= 4:
                    act.wait_ge(*hid_split(m - 4))
                if k < 2:
                    nc.scalar.activation(prob[:, m % 4, :], bank[2][:, :], ACT.Tanh, scale=0.5).then_inc(h_tanh, 1)
                else:
                    nc.scalar.activation(prob[:, m % 4, :], gate_bank(m)[:, :], ACT.Tanh, scale=gcoef[:, j:j + 1]).then_inc(h_tanh, 1)

            def hi_part(m):
                act.wait_ge(h_c if ITEMS[m][0] < 2 else h_u, m + 1)
                if m >= 3:
                    act.wait_ge(d_done, m - 2)
                else:
                    act.wait_ge(o_summed, nw_free(HID_AT + 512 * (m + 1)))
                copy(hid[0][m % 3], prob[:, m % 4, :]).then_inc(h_hi, 1)

            def ytanh(b):
                act.wait_ge(yg_norm, b + 1)
                if b:
                    act.wait_ge(misc_filled, use[("yt", b - 1)] + 1)
                nc.scalar.activation(ysb[:, :, :], xn[:, :, :], ACT.Tanh, scale=0.5).then_inc(yg_tanh, 1)

            do = {"ctx": ctx, "setup": setup, "fold": fold, "ln": ln, "silu": silu, "xp": xp, "dt": dt_part, "abs": abs_part, "scanB": scan_b, "Q": q_part, "R": r_part, "E": e_part, "T": t_part,
                  "V": v_part, "rows": rows_part, "gexp": gexp, "comb": comb, "W": w_part, "G": g_part, "H": hi_part, "ytanh": ytanh}
            for kind, a in order("act"):
                if kind in do:
                    do[kind](a)

        @block.vector
        def _(dve):
            v_ = nc.vector
            chain = [0]

            def link(ins):
                chain[0] += 1
                ins.then_inc(v_chain, 1)
                dve.wait_ge(v_chain, chain[0])

            def misc_ready(key):
                dve.wait_ge(misc_filled, use[key] + 1)

            def ctx(_):
                dve.wait_ge(ctx_hi, 1)
                v_.tensor_tensor(ct[1][:, :], prob[:, 0:2, :].rearrange("p a n -> p (a n)"), ct[0][:, :].bitcast(F32), ALU.subtract).then_inc(ctx_lo, 1)

            def setup(_):
                dve.wait_ge(a_exp, 1)
                a = acoef[:, :, :]
                v_.tensor_scalar(a, a, -1.0, None, ALU.mult)
                v_.tensor_scalar(gcoef[:, :], small_("g_scale"), 0.5, None, ALU.mult)
                v_.scalar_tensor_tensor(ucoef[:, :], small_("g_scale"), 0.5, small_("u_scale"), ALU.mult, ALU.mult)
                v_.tensor_scalar(dhalf[:, :], d_skip, 0.5, None, ALU.mult).then_inc(coef_ready, 1)

            def fold(g):
                for w, bk, hi, lo in zip((mw, nw), fold_banks(g), (m_hi, n_hi), (m_lo, n_lo)):
                    at = slice(g * 512, (g + 1) * 512)
                    dve.wait_ge(hi, g + 1)
                    v_.tensor_tensor(w[1][:, at], bk[:, :], w[0][:, at].bitcast(F32), ALU.subtract).then_inc(lo, 1)

            def stat(arg):
                kind, b = arg
                if kind == 0:
                    dve.wait_ge(x_in if b else x0_in, 16)
                for t in range(TT):
                    last = v_.bn_stats(bn[:, b % 2, t, :], xs[:, b * TT + t, :])
                link(last)
                for t in range(TT):
                    last = v_.bn_aggr(mv[:, b % 2, t, :], bn[:, b % 2, t, :])
                link(last)
                v_.tensor_scalar(rstd[:, b % 2, :].unsqueeze(2), mv[:, b % 2, :, 1:2], EPS, None, ALU.add).then_inc(mv_ready, 1)

            def normalise(arg):
                kind, b = arg
                dve.wait_ge(rstd_ready, stat_no[arg] + 1)
                if xn_use[0]:
                    dve.wait_ge(misc_filled, xn_use[0])
                for t in range(TT):
                    last = v_.tensor_scalar(xn[:, t, :], xs[:, b * TT + t, :], mv[:, b % 2, t, 0:1], rstd[:, b % 2, t:t + 1],
                                            ALU.subtract, ALU.mult)
                return last

            xn_use = [0]

            def norm(arg):
                normalise(arg).then_inc(xn_ready, 1)
                xn_use[0] = use[("ln", arg)] + 1

            def ln(arg):
                kind, b = arg
                dve.wait_ge(xt_hi, ln_no[arg] + 1)
                at = slice(b * T, (b + 1) * T)
                v_.tensor_tensor(xnt[1][:, :, at], misc[:, :].rearrange("p (d t) -> p d t", d=DB),
                                 xnt[0][:, :, at].bitcast(F32), ALU.subtract).then_inc(misc_done, 1)

            def conv(arg):
                p, e = arg
                misc_ready(("in", p, e))
                if p and e == 0:
                    dve.wait_ge(scanned, NS)
                    dve.wait_ge(dbu_ready, NS)
                w = conv_w[:, e * TAPS:(e + 1) * TAPS]
                link(v_.tensor_scalar(xc[:, e, :], misc[:, :], w[:, TAPS - 1:TAPS], conv_b[:, e:e + 1], ALU.mult, ALU.add))
                for back in range(1, TAPS):
                    o = xc[:, e, :].rearrange("p (b l) -> p b l", b=2)[:, :, back:T]
                    i = misc[:, :].rearrange("p (b l) -> p b l", b=2)[:, :, 0:T - back]
                    last = v_.scalar_tensor_tensor(o, i, w[:, TAPS - 1 - back:TAPS - back], o, ALU.mult, ALU.add)
                    if back < TAPS - 1:
                        link(last)
                last.then_inc(misc_done, 1)

            def silu(arg):
                p, e = arg
                dve.wait_ge(pre_tanh, 2 * p + e + 1)
                v_.scalar_tensor_tensor(uu[:, e, :], dtu[:, e, :], 1.0, xc[:, e, :], ALU.add, ALU.mult).then_inc(pre_u, 1)

            def softplus(arg):
                p, n = arg
                if n == 0:
                    dve.wait_ge(pre_e, p + 1)
                for c in LOG1P[::-1][3 * n:3 * n + 3]:
                    if c == LOG1P[-1]:
                        last = v_.tensor_scalar(dtu[:, :, :], dtt[:, :, :], c, None, ALU.mult)
                    else:
                        last = v_.scalar_tensor_tensor(dtu[:, :, :], dtu[:, :, :], c, dtt[:, :, :], ALU.add, ALU.mult)
                    if c != LOG1P[0]:
                        link(last)
                if n == SOFT - 1:
                    last.then_inc(log_ready, 1)

            def scan_c(v):
                s = ring[:, v % 2, :, :]
                flat = s.rearrange("p e l -> p (e l)")
                dve.wait_ge(da_ready, 2 * v + 2)
                dve.wait_ge(dbu_ready, v + 1)
                v_.tensor_tensor_scan(flat, da.rearrange("p e l -> p (e l)"), flat, 0.0, ALU.mult, ALU.add).then_inc(scanned, 1)
                dve.wait_ge(scanned, v + 1)
                v_.tensor_tensor(s, s, bc[v % BC_SLOTS][:, 1, :].unsqueeze(1).to_broadcast([P, ET, 512]), ALU.mult).then_inc(times_c, 1)

            def q_part(u):
                b, g = divmod(u, G)
                if g == 0:
                    if u == 0:
                        dve.wait_ge(mask_in, 16)
                        v_.reduce_max(mask_any[:, :], mask_sb[:, :].rearrange("p (b t) -> p b t", b=B), AX.X)
                    v_.tensor_scalar(mask_bias[:, b % 2, :], mask_sb[:, b * T:(b + 1) * T], 1.0, MASKED,
                                     ALU.subtract, ALU.mult).then_inc(mbias_ready, 1)

            def s_part(u):
                b, g = divmod(u, G)
                if g == 0:
                    dve.wait_ge(mbias_ready, b + 1)
                for h in range(2):
                    dve.wait_ge(s_filled, 2 * u + h + 1)
                    if u >= 3 and h == 0:
                        dve.wait_ge(t_filled, 2 * (u - 2))
                    if u == 2 and h == 0:
                        dve.wait_ge(n_filled, G)
                    if u == 1 and h == 0:
                        dve.wait_ge(setup_done, 1)
                    for t in range(TT):
                        i = 2 * h + t
                        last = v_.tensor_tensor_reduce(
                            out=probs[u % 3][:, h, t * T:(t + 1) * T], in0=bank[2 + h][:, t * T:(t + 1) * T],
                            in1=mask_bias[:, b % 2, :], scale=-(float(P) ** -0.5), scalar=3.0e38, op0=ALU.add, op1=ALU.min,
                            accum_out=s_min[:, u % 3, i:i + 1])
                    last.then_inc(s_masked, 1)

            def t_part(u):
                for h in range(2):
                    dve.wait_ge(t_hi, 2 * u + h + 1)
                    v_.tensor_tensor(pt[1][:, :, h, :], bank[4 + h][:, :].rearrange("p (s t) -> p s t", s=TT),
                                     pt[0][:, :, h, :].bitcast(F32), ALU.subtract).then_inc(t_lo, 1)

            def i_part(u):
                b = u // G
                dve.wait_ge(p_exp, 2 * u + 2)
                link(v_.reciprocal(s_inv[:, u % 3, :], s_sum[:, u % 3, :]))
                v_.tensor_scalar(s_inv[:, u % 3, :], s_inv[:, u % 3, :], mask_any[:, b:b + 1], None, ALU.mult).then_inc(p_inv, 1)

            def v_part(u):
                dve.wait_ge(o_hi, u + 1)
                v_.tensor_tensor(ot[1][:, u % 2, :], bank[6][:, :], ot[0][:, u % 2, :].bitcast(F32), ALU.subtract).then_inc(o_lo, 1)

            def res(b):
                dve.wait_ge(o_summed, G * (b + 1))
                rows = xs[:, b * TT:(b + 1) * TT, :]
                v_.tensor_tensor(rows, rows, bank[0][:, :].rearrange("p (t d) -> p t d", t=TT), ALU.add).then_inc(res_done, 1)
                dve.wait_ge(res_done, b + 1)

            def gate(p):
                misc_ready(("lg", p))
                v_.tensor_copy(lg[:, :, :], misc[:, 0:40].rearrange("p (t n) -> p t n", t=4)).then_inc(misc_done, 1)
                dve.wait_ge(misc_done, use[("lg", p)] + 1)
                L = lg[:, :, 0:E]
                a = L.unsqueeze(2).to_broadcast([P, 4, E, E])
                c = L.unsqueeze(3).to_broadcast([P, 4, E, E])
                v_.tensor_tensor(gt[:, :, :, :], a, c, ALU.is_gt)
                link(v_.tensor_tensor(eq[:, :, :, :], a, c, ALU.is_equal))
                low = small_("lower").unsqueeze(1).to_broadcast([P, 4, E * E])
                eqf = eq[:, :, :, :].rearrange("p t e j -> p t (e j)")
                link(v_.tensor_tensor(eqf, eqf, low, ALU.mult))
                link(v_.tensor_tensor(gt[:, :, :, :], gt[:, :, :, :], eq[:, :, :, :], ALU.add))
                link(v_.reduce_sum(rk[:, :, :], gt[:, :, :, :], AX.X))
                link(v_.tensor_scalar(rk[:, :, :], rk[:, :, :], 1.5, None, ALU.is_lt))
                link(v_.reduce_max(r1[:, :, :].rearrange("p t n -> p (t n)"), L, AX.X))
                link(v_.tensor_tensor(L, L, r1[:, :, :].to_broadcast([P, 4, E]), ALU.subtract))
                v_.tensor_scalar(lg[:, :, E:E + 1], lg[:, :, E:E + 1], -1.0, None, ALU.mult).then_inc(lg_ready, 1)

            def gate2(p):
                dve.wait_ge(lg_exp, p + 1)
                W = ex[:, :, 0:E]
                link(v_.tensor_tensor(W, W, rk[:, :, :], ALU.mult))
                link(v_.reduce_sum(r1[:, :, :].rearrange("p t n -> p (t n)"), W, AX.X))
                link(v_.reciprocal(r1[:, :, :], r1[:, :, :]))
                link(v_.tensor_tensor(W, W, r1[:, :, :].to_broadcast([P, 4, E]), ALU.mult))
                S = ex[:, :, E:E + 1]
                link(v_.tensor_scalar(S, S, 1.0, None, ALU.add))
                link(v_.reciprocal(S, S))
                v_.tensor_scalar(cm[:, :, 0:E + 1], ex[:, :, 0:E + 1], 0.5, None, ALU.mult)
                v_.tensor_scalar(cm[:, :, 32:32 + E + 1], ex[:, :, 0:E + 1], 0.5, None, ALU.mult).then_inc(cm_ready, 1)

            def comb(p):
                dve.wait_ge(ct_hi, p + 1)
                v_.tensor_tensor(combt[p][32:64, :], misc[32:64, :], combt[p][32:64, :].bitcast(F32), ALU.subtract).then_inc(misc_done, 1)

            def g_part(m):
                k, j = ITEMS[m]
                t = prob[:, m % 4, :]
                dve.wait_ge(h_tanh, m + 1)
                v_.scalar_tensor_tensor(t, t, 1.0, gate_bank(m)[:, :], ALU.add, ALU.mult).then_inc(h_g, 1)
                dve.wait_ge(u_filled, m + 1)
                dve.wait_ge(h_g, m + 1)
                if k < 2:
                    v_.tensor_tensor(t, t, bank[3][:, :], ALU.mult).then_inc(h_u, 1)
                else:
                    v_.scalar_tensor_tensor(t, t, ucoef[:, j:j + 1], bank[3][:, :], ALU.mult, ALU.mult).then_inc(h_u, 1)

            def c_part(m):
                k, j = ITEMS[m]
                t = prob[:, m % 4, :]
                if k < 2:
                    dve.wait_ge(h_u, m + 1)
                    dve.wait_ge(c_filled, m + 1)
                    v_.tensor_tensor(t, t, bank[4][:, :], ALU.mult).then_inc(h_c, 1)

            def lo_part(m):
                if m in HID_VECTOR:
                    dve.wait_ge(h_hi, m + 1)
                    v_.tensor_tensor(hid[1][m % 3], prob[:, m % 4, :], hid[0][m % 3].bitcast(F32), ALU.subtract).then_inc(h_lo_vector, 1)

            def w_part(m):
                if m in W_VECTOR:
                    dve.wait_ge(w_hi, m + 1)
                    v_.tensor_tensor(wslot[1][m % WSLOTS], stage_ffn[:, ffn_slot[("W", m)][0], :],
                                     wslot[0][m % WSLOTS].bitcast(F32), ALU.subtract).then_inc(w_lo_vector, 1)

            def w1_part(j):
                slot, times = ffn_slot[("W1", j)]
                dve.wait_ge(ffn_in[slot], 16 * times)
                w = stage_ffn[:, slot, :]
                link(v_.tensor_scalar(q1c[:, :].bitcast(I32), w.bitcast(I32), 0x7F800000, None, ALU.bitwise_and))
                link(v_.tensor_scalar(q1c[:, :], q1c[:, :], 2.0 ** -6, 1.5 * 2.0 ** 20, ALU.max, ALU.mult))
                link(v_.tensor_tensor(w, w, q1c[:, :], ALU.add))

            def w1b_part(j):
                slot, times = ffn_slot[("W1", j)]
                w = stage_ffn[:, slot, :]
                link(v_.tensor_tensor(w, w, q1c[:, :], ALU.subtract))
                link(v_.tensor_scalar(q1c[:, :], w, 7.3e35, 0.0, ALU.mult, ALU.mult))
                if j == 0:
                    dve.wait_ge(o_summed, UNITS)
                v_.tensor_tensor(w1slot[j], q1c[:, :], w, ALU.add).then_inc(w1_ready, 1)
                dve.wait_ge(w1_ready, j + 1)

            def acc(arg):
                k, n = arg
                p = k % 2
                dve.wait_ge(d_done, LAST[k] + 1)
                rows = xs[:, p * 4 + 2 * n:p * 4 + 2 * n + 2, :]
                sums = acc_banks(k)[n][:, :].rearrange("p (t d) -> p t d", t=2)
                if k < 2:
                    v_.tensor_tensor(rows, rows, sums, ALU.add).then_inc(acc_done, 1)
                    dve.wait_ge(acc_done, 2 * k + n + 1)
                else:
                    if k == 2 and n == 0:
                        dve.wait_ge(dsc_in, 16)
                    for t in range(2):
                        last = v_.tensor_tensor(xn[:, t, :], sums[:, t, :], dscale[:, :], ALU.mult)
                    link(last)
                    v_.tensor_tensor(rows, rows, xn[:, :, :], ALU.add).then_inc(out_ready, 1)
                    dve.wait_ge(out_ready, 2 * p + n + 1)

            def ynorm(b):
                normalise((2, b)).then_inc(yg_norm, 1)

            def ymul(b):
                dve.wait_ge(yg_tanh, b + 1)
                link(v_.scalar_tensor_tensor(ysb[:, :, :], ysb[:, :, :], 1.0, xn[:, :, :], ALU.add, ALU.mult))
                dve.wait_ge(y_added, NS * (b // 2 + 1))
                for e in range(ET):
                    last = v_.tensor_tensor(ysb[:, e, :], ysb[:, e, :], ys[:, e, b * T:(b + 1) * T], ALU.mult)
                last.then_inc(yg_ready, 1)

            def yt(b):
                misc_ready(("yt", b))
                rows = xs[:, b * TT:(b + 1) * TT, :]
                v_.scalar_tensor_tensor(rows, misc[:, :].rearrange("p (t d) -> p t d", t=TT), 0.5, rows, ALU.mult, ALU.add).then_inc(misc_done, 1)
                dve.wait_ge(misc_done, use[("yt", b)] + 1)

            do = {"ctx": ctx, "setup": setup, "fold": fold, "stat": stat, "norm": norm, "ln": ln, "conv": conv, "silu": silu, "soft": softplus, "scanC": scan_c, "Q": q_part, "S": s_part, "T": t_part,
                  "I": i_part, "V": v_part, "res": res, "gate": gate, "gate2": gate2, "comb": comb, "G": g_part, "c": c_part, "W": w_part, "W1": w1_part, "W1b": w1b_part, "acc": acc,
                  "H": lo_part, "ynorm": ynorm, "ymul": ymul, "yt": yt}
            for kind, a in order("dve"):
                if kind in do:
                    do[kind](a)

        @block.gpsimd
        def _(pool):
            gp = nc.gpsimd

            def setup(_):
                lower = lambda dst, src, hi: gp.tensor_tensor(dst, src, hi.bitcast(F32), ALU.subtract)
                pool.wait_ge(in_w_hi, 1)
                lower(in_split[1], in_w, in_split[0]).then_inc(in_w_split, 1)
                gp.tensor_scalar(neg_ident[:, :], ident, -1.0, None, ALU.mult)
                gp.memset(cm[:, :, :], 0.0)
                pool.wait_ge(a_exp, 1)
                lower(rw[1][:, :], small_("route_w"), rw[0][:, :])
                pool.wait_ge(ctx_n_hi, 1)
                lower(cn[1][:, :, :].rearrange("p n c -> p (n c)"), prob[:, 2:4, :].rearrange("p a n -> p (a n)"),
                      cn[0][:, :, :].rearrange("p n c -> p (n c)")).then_inc(setup_done, 1)

            def n_part(u):
                s = probs[u % 3].rearrange("p h (t s) -> p (h t) s", t=TT)
                pool.wait_ge(p_inv, u + 1)
                gp.tensor_tensor(s, s, s_inv[:, u % 3, :].unsqueeze(2).to_broadcast([P, 4, T]), ALU.mult).then_inc(p_norm, 1)

            def dt_end(p):
                pool.wait_ge(log_ready, p + 1)
                gp.tensor_tensor(dtt[:, :, :], dtu[:, :, :], xc[:, :, :], ALU.add).then_inc(dt_parts, 1)
                pool.wait_ge(dt_parts, 2 * p + 1)
                gp.tensor_tensor(dtu[:, :, :], dtt[:, :, :], uu[:, :, :], ALU.mult).then_inc(dt_parts, 1)
                pool.wait_ge(dt_parts, 2 * p + 2)
                gp.memset(da.rearrange("p e (b l) -> p (e b) l", b=2)[:, :, 0:1], 0.0).then_inc(dtu_ready, 1)

            def scan_b(v):
                pool.wait_ge(bc_in[v % BC_SLOTS], 16 * (v // BC_SLOTS + 1))
                if v % NS == 0:
                    pool.wait_ge(dtu_ready, v // NS + 1)
                if v >= 2:
                    pool.wait_ge(y_added, v - 1)
                gp.tensor_tensor(ring[:, v % 2, :, :], dtu[:, :, :], bc[v % BC_SLOTS][:, 0, :].unsqueeze(1).to_broadcast([P, ET, 512]),
                                 ALU.mult).then_inc(dbu_ready, 1)

            def sum_part(v):
                y = ys[:, :, v // NS * PAIR:(v // NS + 1) * PAIR]
                pool.wait_ge(times_c, v + 1)
                if v:
                    pool.wait_ge(y_added, v)
                gp.tensor_tensor(y, y, ring[:, v % 2, :, :], ALU.add).then_inc(y_added, 1)

            def esel_load(_):
                pool.wait_ge(o_summed, nw_free(J0 * P))
                gp.dma_start(esel, expert_sel).then_inc(esel_in, 16)

            gp.memset(neg_half[:, :], -0.5).then_inc(g_const, 1)
            pool.wait_ge(g_const, 1)

            def rstd_part(arg):
                pool.wait_ge(mv_ready, stat_no[arg] + 1)
                gp.tensor_tensor(rstd[:, arg[1] % 2, :], rstd[:, arg[1] % 2, :], neg_half[:, :], ALU.pow).then_inc(rstd_ready, 1)

            def w_part(m):
                if m not in W_VECTOR:
                    pool.wait_ge(w_hi, m + 1)
                    gp.tensor_tensor(wslot[1][m % WSLOTS], stage_ffn[:, ffn_slot[("W", m)][0], :],
                                     wslot[0][m % WSLOTS].bitcast(F32), ALU.subtract).then_inc(w_lo_pool, 1)

            def lo_part(m):
                if m not in HID_VECTOR:
                    pool.wait_ge(h_hi, m + 1)
                    gp.tensor_tensor(hid[1][m % 3], prob[:, m % 4, :], hid[0][m % 3].bitcast(F32), ALU.subtract).then_inc(h_lo_pool, 1)

            do = {"setup": setup, "dt_end": dt_end, "esel": esel_load, "stat": rstd_part, "N": n_part, "scanB": scan_b, "sum": sum_part, "W": w_part, "H": lo_part}
            for kind, a in order("pool"):
                if kind in do:
                    do[kind](a)


def kernel(x, ctx_1024, mask_BxS2_bf1, L0_xattn_Wq, L0_xattn_Wk, L0_xattn_Wv, L0_xattn_Wo, L0_ffn_gate_w, L0_ffn_w_gate,
           L0_ffn_w_up, L0_ffn_w_down, L0_ffn_shgate_w, L0_ffn_shw_gate, L0_ffn_shw_up, L0_ffn_shw_down,
           L1_xattn_in_proj_w, L1_xattn_conv_w, L1_xattn_conv_b, L1_xattn_x_proj_w, L1_xattn_dt_proj_w,
           L1_xattn_dt_proj_b, L1_xattn_A_log, L1_xattn_D, L1_ffn_gate_w, L1_ffn_up_w, L1_ffn_down_w,
           L1_ffn_gate_scale, L1_ffn_up_scale, L1_ffn_down_scale):
    import concourse.bacc as bacc
    import numpy as np
    from concourse.bass_utils import run_bass_kernel_spmd

    f32 = np.float32

    def blocks(w):
        n = w.shape[0] // P
        return w.reshape(n, P, -1).transpose(1, 0, 2).reshape(P, -1)

    ctx = np.ascontiguousarray(ctx_1024).reshape(B * T, C)
    wq = np.asarray(L0_xattn_Wq).reshape(D, G, 2, P)
    wk = np.asarray(L0_xattn_Wk).reshape(C, G, P)
    wv = np.asarray(L0_xattn_Wv).reshape(C, G, P)
    wo = np.asarray(L0_xattn_Wo).reshape(G, 2, P, D)
    fold_w = np.concatenate([
        wq.transpose(1, 3, 2, 0).reshape(G, P, 2 * D), wo.transpose(0, 2, 1, 3).reshape(G, P, 2 * D),
        wk.transpose(1, 2, 0), wv.transpose(1, 2, 0)], axis=2)

    pad = J0 * P - E * HE - HS
    wide = lambda w, s: np.concatenate([np.asarray(w).transpose(1, 0, 2).reshape(D, E * HE), np.asarray(s), np.zeros((D, pad), f32)], axis=1)
    down0 = np.concatenate([np.asarray(L0_ffn_w_down).reshape(E * HE, D), np.asarray(L0_ffn_shw_down), np.zeros((pad, D), f32)])

    def tiles(gate, up, down):
        n = down.shape[0] // P
        cut = lambda w: w.reshape(DB, P, n, P).transpose(2, 1, 0, 3).reshape(n, P, DB * P)
        return np.concatenate([cut(gate), cut(up), down.reshape(n, P, D)], axis=2)

    ffn_w = np.concatenate([
        tiles(wide(L0_ffn_w_gate, L0_ffn_shw_gate), wide(L0_ffn_w_up, L0_ffn_shw_up), down0),
        tiles(np.asarray(L1_ffn_gate_w), np.asarray(L1_ffn_up_w), np.asarray(L1_ffn_down_w))])

    xp_t = np.zeros((ET * P, P), f32)
    xp_t[:, :XP] = np.asarray(L1_xattn_x_proj_w).T
    dt_w = np.zeros((P, ET * P), f32)
    dt_w[:RANK] = np.asarray(L1_xattn_dt_proj_w).T
    route = np.zeros((D, 10), f32)
    route[:, :E] = np.asarray(L0_ffn_gate_w).T
    route[:, E] = np.asarray(L0_ffn_shgate_w)
    lower = np.broadcast_to((np.arange(E)[None, :] < np.arange(E)[:, None]).astype(f32).reshape(1, E * E), (P, E * E))
    xp_scale = np.full((P, 1), 0.5, f32)
    xp_scale[RANK:RANK + NS] = 0.25
    expert_sel = np.zeros((64, J0 * P), f32)
    for e in range(E + 1):
        expert_sel[[e, 32 + e], e * HE:(e * HE + (HE if e < E else HS))] = 1
    parts = {
        "ident": np.eye(P, dtype=f32), "in_w": np.asarray(L1_xattn_in_proj_w).T, "xp_w": blocks(xp_t), "dt_w": dt_w,
        "a_log": blocks(np.asarray(L1_xattn_A_log)), "conv_w": blocks(np.asarray(L1_xattn_conv_w).reshape(ET * P, TAPS)),
        "conv_b": blocks(np.asarray(L1_xattn_conv_b)[:, None]), "dt_b": blocks(np.asarray(L1_xattn_dt_proj_b)[:, None]),
        "d_skip": blocks(np.asarray(L1_xattn_D)[:, None]), "g_scale": blocks(np.asarray(L1_ffn_gate_scale)[:, None]),
        "u_scale": blocks(np.asarray(L1_ffn_up_scale)[:, None]), "route_w": blocks(route), "lower": lower, "xp_scale": xp_scale,
    }
    small = np.concatenate([parts[n] for n, _ in SMALL], axis=1)

    arrays = {
        "x": np.asarray(x).reshape(B * T, D), "ctx_n": ctx, "ctx_t": ctx.T, "fold_w": fold_w, "ffn_w": ffn_w, "small": small,
        "expert_sel": expert_sel, "mask": np.asarray(mask_BxS2_bf1).reshape(B * T).view(np.uint8),
        "down_scale": np.asarray(L1_ffn_down_scale),
    }
    nc = bacc.Bacc("TRN2", target_bir_lowering=False, num_devices=1)
    args, given = [], {}
    for name, a in arrays.items():
        given[f"in_{name}"] = a = np.ascontiguousarray(a)
        args.append(nc.dram_tensor(f"in_{name}", a.shape, mybir.dt.from_np(a.dtype), kind="ExternalInput").ap())
    out = nc.dram_tensor("out", (B * T, D), F32, kind="ExternalOutput").ap()
    bc_rows = nc.dram_tensor("bc_rows", (2 * NS, 2, 512), F32, kind="Internal").ap()
    build_program(nc, *args, bc_rows, out)
    r = run_bass_kernel_spmd(nc, [given], core_ids=[0])
    return r.results[0]["out"].reshape(B, T, D)
```
